# Optimizing a Trainium2 kernel written in Bass

```python
import numpy as np
import jax
import jax.numpy as jnp

def _softmax(x, axis=-1):
    return jax.nn.softmax(x, axis=axis)

def _gelu(x):
    return jax.nn.gelu(x, approximate=True)

def _silu(x):
    return jax.nn.silu(x)

def _sigmoid(x):
    return jax.nn.sigmoid(x)

def _layernorm(x, axis=-1, eps=1e-05):
    m = jnp.mean(x, axis=axis, keepdims=True)
    v = jnp.var(x, axis=axis, keepdims=True)
    return (x - m) / jnp.sqrt(v + eps)

def _scatter_add(tgt, idx, src, axis=0):
    return tgt.at[idx].add(src)

def _segment_sum(src, seg, n):
    return jax.ops.segment_sum(src, seg, n)
kernel_name = 'mk_decoder_postln_d1_seqx_r4_b80d73'

def setup_inputs(seed: int=0):
    np.random.seed(seed)
    _w = jnp.asarray

    def _rec_inputs():
        import jax
        import jax.numpy as jnp
        _rk = jax.random.key(seed)
        x = -0.0002928 + 1 * jax.random.normal(jax.random.fold_in(_rk, 1), (2, 1024, 256), jnp.float32)
        _lenS = 1024 - jax.random.randint(jax.random.fold_in(_rk, 7), (2,), 0, max(1, 1024 // 4) + 1, jnp.int32)
        _lenS2 = 64 - jax.random.randint(jax.random.fold_in(_rk, 8), (2,), 0, max(1, 64 // 4) + 1, jnp.int32)
        _ctx_1024P = jax.random.normal(jax.random.fold_in(_rk, 11), (2, 16, 256), jnp.float32)
        _ctx_1024c = jax.random.dirichlet(jax.random.fold_in(_rk, 511), 0.3 * jnp.ones((16,), jnp.float32), (2, 64))
        _ctx_1024t = jnp.einsum('bsk,bkd->bsd', _ctx_1024c, _ctx_1024P)
        _ctx_1024t = _ctx_1024t * jax.lax.rsqrt(jnp.mean(jnp.square(_ctx_1024t)) + 1e-12) * 0.953939
        ctx_1024 = -1.39393e-06 + 0.999914 * (_ctx_1024t + 0.3 * jax.random.normal(jax.random.fold_in(_rk, 611), (2, 64, 256), jnp.float32))
        _validS = jnp.arange(1024)[None, :] < _lenS[:, None]
        _validS2 = jnp.arange(64)[None, :] < _lenS2[:, None]
        _causal = jnp.tril(jnp.ones((1024, 1024), dtype=bool))
        mask_BxS2_ik0 = jnp.where(jnp.broadcast_to(_validS2[:, :], (2, 64)), 0, 1).astype(jnp.int32)
        return (x, ctx_1024, mask_BxS2_ik0)
    x, ctx_1024, mask_BxS2_ik0 = _rec_inputs()

    def _L0_attn_setup():
        import jax, jax.numpy as jnp
        import numpy as np
        HIDDEN = 256
        key = jax.random.key(seed)
        k0, k1, k2, k3, k4 = jax.random.split(key, 5)
        B, S, H = (2, 1024, HIDDEN)
        s = 1.0 / np.sqrt(H)
        return {'hidden_states': jax.random.normal(k0, (B, S, H), dtype=jnp.float32), 'qkv_w': jax.random.uniform(k1, (3 * H, H), jnp.float32, -s, s), 'qkv_b': jax.random.uniform(k2, (3 * H,), jnp.float32, -s, s), 'out_w': jax.random.uniform(k3, (H, H), jnp.float32, -s, s), 'out_b': jax.random.uniform(k4, (H,), jnp.float32, -s, s)}
    _L0_attn_all = _L0_attn_setup()
    _L0_attn_in = {k: v for k, v in _L0_attn_all.items() if k in ('qkv_w', 'qkv_b', 'out_w', 'out_b')}
    del _L0_attn_all

    def _L0_xattn_setup():
        import jax, jax.numpy as jnp
        import numpy as np
        D_MODEL = 256
        NUM_HEADS = 16
        D_K = D_MODEL // NUM_HEADS
        NEG = -10000.0
        key = jax.random.key(seed)
        ks = jax.random.split(key, 8)
        B, S = (2, 512)
        query = jax.random.normal(ks[0], (B, S, D_MODEL), dtype=jnp.float32)
        key_t = jax.random.normal(ks[1], (B, S, D_MODEL), dtype=jnp.float32)
        value = jax.random.normal(ks[2], (B, S, D_MODEL), dtype=jnp.float32)
        mask = jax.random.randint(ks[3], (B, S), 0, 2, dtype=jnp.int32)
        scale = 1.0 / np.sqrt(D_MODEL)
        Wq = jax.random.normal(ks[4], (D_MODEL, D_MODEL), dtype=jnp.float32) * scale
        Wk = jax.random.normal(ks[5], (D_MODEL, D_MODEL), dtype=jnp.float32) * scale
        Wv = jax.random.normal(ks[6], (D_MODEL, D_MODEL), dtype=jnp.float32) * scale
        Wo = jax.random.normal(ks[7], (D_MODEL, D_MODEL), dtype=jnp.float32) * scale
        return {'query': query, 'key': key_t, 'value': value, 'mask': mask, 'Wq': Wq, 'Wk': Wk, 'Wv': Wv, 'Wo': Wo}
    _L0_xattn_all = _L0_xattn_setup()
    _L0_xattn_in = {k: v for k, v in _L0_xattn_all.items() if k in ('Wq', 'Wk', 'Wv', 'Wo')}
    del _L0_xattn_all

    def _L0_ffn_setup():
        import jax, jax.numpy as jnp
        import numpy as np
        E = 16
        K = 4
        B, S, H, I = (4, 256, 256, 512)
        key = jax.random.key(seed)
        k0, k1, k2, k3 = jax.random.split(key, 4)
        scale = 0.02
        return {'hidden_states': jax.random.normal(k0, (B, S, H), jnp.float32), 'router_w': jax.random.normal(k1, (H, E), jnp.float32) * scale, 'router_b': jnp.zeros((E,), jnp.float32), 'w1': jax.random.normal(k2, (E, H, I), jnp.float32) * scale, 'b1': jnp.zeros((E, I), jnp.float32), 'w2': jax.random.normal(k3, (E, I, H), jnp.float32) * scale, 'b2': jnp.zeros((E, H), jnp.float32)}
    _L0_ffn_all = _L0_ffn_setup()
    _L0_ffn_in = {k: v for k, v in _L0_ffn_all.items() if k in ('router_w', 'router_b', 'w1', 'b1', 'w2', 'b2')}
    del _L0_ffn_all
    return {'x': x, 'ctx_1024': ctx_1024, 'mask_BxS2_ik0': mask_BxS2_ik0, 'L0_attn_qkv_w': _L0_attn_in['qkv_w'], 'L0_attn_qkv_b': _L0_attn_in['qkv_b'], 'L0_attn_out_w': _L0_attn_in['out_w'], 'L0_attn_out_b': _L0_attn_in['out_b'], 'L0_xattn_Wq': _L0_xattn_in['Wq'], 'L0_xattn_Wk': _L0_xattn_in['Wk'], 'L0_xattn_Wv': _L0_xattn_in['Wv'], 'L0_xattn_Wo': _L0_xattn_in['Wo'], 'L0_ffn_router_w': _L0_ffn_in['router_w'], 'L0_ffn_router_b': _L0_ffn_in['router_b'], 'L0_ffn_w1': _L0_ffn_in['w1'], 'L0_ffn_b1': _L0_ffn_in['b1'], 'L0_ffn_w2': _L0_ffn_in['w2'], 'L0_ffn_b2': _L0_ffn_in['b2']}

def reference(x, ctx_1024, mask_BxS2_ik0, L0_attn_qkv_w, L0_attn_qkv_b, L0_attn_out_w, L0_attn_out_b, L0_xattn_Wq, L0_xattn_Wk, L0_xattn_Wv, L0_xattn_Wo, L0_ffn_router_w, L0_ffn_router_b, L0_ffn_w1, L0_ffn_b1, L0_ffn_w2, L0_ffn_b2):
    import jax
    import jax.numpy as jnp

    def _L0_attn_ref(hidden_states, qkv_w, qkv_b, out_w, out_b):
        import jax, jax.numpy as jnp
        import numpy as np
        HIDDEN = 256
        H = hidden_states.shape[-1]
        qkv = jnp.einsum('bsh,oh->bso', hidden_states, qkv_w) + qkv_b
        q, k, v = jnp.split(qkv, 3, axis=-1)
        scores = jnp.einsum('bqh,bkh->bqk', q, k) / jnp.sqrt(jnp.asarray(H, q.dtype))
        attn = jax.nn.softmax(scores, axis=-1)
        ctx = jnp.einsum('bqk,bkh->bqh', attn, v)
        return jnp.einsum('bsh,oh->bso', ctx, out_w) + out_b

    def _L0_xattn_ref(query, key, value, mask, Wq, Wk, Wv, Wo):
        import jax, jax.numpy as jnp
        import numpy as np
        D_MODEL = 256
        NUM_HEADS = 16
        D_K = D_MODEL // NUM_HEADS
        NEG = -10000.0
        B, Sq, _ = query.shape
        Sk = key.shape[1]

        def proj(x, W, S):
            return (x @ W.T).reshape(B, S, NUM_HEADS, D_K).transpose(0, 2, 1, 3)
        Q = proj(query, Wq, Sq)
        K = proj(key, Wk, Sk)
        V = proj(value, Wv, Sk)
        scores = jnp.einsum('bhqd,bhkd->bhqk', Q, K) / jnp.sqrt(jnp.float32(D_K))
        pad = mask[:, None, None, :]
        scores = jnp.where(pad == 0, NEG, scores)
        causal = jnp.tril(jnp.ones((Sq, Sk), dtype=bool))
        scores = jnp.where(causal, scores, NEG)
        probs = jax.nn.softmax(scores, axis=-1)
        out = jnp.einsum('bhqk,bhkd->bhqd', probs, V)
        out = out.transpose(0, 2, 1, 3).reshape(B, Sq, D_MODEL)
        return out @ Wo.T

    def _L0_ffn_ref(hidden_states, router_w, router_b, w1, b1, w2, b2):
        import jax, jax.numpy as jnp
        import numpy as np
        E = 16
        K = 4
        B, S, H, I = (4, 256, 256, 512)
        b, s, h = hidden_states.shape
        logits = hidden_states @ router_w + router_b
        probs = jax.nn.softmax(logits, axis=-1)
        topw, topi = jax.lax.top_k(probs, K)
        topw = topw / jnp.sum(topw, axis=-1, keepdims=True)
        combine = jnp.sum(jax.nn.one_hot(topi, E, dtype=hidden_states.dtype) * topw[..., None], axis=2)
        x = hidden_states.reshape(b * s, h)
        c = combine.reshape(b * s, E)

        def body(acc, expert):
            w1e, b1e, w2e, b2e, ce = expert
            hmid = jax.nn.gelu(x @ w1e + b1e, approximate=False)
            return (acc + (hmid @ w2e + b2e) * ce[:, None], None)
        out, _ = jax.lax.scan(body, jnp.zeros_like(x), (w1, b1, w2, b2, c.T))
        return out.reshape(b, s, h)
    x = _layernorm(x + _L0_attn_ref(x, L0_attn_qkv_w, L0_attn_qkv_b, L0_attn_out_w, L0_attn_out_b), axis=-1)
    x = _layernorm(x + _L0_xattn_ref(x, ctx_1024, ctx_1024, mask_BxS2_ik0, L0_xattn_Wq, L0_xattn_Wk, L0_xattn_Wv, L0_xattn_Wo), axis=-1)
    x = _layernorm(x + _L0_ffn_ref(x, L0_ffn_router_w, L0_ffn_router_b, L0_ffn_w1, L0_ffn_b1, L0_ffn_w2, L0_ffn_b2), axis=-1)
    return x

_drawn_inputs = setup_inputs


def setup_inputs(seed=0):
    import zlib

    import numpy as np

    out = dict(_drawn_inputs(seed))
    spreads = {'L0_ffn_router_b': (0.0, 0.1), 'L0_ffn_b1': (0.0, 0.617), 'L0_ffn_b2': (0.0, 0.1)}
    factors = {'L0_attn_qkv_w': 3.137}
    for name, (base, spread) in spreads.items():
        noise = np.random.default_rng([zlib.crc32(name.encode()), seed]).standard_normal(out[name].shape)
        drawn = base * np.exp(spread * noise) if base else spread * noise
        out[name] = jnp.asarray(drawn.astype(out[name].dtype))
    for name, factor in factors.items():
        out[name] = (out[name] * factor).astype(out[name].dtype)
    return out
```

```python
from contextlib import ExitStack

import concourse.bass as bass
from concourse import mybir
from concourse.alu_op_type import AluOpType as ALU

F32 = mybir.dt.float32
F32R = mybir.dt.float32r
I32 = mybir.dt.int32
U32 = mybir.dt.uint32
ACT = mybir.ActivationFunctionType
AX = mybir.AxisListType
ds = bass.ds

P = 128
B, S, D = 2, 1024, 256
KD = D // P
NT = B * S // P
TPB = S // P
HEADS, DK, SK = 16, 16, 64
HPC = P // DK
PAIRS = HEADS // 2
VW = DK + 1
E, K, I = 16, 4, 512
KI = I // P
CAP = B * S
SLOT = 256
NSTEP = (B * S * K) // SLOT + E - 1
EPS = 1e-5
NEG = -10000.0
BIAS = 2


def done(t):
    return t + 1 + BIAS


def freed(t):
    return t + 1


def upto(t, ahead):
    return min(t + ahead, NT - 1) if isinstance(t, int) else t + ahead


def pipeline(eng, n, stages):
    depth = max(skew for skew, _ in stages)
    first = depth + depth % 2 + 2
    pairs = (n - first) // 2

    def static(t):
        for skew, fn in stages:
            if 0 <= t - skew < n:
                fn(t - skew, (t - skew) % 2, (t - skew) // 2)

    for t in range(first):
        static(t)
    if pairs > 0:
        with eng.Fori(first // 2, first // 2 + pairs) as i:
            for q in range(2):
                for skew, fn in stages:
                    par = (q - skew) % 2
                    half = (q - skew - par) // 2
                    fn(i * 2 + (q - skew), par, i + half)
    for t in range(first + 2 * max(pairs, 0), n + depth):
        static(t)


def decoder_layer(nc, x, ctx, mask, qkv_w, qkv_b, out_w, out_b, wq, wk, wv, wo,
                  router_w, router_b, w1, b1, w2, b2, out):
    xg_dram = nc.dram_tensor("expert_rows", [E * CAP, D], F32, kind="Internal").ap()
    yg_dram = nc.dram_tensor("expert_out", [NSTEP * SLOT, D], F32, kind="Internal").ap()
    x_rows = x.rearrange("b s d -> (b s) d")
    out_rows = out.rearrange("b s d -> (b s) d")
    w1_rows = w1.rearrange("e d h -> (e d) h")
    w2_rows = w2.rearrange("e h d -> (e h) d")

    with ExitStack() as stack:
        names = []

        def sem(name):
            return stack.enter_context(nc.semaphore(name))

        def count(name):
            s = sem(name)
            names.append(s)
            return s

        def sb(name, shape, dt=F32, where=stack):
            return where.enter_context(nc.sbuf_tensor(name, shape, dt))

        ps = stack.enter_context(nc.psum_tensor("ps", [P, 8, 512], F32))

        ident = sb("ident", [P, P])
        ones = sb("ones", [P, P])
        tri = sb("tri", [P, P])
        iota16i = sb("iota16i", [P, E], I32)
        iota16 = sb("iota16", [P, E])
        mhalf = sb("mhalf", [P, 1])
        carry = sb("carry", [P, E])
        x_all = sb("x_all", [P, NT, D])
        slot_all = sb("slot_all", [P, NT, K])
        exp_all = sb("exp_all", [P, NT, K])
        yrow_all = sb("yrow_all", [P, NT, K], U32)
        wts_all = sb("wts_all", [P, NT, K])
        bn = sb("bn", [P, 2, 6])
        mv = sb("mv", [P, 2, 2])
        ve = sb("ve", [P, 2])
        rstd = sb("rstd", [P, 2])
        yres = sb("yres", [P, 2, D])
        xs = sb("xs", [P, 2, D])
        tab = sb("tab", [1, NSTEP, 4], I32)
        thr_i = sb("thr_i", [P, CAP // SLOT], I32)
        thr = sb("thr", [P, CAP // SLOT])
        trie = sb("trie", [P, E, E])
        sid_i = sb("sid_i", [1, NSTEP], I32)
        sid = sb("sid", [1, NSTEP])

        early = ExitStack()

        def sbe(name, shape, dt=F32):
            return sb(name, shape, dt, early)

        a_h, a_l = sbe("a_h", [P, KD, D], F32R), sbe("a_l", [P, KD, D], F32R)
        wvo_h, wvo_l = sbe("wvo_h", [P, KD, D], F32R), sbe("wvo_l", [P, KD, D], F32R)
        zeros = sbe("zeros", [P, 1, D])
        blk = sbe("blk", [P, HPC])
        mask_i = sbe("mask_i", [P, B, SK], I32)
        keep = sbe("keep", [P, B, SK])
        msk_mul = sbe("msk_mul", [P, NT, SK])
        msk_add = sbe("msk_add", [P, NT, SK])
        rb = sbe("rb", [P, E])
        rw = sbe("rw", [P, KD, E])
        bq = sbe("bq", [P, KD])
        bv = sbe("bv", [P, KD])
        bo = sbe("bo", [P, D])
        u = sbe("u", [P, KD])
        vo = sbe("vo", [P, D])
        wq_h, wq_l = sbe("wq_h", [P, KD, D], F32R), sbe("wq_l", [P, KD, D], F32R)
        wo_h, wo_l = sbe("wo_h", [P, KD, D], F32R), sbe("wo_l", [P, KD, D], F32R)
        kb_h = sbe("kb_h", [P, B * KD, HPC, SK], F32R)
        kb_l = sbe("kb_l", [P, B * KD, HPC, SK], F32R)
        vb_h = sbe("vb_h", [P, B, PAIRS, 2 * VW], F32R)
        vb_l = sbe("vb_l", [P, B, PAIRS, 2 * VW], F32R)
        xT_h, xT_l = sbe("xT_h", [P, KD, B * S], F32R), sbe("xT_l", [P, KD, B * S], F32R)
        v_h, v_l = sbe("v_h", [P, NT, D], F32R), sbe("v_l", [P, NT, D], F32R)
        sT_h, sT_l = sbe("sT_h", [P, 2, KD, P], F32R), sbe("sT_l", [P, 2, KD, P], F32R)
        q_h, q_l = sbe("q_h", [P, 2, KD, P], F32R), sbe("q_l", [P, 2, KD, P], F32R)
        prob = sbe("prob", [P, 2, S])
        pT_h, pT_l = sbe("pT_h", [P, TPB, P], F32R), sbe("pT_l", [P, TPB, P], F32R)
        nmax = sbe("nmax", [P, 2])
        nmaxs = sbe("nmaxs", [P, 2])
        rsum = sbe("rsum", [P, 2])
        rinv = sbe("rinv", [P, 2])
        hmax = sbe("hmax", [P, 2, HEADS])
        hinv = sbe("hinv", [P, 2, HEADS])
        octx = sbe("octx", [P, 2, D])
        oT_h, oT_l = sbe("oT_h", [P, KD, P], F32R), sbe("oT_l", [P, KD, P], F32R)
        x2T = sbe("x2T", [P, 2, KD, P])
        lg = sbe("lg", [P, 2, E])
        lmax = sbe("lmax", [P, 2])
        lexp = sbe("lexp", [P, 2, E])
        lsum = sbe("lsum", [P, 2])
        linv = sbe("linv", [P, 2])
        rp = sbe("rp", [P, 2, E])
        mx8 = sbe("mx8", [P, 2, 8])
        ix8 = sbe("ix8", [P, 2, 8], U32)
        ixf = sbe("ixf", [P, 2, K])
        wsum = sbe("wsum", [P, 2])
        winv = sbe("winv", [P, 2])
        oh = sbe("oh", [P, 2, K, E])
        mk = sbe("mk", [P, 2, E])
        pos = sbe("pos", [P, 2, E])
        ohp = sbe("ohp", [P, 2, K, E])
        slotf = sbe("slotf", [P, 2, K])
        idx = sbe("idx", [P, 2, K], U32)
        xd = sbe("xd", [P, 2, D])

        setup = ExitStack()

        def sbs(name, shape, dt=F32):
            return sb(name, shape, dt, setup)

        n_qkv = sbs("n_qkv", [P, 3 * KD, D])
        n_out = sbs("n_out", [P, KD, D])
        n_x = sbs("n_x", [P, 4, KD, D])
        n_ctx = sbs("n_ctx", [P, D])
        aoT = sbs("aoT", [P, KD, D])
        wkT = sbs("wkT", [P, KD, D])
        wvT = sbs("wvT", [P, KD, D])
        cT = sbs("cT", [P, KD, P])
        cT2 = sbs("cT2", [P, KD, B, 2, SK])
        bvr = sbs("bvr", [P, KD, P])
        kt_h = sbs("kt_h", [P, KD, P], F32R)
        kt_l = sbs("kt_l", [P, KD, P])
        setup.close()
        x1T_h, x1T_l = sbe("x1T_h", [P, KD, B * S], F32R), sbe("x1T_l", [P, KD, B * S], F32R)
        early.close()

        late = ExitStack()

        def sbl(name, shape, dt=F32):
            return sb(name, shape, dt, late)

        ends = sbl("ends", [P, E])
        ntile = sbl("ntile", [P, E])
        cnt = sbl("cnt", [P, E])
        cmp8 = sbl("cmp8", [P, E, CAP // SLOT])
        cmpe = sbl("cmpe", [P, E, E])
        past = sbl("past", [1, NSTEP, E])
        past2 = sbl("past2", [1, NSTEP, E])
        es = sbl("es", [1, NSTEP])
        st = sbl("st", [1, NSTEP])
        live = sbl("live", [1, NSTEP])
        row = sbl("row", [1, NSTEP])
        delta = sbl("delta", [P, E])
        first_row = sbl("first_row", [P, E])
        owner = sbl("owner", [P, NT * K, E])
        shift = sbl("shift", [P, NT * K, E])
        moved = sbl("moved", [P, NT * K])
        tabf = sbl("tabf", [1, NSTEP, 4])
        xg = sbl("xg", [P, 2, 2, D])
        w1f = sbl("w1f", [P, 2, KD, I])
        w2f = sbl("w2f", [P, 2, KI, D])
        b1f = sbl("b1f", [P, 2, KI])
        b2f = sbl("b2f", [P, 2, D])
        w1_h, w1_l = sbl("w1_h", [P, 2, KD, I], F32R), sbl("w1_l", [P, 2, KD, I], F32R)
        w2_h, w2_l = sbl("w2_h", [P, 2, KI, D], F32R), sbl("w2_l", [P, 2, KI, D], F32R)
        gT_h, gT_l = sbl("gT_h", [P, 2, KD, SLOT], F32R), sbl("gT_l", [P, 2, KD, SLOT], F32R)
        hf = sbl("hf", [P, 2, KI, SLOT])
        h_h, h_l = sbl("h_h", [P, 2, KI, SLOT], F32R), sbl("h_l", [P, 2, KI, SLOT], F32R)
        yb = sbl("yb", [P, 2, 2, D])
        gat = sbl("gat", [P, 2, K, D])
        gidx = sbl("gidx", [P, 2, K], U32)
        acc = sbl("acc", [P, 2, K, D])
        ot = sbl("ot", [P, 2, D])
        late.close()

        ld_w = sem("ld_w"); ld_wx = sem("ld_wx"); ld_c = sem("ld_c"); ld_zero = sem("ld_zero")
        ld_x = [sem("ld_x0"), sem("ld_x1")]
        c_pool = sem("c_pool"); c_dve = sem("c_dve"); c_pe = sem("c_pe"); c_act = sem("c_act")
        passed = sem("passed")
        c_mm = sem("c_mm"); m_keep = sem("m_keep"); m_rep = sem("m_rep"); m_mul = sem("m_mul")
        kt_ok = sem("kt_ok"); z_ok = sem("z_ok")
        xT_ps = count("xT_ps"); sTh = count("sTh"); sTl = count("sTl"); v_ps = count("v_ps")
        vh = count("vh"); vl = count("vl"); xres = count("xres"); xTcopy = count("xTcopy")
        q_ps = count("q_ps"); qh = count("qh"); ql = count("ql"); s_ps = count("s_ps")
        mx = count("mx"); mxs = count("mxs"); ex = count("ex"); tp = count("tp"); pth = count("pth"); ptl = count("ptl")
        o_ps = count("o_ps"); ri = count("ri"); res = count("res"); bns = count("bns"); bna = count("bna")
        var = count("var"); rst = count("rst"); x1 = count("x1"); x1c = count("x1c")
        t1 = count("t1"); x1h = count("x1h"); x1l = count("x1l")
        cq_ps = count("cq_ps"); cqh = count("cqh"); cql = count("cql"); cs_ps = count("cs_ps")
        cmul = count("cmul"); cadd = count("cadd"); cmx = count("cmx"); csub = count("csub"); cex = count("cex")
        ctp = count("ctp"); cpth = count("cpth"); cptl = count("cptl"); co_ps = count("co_ps")
        cinv = count("cinv"); co = count("co"); cot = count("cot"); coth = count("coth"); cotl = count("cotl")
        cy = count("cy"); cres = count("cres"); cbns = count("cbns"); cbna = count("cbna")
        cvar = count("cvar"); crst = count("crst"); x2 = count("x2"); x2c = count("x2c")
        t2 = count("t2"); x2t = count("x2t"); lg_ps = count("lg_ps"); lgb = count("lgb"); lmx = count("lmx")
        lex = count("lex"); lin = count("lin"); lpr = count("lpr"); l8 = count("l8"); li8 = count("li8")
        lif = count("lif"); lxa = count("lxa"); loh = count("loh"); lmk = count("lmk"); lws = count("lws"); lwi = count("lwi")
        lw = count("lw"); pos_ps = count("pos_ps"); lpos = count("lpos"); lcar = count("lcar"); lohp = count("lohp"); lsl = count("lsl")
        lidx = count("lidx"); xdc = count("xdc"); lall = count("lall")
        sc_dma = [[sem(f"sc_dma{p}{r}") for r in range(K)] for p in range(2)]
        tb = sem("tb"); tb_pool = sem("tb_pool")
        f_x = [sem("f_x0"), sem("f_x1")]; f_w1 = [sem("f_w10"), sem("f_w11")]
        f_w2 = [sem("f_w20"), sem("f_w21")]; f_b1 = [sem("f_b10"), sem("f_b11")]; f_b2 = [sem("f_b20"), sem("f_b21")]
        w1h = count("w1h"); w1l = count("w1l"); w2h = count("w2h"); w2l = count("w2l")
        gt = count("gt"); gth = count("gth"); gtl = count("gtl"); hps = count("hps"); gel = count("gel")
        hh = count("hh"); hl = count("hl"); yps = count("yps"); yok = count("yok")
        st_y = [sem("st_y0"), sem("st_y1")]
        gix = count("gix")
        g_dma = [[sem(f"g_dma{p}{r}") for r in range(K)] for p in range(2)]
        ac = [count(f"ac{r}") for r in range(K)]
        ebns = count("ebns"); ebna = count("ebna"); evar = count("evar"); erst = count("erst"); eo = count("eo")
        st_o = [sem("st_o0"), sem("st_o1")]

        def mm3(pe, o, ah, al, bh, bl, first, last):
            pe.matmul(o, ah, bh, start=first, stop=False)
            pe.matmul(o, ah, bl, start=False, stop=False)
            return pe.matmul(o, al, bh, start=False, stop=last)

        f = lambda ap: ap.bitcast(F32)

        block = stack.enter_context(nc.Block())

        @block.sync
        def _(sp):
            for s in names:
                sp.sem_inc(s, BIAS)
            sp.dma_start(n_qkv[:], qkv_w.rearrange("(k p) c -> p k c", p=P)).then_inc(ld_w, 16)
            sp.dma_start(n_out[:], out_w.rearrange("(k p) c -> p k c", p=P)).then_inc(ld_w, 16)
            for n, w in enumerate((wq, wk, wv, wo)):
                sp.dma_start(n_x[:, n], w.rearrange("(k p) c -> p k c", p=P)).then_inc(ld_wx, 16)
            sp.dma_start(n_ctx[:], ctx.rearrange("b s d -> (b s) d")).then_inc(ld_wx, 16)

            def load_x(t, p, k):
                sp.wait_ge(xT_ps, freed(t))
                sp.wait_ge(xres, freed(t))
                sp.dma_start(xs[:, p], x_rows[ds(t * P, P), :]).then_inc(ld_x[p], 16)

            pipeline(sp, NT, [(0, load_x)])
            sp.wait_ge(z_ok, 1)
            with sp.Fori(0, E * CAP // (8 * P)) as i:
                sp.dma_start(xg_dram[ds(i * (8 * P), 8 * P), :].rearrange("(p c) d -> p c d", c=8),
                             zeros[:].broadcast_to([P, 8, D])).then_inc(ld_zero, 16)

            sp.wait_ge(tb, 1)
            for p in range(2):
                for r in range(K):
                    sp.wait_ge(sc_dma[p][r], 16 * (NT // 2))

            def load_step(t, p, k):
                rx = sp.value_load(tab[0:1, ds(t, 1), 0:1], min_val=0, max_val=E * CAP - SLOT)
                re = sp.value_load(tab[0:1, ds(t, 1), 1:2], min_val=0, max_val=E - 1)
                sp.wait_ge(gt, freed(t))
                sp.dma_start(xg[:, p], xg_dram[ds(rx, SLOT), :].rearrange("(c p) d -> p c d", p=P)).then_inc(f_x[p], 16)
                sp.wait_ge(w1h, freed(t))
                sp.wait_ge(w1l, freed(t))
                sp.dma_start(w1f[:, p], w1_rows[ds(re * D, D), :].rearrange("(k p) h -> p k h", p=P)).then_inc(f_w1[p], 16)
                sp.wait_ge(w2h, freed(t))
                sp.wait_ge(w2l, freed(t))
                sp.dma_start(w2f[:, p], w2_rows[ds(re * I, I), :].rearrange("(p j) d -> p j d", j=KI)).then_inc(f_w2[p], 16)
                sp.wait_ge(gel, freed(t))
                sp.sem_inc(passed, 1)
                sp.dma_start(b1f[:, p], b1[ds(re, 1), :].rearrange("o (p j) -> (o p) j", j=KI)).then_inc(f_b1[p], 16)

            def load_b2(t, p, k):
                r = sp.value_load(tab[0:1, ds(t, 1), 1:2], min_val=0, max_val=E - 1)
                sp.wait_ge(yok, freed(t))
                sp.dma_start(b2f[:, p], b2[ds(r, 1), :].broadcast_to([P, D])).then_inc(f_b2[p], 16)

            pipeline(sp, NSTEP, [(0, load_step), (2, load_b2)])

            def store_out(t, p, k):
                sp.wait_ge(eo, done(t))
                sp.dma_start(out_rows[ds(t * P, P), :], ot[:, p]).then_inc(st_o[p], 16)

            pipeline(sp, NT, [(0, store_out)])
            for p in range(2):
                sp.wait_ge(st_o[p], 16 * (NT // 2))

        @block.gpsimd
        def _(pool):
            pool.memset(ident[:], 0.0).then_inc(c_pool, 1)
            pool.memset(ones[:], 1.0).then_inc(c_pool, 1)
            pool.memset(tri[:], 1.0).then_inc(c_pool, 1)
            pool.memset(blk[:], 1.0).then_inc(c_pool, 1)
            pool.memset(mhalf[:], -0.5).then_inc(c_pool, 1)
            pool.memset(trie[:], 1.0).then_inc(c_pool, 1)
            pool.iota(iota16i[:], [[1, E]], base=0, channel_multiplier=0).then_inc(c_pool, 1)
            pool.iota(thr_i[:], [[SLOT, CAP // SLOT]], base=0, channel_multiplier=0).then_inc(c_pool, 1)
            pool.iota(sid_i[:], [[1, NSTEP]], base=0, channel_multiplier=0).then_inc(c_pool, 1)
            pool.wait_ge(c_pool, 9)
            pool.affine_select(ident[:], ident[:], [[-1, P]], ALU.not_equal, 1.0, base=0, channel_multiplier=1).then_inc(c_pool, 1)
            pool.affine_select(tri[:], tri[:], [[1, P]], ALU.is_gt, 0.0, base=0, channel_multiplier=-1).then_inc(c_pool, 1)
            pool.affine_select(blk[:], blk[:], [[-DK, HPC]], ALU.is_ge, 0.0, base=0, channel_multiplier=1).then_inc(c_pool, 1)
            pool.affine_select(trie[:], trie[:], [[1, E], [-1, E]], ALU.is_ge, 0.0, base=0, channel_multiplier=0).then_inc(c_pool, 1)
            pool.wait_ge(c_pool, 13)
            pool.affine_select(blk[:], blk[:], [[DK, HPC]], ALU.is_ge, 0.0, base=DK - 1, channel_multiplier=-1).then_inc(c_pool, 1)
            pool.tensor_copy(iota16[:], iota16i[:]).then_inc(c_pool, 1)
            pool.tensor_copy(thr[:], thr_i[:]).then_inc(c_pool, 1)
            pool.tensor_copy(sid[:], sid_i[:]).then_inc(c_pool, 1)
            pool.wait_ge(c_pool, 17)
            pool.tensor_scalar(carry[:], iota16[:], float(CAP), 0.0, ALU.mult, ALU.add).then_inc(c_pool, 1)
            pool.memset(zeros[:], 0.0).then_inc(z_ok, 1)
            pool.wait_ge(m_rep, 1)
            for b in range(B):
                pool.affine_select(msk_mul[:, b * TPB], msk_mul[:, b * TPB], [[-1, SK]], ALU.is_ge, 0.0,
                                   base=0, channel_multiplier=1).then_inc(m_mul, 1)

            def residual(t, p, k):
                if isinstance(t, int) and t == 0:
                    pool.wait_ge(c_dve, 20)
                pool.wait_ge(ld_x[p], 16 * k + 16)
                pool.tensor_tensor(x_all[:, ds(t, 1), :], xs[:, ds(p, 1), :], vo[:].unsqueeze(1), ALU.add).then_inc(xres, 1)

            def place(t, p, k):
                pool.wait_ge(sTh, done(t))
                pool.wait_ge(sTl, done(t))
                pool.tensor_copy(xT_h[:, :, ds(t * P, P)], f(sT_h[:, p]))
                pool.tensor_copy(xT_l[:, :, ds(t * P, P)], f(sT_l[:, p])).then_inc(xTcopy, 1)

            pipeline(pool, NT, [(0, residual), (1, place)])

            def root(t, p, k):
                pool.wait_ge(var, done(t))
                pool.tensor_tensor(rstd[:, p:p + 1], ve[:, p:p + 1], mhalf[:], ALU.pow).then_inc(rst, 1)

            def keep_x1(t, p, k):
                pool.wait_ge(x1, done(t))
                pool.tensor_copy(x_all[:, ds(t, 1), :], xs[:, ds(p, 1), :]).then_inc(x1c, 1)

            pipeline(pool, NT, [(0, root), (0, keep_x1)])

            def mask_add(t, p, k):
                pool.wait_ge(cmul, done(t))
                pool.tensor_tensor(prob[:, p].rearrange("p (h k) -> p h k", k=SK),
                                   prob[:, p].rearrange("p (h k) -> p h k", k=SK),
                                   msk_add[:, ds(t, 1), :].broadcast_to([P, HEADS, SK]), ALU.add).then_inc(cadd, 1)

            def sub_max(t, p, k):
                pool.wait_ge(cmx, done(t))
                pool.tensor_tensor(prob[:, p].rearrange("p (h k) -> p h k", k=SK),
                                   prob[:, p].rearrange("p (h k) -> p h k", k=SK),
                                   hmax[:, p].unsqueeze(2).broadcast_to([P, HEADS, SK]), ALU.subtract).then_inc(csub, 1)

            def root2(t, p, k):
                pool.wait_ge(cvar, done(t))
                pool.tensor_tensor(rstd[:, p:p + 1], ve[:, p:p + 1], mhalf[:], ALU.pow).then_inc(crst, 1)

            def keep_x2(t, p, k):
                pool.wait_ge(x2, done(t))
                pool.tensor_copy(x_all[:, ds(t, 1), :], xs[:, ds(p, 1), :]).then_inc(x2c, 1)

            def dispatch(t, p, k):
                pool.wait_ge(lidx, done(t))
                pool.tensor_copy(xd[:, p], x_all[:, ds(t, 1), :].rearrange("p a d -> p (a d)")).then_inc(xdc, 1)
                pool.wait_ge(xdc, done(t))
                pool.sem_inc(passed, 1)
                for r in range(K):
                    pool.indirect_dma_start(
                        out=xg_dram, out_offset=bass.IndirectOffsetOnAxis(ap=idx[:, p, r:r + 1], axis=0),
                        in_=xd[:, p], in_offset=None).then_inc(sc_dma[p][r], 16)

            pool.wait_ge(ld_zero, 16 * (E * CAP // (8 * P)))
            pipeline(pool, NT, [(1, mask_add), (1, sub_max), (3, root2), (3, keep_x2), (6, dispatch)])

            def split_w2(t, p, k):
                pool.wait_ge(w2h, done(t))
                pool.wait_ge(yps, freed(t))
                pool.tensor_tensor(w2_l[:, p], w2f[:, p], f(w2_h[:, p]), ALU.subtract).then_inc(w2l, 1)

            pipeline(pool, NSTEP, [(0, split_w2)])

            for p in range(2):
                pool.wait_ge(st_y[p], 16 * ((NSTEP + 1 - p) // 2))

            def gather(t, p, k):
                pool.wait_ge(gix, done(t))
                pool.wait_ge(ac[K - 1], freed(t))
                pool.sem_inc(passed, 1)
                for r in range(K):
                    pool.indirect_dma_start(
                        out=gat[:, p, r], out_offset=None, in_=yg_dram,
                        in_offset=bass.IndirectOffsetOnAxis(ap=gidx[:, p, r:r + 1], axis=0)).then_inc(g_dma[p][r], 16)

            def root3(t, p, k):
                pool.wait_ge(evar, done(t))
                pool.tensor_tensor(rstd[:, p:p + 1], ve[:, p:p + 1], mhalf[:], ALU.pow).then_inc(erst, 1)

            pipeline(pool, NT, [(0, gather), (1, root3)])

        @block.tensor
        def _(pe):
            def turn(bank, w):
                for kc in range(KD):
                    for ko in range(KD):
                        mm = pe.transpose(ps[:, bank, kc * D + ko * P:kc * D + (ko + 1) * P],
                                          w[:, ko, kc * P:(kc + 1) * P], ident[:])
                mm.then_inc(c_pe, 1)

            pe.wait_ge(c_pool, 18)
            pe.wait_ge(ld_w, 32)
            turn(0, n_out)
            pe.wait_ge(ld_wx, 80)
            for n in range(4):
                turn(1 + n, n_x[:, n])
            for kc in range(KD):
                mm = pe.transpose(ps[:, 5, kc * P:(kc + 1) * P], n_ctx[:, kc * P:(kc + 1) * P], ident[:])
            mm.then_inc(c_pe, 1)
            for kc in range(KD):
                for ko in range(KD):
                    mm = pe.matmul(ps[:, 6, kc * D:(kc + 1) * D], n_qkv[:, ko, kc * P:(kc + 1) * P],
                                   n_qkv[:, KD + ko], start=ko == 0, stop=ko == KD - 1)
            mm.then_inc(c_mm, 1)
            pe.wait_ge(c_dve, 1)
            for kc in range(KD):
                for ko in range(KD):
                    mm = pe.matmul(ps[:, 7, kc * D:(kc + 1) * D], n_qkv[:, 2 * KD + ko, kc * P:(kc + 1) * P],
                                   aoT[:, ko], start=ko == 0, stop=ko == KD - 1)
            mm.then_inc(c_mm, 1)
            pe.wait_ge(c_dve, 8)
            pe.wait_ge(ld_c, 16 * 9)
            for ko in range(KD):
                pe.matmul(ps[:, 0, 0:D], bvr[:, ko], aoT[:, ko], start=ko == 0, stop=ko == KD - 1)
            for kc in range(KD):
                for ko in range(KD):
                    mm = pe.matmul(ps[:, 0, D + kc:D + kc + 1], n_qkv[:, KD + ko, kc * P:(kc + 1) * P],
                                   bq[:, ko:ko + 1], start=ko == 0, stop=ko == KD - 1)
            mm.then_inc(c_mm, 1)
            pe.wait_ge(c_dve, 9)
            for ko in range(KD):
                for ki in range(KD):
                    mm = pe.matmul(ps[:, 1, ko * P:(ko + 1) * P], wkT[:, ki, ko * P:(ko + 1) * P], cT[:, ki],
                                   start=ki == 0, stop=ki == KD - 1)
            mm.then_inc(c_mm, 1)
            for b in range(B):
                for ki in range(KD):
                    mm = pe.matmul(ps[:, 2, b * D:(b + 1) * D], cT2[:, ki, b].rearrange("p a k -> p (a k)"),
                                   wvT[:, ki], start=ki == 0, stop=ki == KD - 1)
            mm.then_inc(c_mm, 1)
            pe.wait_ge(c_dve, 40)
            pe.wait_ge(c_act, 4)

            def turn_x(t, p, k):
                pe.wait_ge(ld_x[p], 16 * k + 16)
                pe.wait_ge(sTl, freed(t))
                for kc in range(KD):
                    mm = pe.transpose(ps[:, p, kc * P:(kc + 1) * P], xs[:, p, kc * P:(kc + 1) * P], ident[:])
                mm.then_inc(xT_ps, 1)

            def values(t, p, k):
                pe.wait_ge(sTl, done(t))
                pe.wait_ge(sTh, done(t))
                pe.wait_ge(vl, freed(t))
                for kc in range(KD):
                    mm = mm3(pe, ps[:, 2 + p, 0:D], sT_h[:, p, kc], sT_l[:, p, kc], wvo_h[:, kc], wvo_l[:, kc],
                             kc == 0, kc == KD - 1)
                mm.then_inc(v_ps, 1)

            pipeline(pe, NT, [(0, turn_x), (1, values)])
            pe.wait_ge(vl, done(NT - 1))
            pe.wait_ge(vh, done(NT - 1))
            pe.wait_ge(xTcopy, done(NT - 1))

            def query(t, p, k):
                pe.wait_ge(ql, freed(t) + 1)
                if not (isinstance(t, int) and t < 4):
                    pe.wait_ge(x1l, done(t - 4))
                for jc in range(KD):
                    for ic in range(KD):
                        mm = mm3(pe, ps[:, 6, jc * P:(jc + 1) * P],
                                 a_h[:, ic, jc * P:(jc + 1) * P], a_l[:, ic, jc * P:(jc + 1) * P],
                                 xT_h[:, ic, ds(t * P, P)], xT_l[:, ic, ds(t * P, P)], ic == 0, ic == KD - 1)
                mm.then_inc(q_ps, 1)

            def scores(t, p, k):
                pe.wait_ge(ql, done(t))
                pe.wait_ge(qh, done(t))
                pe.wait_ge(ex, freed(t))
                b = t // TPB
                for jc in range(KD):
                    for kh in range(2):
                        mm = mm3(pe, ps[:, 2 * p + kh, :], q_h[:, p, jc], q_l[:, p, jc],
                                 xT_h[:, jc, ds(b * S + kh * 512, 512)], xT_l[:, jc, ds(b * S + kh * 512, 512)],
                                 jc == 0, jc == KD - 1)
                mm.then_inc(s_ps, 1)

            def turn_p(t, p, k):
                pe.wait_ge(ex, done(t))
                pe.wait_ge(ptl, freed(t) + 1)
                for kt in range(TPB):
                    mm = pe.transpose(ps[:, 4 + kt // 4, (kt % 4) * P:(kt % 4 + 1) * P],
                                      prob[:, p, kt * P:(kt + 1) * P], ident[:])
                mm.then_inc(tp, 1)

            def attend(t, p, k):
                pe.wait_ge(ptl, done(t))
                pe.wait_ge(pth, done(t))
                pe.wait_ge(res, freed(t) + 1)
                b = t // TPB
                for kt in range(TPB):
                    mm = mm3(pe, ps[:, 7, 0:D], pT_h[:, kt], pT_l[:, kt],
                             v_h[:, ds(b * TPB + kt, 1), :].rearrange("p a d -> p (a d)"),
                             v_l[:, ds(b * TPB + kt, 1), :].rearrange("p a d -> p (a d)"), kt == 0, kt == TPB - 1)
                mm.then_inc(o_ps, 1)

            def turn_x1(t, p, k):
                pe.wait_ge(x1, done(t))
                pe.wait_ge(x1l, freed(t) + 1)
                pe.wait_ge(ql, done(upto(t, 3)))
                for kc in range(KD):
                    mm = pe.transpose(ps[:, 6, D + kc * P:D + (kc + 1) * P], xs[:, p, kc * P:(kc + 1) * P], ident[:])
                mm.then_inc(t1, 1)

            pipeline(pe, NT, [(1, scores), (0, query), (2, turn_p), (2, attend), (3, turn_x1)])
            pe.wait_ge(x1l, done(NT - 1))
            pe.wait_ge(x1h, done(NT - 1))

            def cquery(t, p, k):
                pe.wait_ge(cql, freed(t) + 1)
                for oc in range(KD):
                    for ic in range(KD):
                        mm = mm3(pe, ps[:, 4, oc * P:(oc + 1) * P],
                                 wq_h[:, ic, oc * P:(oc + 1) * P], wq_l[:, ic, oc * P:(oc + 1) * P],
                                 x1T_h[:, ic, ds(t * P, P)], x1T_l[:, ic, ds(t * P, P)], ic == 0, ic == KD - 1)
                mm.then_inc(cq_ps, 1)

            def cscores(t, p, k):
                pe.wait_ge(cql, done(t))
                pe.wait_ge(cqh, done(t))
                pe.wait_ge(cmul, freed(t) + 1)
                b = t // TPB
                for hc in range(KD):
                    mm = mm3(pe, ps[:, hc, :], q_h[:, p, hc], q_l[:, p, hc],
                             kb_h[:, ds(b * KD + hc, 1)].rearrange("p a h k -> p (a h k)"),
                             kb_l[:, ds(b * KD + hc, 1)].rearrange("p a h k -> p (a h k)"), True, True)
                mm.then_inc(cs_ps, 1)

            def cturn_p(t, p, k):
                pe.wait_ge(cex, done(t))
                pe.wait_ge(cptl, freed(t) + 1)
                for g in range(PAIRS):
                    mm = pe.transpose(ps[:, 2 + g // 4, (g % 4) * P:(g % 4 + 1) * P],
                                      prob[:, p, g * P:(g + 1) * P], ident[:])
                mm.then_inc(ctp, 1)

            def cattend(t, p, k):
                pe.wait_ge(cptl, done(t))
                pe.wait_ge(cpth, done(t))
                pe.wait_ge(co, freed(t) + 1)
                b = t // TPB
                for g in range(PAIRS):
                    mm = mm3(pe, ps[:, 5, g * 2 * VW:(g + 1) * 2 * VW], pT_h[:, g], pT_l[:, g],
                             vb_h[:, ds(b, 1), g].rearrange("p a c -> p (a c)"),
                             vb_l[:, ds(b, 1), g].rearrange("p a c -> p (a c)"), True, True)
                mm.then_inc(co_ps, 1)

            def turn_o(t, p, k):
                pe.wait_ge(co, done(t))
                pe.wait_ge(cotl, freed(t) + 1)
                pe.wait_ge(x2t, freed(t))
                for kc in range(KD):
                    mm = pe.transpose(ps[:, 6, kc * P:(kc + 1) * P], octx[:, p, kc * P:(kc + 1) * P], ident[:])
                mm.then_inc(cot, 1)

            def project(t, p, k):
                pe.wait_ge(cotl, done(t))
                pe.wait_ge(coth, done(t))
                pe.wait_ge(cres, freed(t) + 1)
                pe.wait_ge(lgb, freed(t))
                if not (isinstance(t, int) and t < 3):
                    pe.wait_ge(lcar, done(t - 3))
                for kc in range(KD):
                    mm = mm3(pe, ps[:, 7, 0:D], oT_h[:, kc], oT_l[:, kc], wo_h[:, kc], wo_l[:, kc],
                             kc == 0, kc == KD - 1)
                mm.then_inc(cy, 1)

            def turn_x2(t, p, k):
                pe.wait_ge(x2, done(t))
                pe.wait_ge(x2t, freed(t) + 1)
                for kc in range(KD):
                    mm = pe.transpose(ps[:, 6, D + kc * P:D + (kc + 1) * P], xs[:, p, kc * P:(kc + 1) * P], ident[:])
                mm.then_inc(t2, 1)

            def logits(t, p, k):
                pe.wait_ge(x2t, done(t))
                pe.wait_ge(lgb, freed(t) + 1)
                pe.wait_ge(cres, done(upto(t, 1)))
                if not (isinstance(t, int) and t < 1):
                    pe.wait_ge(lcar, done(t - 1))
                for kc in range(KD):
                    mm = pe.matmul(ps[:, 7, D:D + E], x2T[:, p, kc], rw[:, kc], start=kc == 0, stop=kc == KD - 1)
                mm.then_inc(lg_ps, 1)

            def positions(t, p, k):
                pe.wait_ge(lmk, done(t))
                pe.wait_ge(lcar, freed(t) + 1)
                pe.wait_ge(cres, done(upto(t, 2)))
                pe.wait_ge(lgb, done(upto(t, 0)))
                pe.matmul(ps[:, 7, D + E:D + 2 * E], tri[:], mk[:, p], start=True, stop=True)
                pe.matmul(ps[:, 7, D + 2 * E:D + 3 * E], ones[:], mk[:, p], start=True, stop=True).then_inc(pos_ps, 1)

            pipeline(pe, NT, [(1, cscores), (6, positions), (5, logits), (0, cquery), (2, cturn_p), (3, turn_o),
                              (2, cattend), (3, project), (4, turn_x2)])
            pe.wait_ge(lcar, done(NT - 1))

            def turn_g(t, p, k):
                pe.wait_ge(f_x[p], 16 * k + 16)
                pe.wait_ge(gtl, freed(t))
                for c in range(2):
                    for kc in range(KD):
                        mm = pe.transpose(ps[:, p, kc * SLOT + c * P:kc * SLOT + (c + 1) * P],
                                          xg[:, p, c, kc * P:(kc + 1) * P], ident[:])
                mm.then_inc(gt, 1)

            def up(t, p, k):
                pe.wait_ge(gtl, done(t))
                pe.wait_ge(gth, done(t))
                pe.wait_ge(w1l, done(t))
                pe.wait_ge(gel, freed(t))
                for j in range(KI):
                    for kc in range(KD):
                        mm = mm3(pe, ps[:, 2 + 2 * p + j // 2, (j % 2) * SLOT:(j % 2 + 1) * SLOT],
                                 w1_h[:, p, kc, j::KI], w1_l[:, p, kc, j::KI], gT_h[:, p, kc], gT_l[:, p, kc],
                                 kc == 0, kc == KD - 1)
                mm.then_inc(hps, 1)

            def down(t, p, k):
                pe.wait_ge(hl, done(t))
                pe.wait_ge(hh, done(t))
                pe.wait_ge(w2l, done(t))
                pe.wait_ge(yok, freed(t))
                for c in range(2):
                    for j in range(KI):
                        mm = mm3(pe, ps[:, 6 + p, c * D:(c + 1) * D], h_h[:, p, j, c * P:(c + 1) * P],
                                 h_l[:, p, j, c * P:(c + 1) * P], w2_h[:, p, j], w2_l[:, p, j], j == 0, j == KI - 1)
                mm.then_inc(yps, 1)

            pipeline(pe, NSTEP, [(1, up), (0, turn_g), (2, down)])

        @block.scalar
        def _(act):
            for kc in range(KD):
                for dst, base in ((bq, 0), (bv, 2 * D)):
                    act.dma_start(dst[:, kc:kc + 1], qkv_b[base + kc * P:base + (kc + 1) * P].rearrange("(p o) -> p o", o=1)).then_inc(ld_c, 16)
            act.dma_start(bo[:], out_b.rearrange("(o d) -> o d", o=1).broadcast_to([P, D])).then_inc(ld_c, 16)
            act.dma_start(mask_i[:].rearrange("p b k -> p (b k)"),
                          mask.rearrange("b k -> (b k)").rearrange("(o n) -> o n", o=1).broadcast_to([P, B * SK])).then_inc(ld_c, 16)
            act.dma_start(rb[:], router_b.rearrange("(o e) -> o e", o=1).broadcast_to([P, E])).then_inc(ld_c, 16)
            for kc in range(KD):
                act.dma_start(rw[:, kc], router_w[kc * P:(kc + 1) * P, :]).then_inc(ld_c, 16)

            act.wait_ge(c_pe, 2)
            act.activation(wq_h[:].rearrange("p k c -> p (k c)"), ps[:, 1], ACT.Copy).then_inc(c_act, 1)
            act.wait_ge(c_pe, 5)
            act.activation(wo_h[:].rearrange("p k c -> p (k c)"), ps[:, 4], ACT.Copy).then_inc(c_act, 1)
            act.wait_ge(c_mm, 1)
            act.activation(a_h[:].rearrange("p k c -> p (k c)"), ps[:, 6], ACT.Copy).then_inc(c_act, 1)
            act.wait_ge(c_mm, 2)
            act.activation(wvo_h[:].rearrange("p k c -> p (k c)"), ps[:, 7], ACT.Copy).then_inc(c_act, 1)

            def x_high(t, p, k):
                act.wait_ge(xT_ps, done(t))
                act.wait_ge(v_ps, freed(t))
                act.wait_ge(xTcopy, freed(t))
                act.activation(sT_h[:, p].rearrange("p k c -> p (k c)"), ps[:, p, 0:D], ACT.Copy).then_inc(sTh, 1)

            def v_high(t, p, k):
                act.wait_ge(v_ps, done(t))
                act.activation(v_h[:, ds(t, 1), :].rearrange("p a d -> p (a d)"), ps[:, 2 + p, 0:D], ACT.Copy).then_inc(vh, 1)

            pipeline(act, NT, [(0, x_high), (1, v_high)])

            def q_high(t, p, k):
                act.wait_ge(q_ps, done(t))
                act.wait_ge(s_ps, freed(t))
                for jc in range(KD):
                    ins = act.activation(q_h[:, p, jc], ps[:, 6, jc * P:(jc + 1) * P], ACT.Identity,
                                         bias=u[:, jc:jc + 1])
                ins.then_inc(qh, 1)

            def p_high(t, p, k):
                act.wait_ge(tp, done(t))
                act.wait_ge(o_ps, freed(t) + 1)
                act.activation(pT_h[:].rearrange("p k c -> p (k c)"), ps[:, 4:6].rearrange("p b c -> p (b c)"),
                               ACT.Copy).then_inc(pth, 1)

            def exps(t, p, k):
                act.wait_ge(mxs, done(t))
                act.wait_ge(s_ps, done(t))
                act.wait_ge(tp, freed(t))
                act.wait_ge(ri, freed(t))
                act.activation(prob[:, p], ps[:, 2 * p:2 * p + 2].rearrange("p b c -> p (b c)"), ACT.Exp,
                               bias=nmaxs[:, p:p + 1], scale=1.0 / 16.0, accum_out=rsum[:, p:p + 1]).then_inc(ex, 1)

            def x1_high(t, p, k):
                act.wait_ge(t1, done(t))
                act.activation(x1T_h[:, :, ds(t * P, P)], ps[:, 6, D:2 * D].rearrange("p (k c) -> p k c", c=P),
                               ACT.Copy).then_inc(x1h, 1)

            pipeline(act, NT, [(0, q_high), (2, p_high), (1, exps), (3, x1_high)])

            def cq_high(t, p, k):
                act.wait_ge(cq_ps, done(t))
                act.wait_ge(cs_ps, freed(t))
                act.activation(q_h[:, p].rearrange("p k c -> p (k c)"), ps[:, 4, 0:D], ACT.Copy).then_inc(cqh, 1)

            def cp_high(t, p, k):
                act.wait_ge(ctp, done(t))
                act.wait_ge(co_ps, freed(t) + 1)
                act.activation(pT_h[:].rearrange("p k c -> p (k c)"), ps[:, 2:4].rearrange("p b c -> p (b c)"),
                               ACT.Copy).then_inc(cpth, 1)

            def o_high(t, p, k):
                act.wait_ge(cot, done(t))
                act.wait_ge(cy, freed(t) + 1)
                act.activation(oT_h[:].rearrange("p k c -> p (k c)"), ps[:, 6, 0:D], ACT.Copy).then_inc(coth, 1)

            def cexps(t, p, k):
                act.wait_ge(csub, done(t))
                act.activation(prob[:, p], prob[:, p], ACT.Exp, scale=0.25).then_inc(cex, 1)

            def x2_turned(t, p, k):
                act.wait_ge(t2, done(t))
                act.wait_ge(lg_ps, freed(t))
                act.activation(x2T[:, p].rearrange("p k c -> p (k c)"), ps[:, 6, D:2 * D], ACT.Copy).then_inc(x2t, 1)

            def rexps(t, p, k):
                act.wait_ge(lmx, done(t))
                act.activation(lexp[:, p], lg[:, p], ACT.Exp, bias=lmax[:, p:p + 1], accum_out=lsum[:, p:p + 1]).then_inc(lex, 1)

            pipeline(act, NT, [(0, cq_high), (2, cp_high), (3, o_high), (5, rexps), (1, cexps), (4, x2_turned)])

            def g_high(t, p, k):
                act.wait_ge(gt, done(t))
                act.wait_ge(hps, freed(t))
                act.activation(gT_h[:, p].rearrange("p k c -> p (k c)"), ps[:, p], ACT.Copy).then_inc(gth, 1)

            def gelus(t, p, k):
                act.wait_ge(hps, done(t))
                act.wait_ge(f_b1[p], 16 * k + 16)
                act.wait_ge(hl, freed(t))
                act.wait_ge(hh, freed(t))
                for j in range(KI):
                    ins = act.activation(hf[:, p, j], ps[:, 2 + 2 * p + j // 2, (j % 2) * SLOT:(j % 2 + 1) * SLOT],
                                         ACT.Gelu, bias=b1f[:, p, j:j + 1])
                ins.then_inc(gel, 1)

            def h_high(t, p, k):
                act.wait_ge(gel, done(t))
                act.wait_ge(yps, freed(t))
                act.activation(h_h[:, p], hf[:, p], ACT.Copy).then_inc(hh, 1)

            def store_step(t, p, k):
                act.wait_ge(yok, done(t))
                act.dma_start(yg_dram[ds(t * SLOT, SLOT), :].rearrange("(c p) d -> p c d", p=P), yb[:, p]).then_inc(st_y[p], 16)

            pipeline(act, NSTEP, [(4, store_step), (1, gelus), (0, g_high), (1, h_high)])

        @block.vector
        def _(dve):
            n = [0]

            def step(ins):
                n[0] += 1
                ins.then_inc(c_dve, 1)

            def low(o, src, hi):
                step(dve.tensor_tensor(o, src, f(hi), ALU.subtract))

            flat = "p k c -> p (k c)"
            dve.wait_ge(c_pe, 1)
            step(dve.tensor_copy(aoT[:].rearrange(flat), ps[:, 0]))
            dve.wait_ge(c_pe, 4)
            step(dve.tensor_copy(wkT[:].rearrange(flat), ps[:, 2]))
            step(dve.tensor_copy(wvT[:].rearrange(flat), ps[:, 3]))
            dve.wait_ge(c_pe, 6)
            step(dve.tensor_copy(cT[:].rearrange(flat), ps[:, 5, 0:D]))
            for a in range(2):
                step(dve.tensor_copy(cT2[:, :, :, a], ps[:, 5, 0:D].rearrange("p (k b s) -> p k b s", b=B, s=SK)))
            dve.wait_ge(ld_c, 16 * 9)
            for kc in range(KD):
                step(dve.tensor_copy(bvr[:, kc], bv[:, kc:kc + 1].broadcast_to([P, P])))
            dve.wait_ge(c_act, 1)
            low(wq_l[:].rearrange(flat), ps[:, 1], wq_h[:].rearrange(flat))
            dve.wait_ge(c_act, 2)
            low(wo_l[:].rearrange(flat), ps[:, 4], wo_h[:].rearrange(flat))
            dve.wait_ge(c_act, 3)
            low(a_l[:].rearrange(flat), ps[:, 6], a_h[:].rearrange(flat))
            dve.wait_ge(c_act, 4)
            low(wvo_l[:].rearrange(flat), ps[:, 7], wvo_h[:].rearrange(flat))
            step(dve.tensor_scalar(keep[:], mask_i[:], 0.0, None, ALU.not_equal))
            dve.wait_ge(c_dve, n[0])
            for b in range(B):
                step(dve.tensor_copy(msk_mul[:, b * TPB:(b + 1) * TPB], keep[:, b].unsqueeze(1).broadcast_to([P, TPB, SK])))
            dve.wait_ge(c_dve, n[0])
            step(dve.memset(f(vb_h[:]), 0.0))
            dve.sem_inc(m_rep, 1)
            step(dve.memset(f(vb_l[:]), 0.0))
            dve.wait_ge(m_mul, B)
            step(dve.tensor_scalar(msk_add[:], msk_mul[:], -1.0, -NEG * 4.0, ALU.add, ALU.mult))
            dve.wait_ge(c_mm, 3)
            step(dve.tensor_copy(u[:], ps[:, 0, D:D + KD]))
            step(dve.tensor_tensor(vo[:], ps[:, 0, 0:D], bo[:], ALU.add))
            assert n[0] == 20, n[0]
            dve.wait_ge(c_mm, 4)
            step(dve.tensor_copy(kt_h[:].rearrange(flat), ps[:, 1, 0:D]))
            dve.wait_ge(c_dve, n[0])
            low(kt_l[:].rearrange(flat), ps[:, 1, 0:D], kt_h[:].rearrange(flat))
            dve.wait_ge(c_dve, n[0])
            dve.wait_ge(c_pool, 18)
            for b in range(B):
                for hc in range(KD):
                    for src, dst in ((f(kt_h[:]), kb_h), (kt_l[:], kb_l)):
                        step(dve.tensor_tensor(dst[:, b * KD + hc], src[:, hc, b * SK:(b + 1) * SK].unsqueeze(1).broadcast_to([P, HPC, SK]),
                                               blk[:].unsqueeze(2).broadcast_to([P, HPC, SK]), ALU.mult))
            dve.wait_ge(c_mm, 5)
            for b in range(B):
                for a in range(2):
                    rows = slice(a * SK, (a + 1) * SK)
                    src = ps[rows, 2, b * D:(b + 1) * D].rearrange("p (g h d) -> p g h d", h=2, d=DK)[:, :, a]
                    step(dve.tensor_copy(vb_h[rows, b, :, a * VW:a * VW + DK], src))
                    dve.wait_ge(c_dve, n[0])
                    step(dve.tensor_tensor(vb_l[rows, b, :, a * VW:a * VW + DK], src, f(vb_h[rows, b, :, a * VW:a * VW + DK]), ALU.subtract))
            for a in range(2):
                rows = slice(a * SK, (a + 1) * SK)
                step(dve.memset(f(vb_h[rows, :, :, a * VW + DK:(a + 1) * VW]), 1.0))
            assert n[0] == 40, n[0]

            def x_low(t, p, k):
                dve.wait_ge(sTh, done(t))
                dve.wait_ge(v_ps, freed(t))
                dve.wait_ge(xTcopy, freed(t))
                dve.tensor_tensor(sT_l[:, p].rearrange(flat), ps[:, p, 0:D], f(sT_h[:, p].rearrange(flat)), ALU.subtract).then_inc(sTl, 1)

            def v_low(t, p, k):
                dve.wait_ge(vh, done(t))
                dve.tensor_tensor(v_l[:, ds(t, 1), :].rearrange("p a d -> p (a d)"), ps[:, 2 + p, 0:D],
                                  f(v_h[:, ds(t, 1), :].rearrange("p a d -> p (a d)")), ALU.subtract).then_inc(vl, 1)

            pipeline(dve, NT, [(0, x_low), (1, v_low)])

            def norm(t, p, src, dst, s_in, s_bn, s_ag, s_var, s_rst, s_out):
                dve.wait_ge(s_in, done(t))
                dve.bn_stats(bn[:, p], src).then_inc(s_bn, 1)
                dve.wait_ge(s_bn, done(t))
                dve.sem_inc(passed, 1)
                dve.bn_aggr(mv[:, p], bn[:, p]).then_inc(s_ag, 1)
                dve.wait_ge(s_ag, done(t))
                dve.tensor_scalar(ve[:, p:p + 1], mv[:, p, 1:2], EPS, None, ALU.add).then_inc(s_var, 1)
                dve.wait_ge(s_rst, done(t))
                dve.tensor_scalar(dst, src, mv[:, p, 0:1], rstd[:, p:p + 1], ALU.subtract, ALU.mult).then_inc(s_out, 1)

            dve.wait_ge(xres, done(NT - 1))

            def row_max(t, p, k):
                dve.wait_ge(s_ps, done(t))
                dve.wait_ge(ex, freed(t))
                dve.tensor_reduce(nmax[:, p:p + 1], ps[:, 2 * p:2 * p + 2].rearrange("p b c -> p (b c)"), AX.X, ALU.max).then_inc(mx, 1)
                dve.wait_ge(mx, done(t))
                dve.tensor_scalar(nmaxs[:, p:p + 1], nmax[:, p:p + 1], -1.0 / 16.0, None, ALU.mult).then_inc(mxs, 1)

            def q_low(t, p, k):
                dve.wait_ge(qh, done(t))
                dve.wait_ge(s_ps, freed(t))
                for jc in range(KD):
                    ins = dve.scalar_tensor_tensor(q_l[:, p, jc], ps[:, 6, jc * P:(jc + 1) * P], u[:, jc:jc + 1],
                                                   f(q_h[:, p, jc]), ALU.add, ALU.subtract)
                ins.then_inc(ql, 1)

            def p_low(t, p, k):
                dve.wait_ge(pth, done(t))
                dve.wait_ge(o_ps, freed(t) + 1)
                dve.tensor_tensor(pT_l[:].rearrange(flat), ps[:, 4:6].rearrange("p b c -> p (b c)"), f(pT_h[:].rearrange(flat)),
                                  ALU.subtract).then_inc(ptl, 1)

            def finish(t, p, k):
                dve.wait_ge(ex, done(t))
                dve.reciprocal(rinv[:, p:p + 1], rsum[:, p:p + 1]).then_inc(ri, 1)
                dve.wait_ge(ri, done(t))
                dve.wait_ge(o_ps, done(t))
                dve.scalar_tensor_tensor(yres[:, p], ps[:, 7, 0:D], rinv[:, p:p + 1],
                                         x_all[:, ds(t, 1), :].rearrange("p a d -> p (a d)"), ALU.mult, ALU.add).then_inc(res, 1)
                dve.wait_ge(t1, freed(t))
                dve.wait_ge(x1c, freed(t))
                norm(t, p, yres[:, p], xs[:, p], res, bns, bna, var, rst, x1)

            def x1_low(t, p, k):
                dve.wait_ge(x1h, done(t))
                dve.tensor_tensor(x1T_l[:, :, ds(t * P, P)], ps[:, 6, D:2 * D].rearrange("p (k c) -> p k c", c=P),
                                  f(x1T_h[:, :, ds(t * P, P)]), ALU.subtract).then_inc(x1l, 1)

            pipeline(dve, NT, [(1, row_max), (0, q_low), (2, p_low), (2, finish), (3, x1_low)])

            heads = "p (h k) -> p h k"

            def mask_mul(t, p, k):
                dve.wait_ge(cs_ps, done(t))
                dve.wait_ge(ctp, freed(t))
                dve.tensor_tensor(prob[:, p].rearrange(heads, k=SK), ps[:, 0:2].rearrange("p b (h k) -> p (b h) k", k=SK),
                                  msk_mul[:, ds(t, 1), :].broadcast_to([P, HEADS, SK]), ALU.mult).then_inc(cmul, 1)

            def cq_low(t, p, k):
                dve.wait_ge(cqh, done(t))
                dve.wait_ge(cs_ps, freed(t))
                dve.tensor_tensor(q_l[:, p].rearrange(flat), ps[:, 4, 0:D], f(q_h[:, p].rearrange(flat)), ALU.subtract).then_inc(cql, 1)

            def cp_low(t, p, k):
                dve.wait_ge(cpth, done(t))
                dve.wait_ge(co_ps, freed(t) + 1)
                dve.tensor_tensor(pT_l[:].rearrange(flat), ps[:, 2:4].rearrange("p b c -> p (b c)"), f(pT_h[:].rearrange(flat)),
                                  ALU.subtract).then_inc(cptl, 1)

            def o_low(t, p, k):
                dve.wait_ge(coth, done(t))
                dve.wait_ge(cy, freed(t) + 1)
                dve.tensor_tensor(oT_l[:].rearrange(flat), ps[:, 6, 0:D], f(oT_h[:].rearrange(flat)), ALU.subtract).then_inc(cotl, 1)

            def head_max(t, p, k):
                dve.wait_ge(cadd, done(t))
                dve.wait_ge(csub, freed(t))
                dve.tensor_reduce(hmax[:, p], prob[:, p].rearrange(heads, k=SK), AX.X, ALU.max).then_inc(cmx, 1)

            def head_norm(t, p, k):
                dve.wait_ge(co_ps, done(t))
                dve.wait_ge(cot, freed(t))
                o = ps[:, 5, 0:PAIRS * 2 * VW].rearrange("p (h c) -> p h c", c=VW)
                dve.reciprocal(hinv[:, p].unsqueeze(2), o[:, :, DK:VW]).then_inc(cinv, 1)
                dve.wait_ge(cinv, done(t))
                dve.tensor_tensor(octx[:, p].rearrange("p (h d) -> p h d", d=DK), o[:, :, 0:DK],
                                  hinv[:, p].unsqueeze(2).broadcast_to([P, HEADS, DK]), ALU.mult).then_inc(co, 1)

            def finish2(t, p, k):
                dve.wait_ge(cy, done(t))
                dve.tensor_tensor(yres[:, p], ps[:, 7, 0:D],
                                  x_all[:, ds(t, 1), :].rearrange("p a d -> p (a d)"), ALU.add).then_inc(cres, 1)
                dve.wait_ge(t2, freed(t))
                dve.wait_ge(x2c, freed(t))
                norm(t, p, yres[:, p], xs[:, p], cres, cbns, cbna, cvar, crst, x2)

            def route_a(t, p, k):
                dve.wait_ge(lg_ps, done(t))
                dve.tensor_tensor(lg[:, p], ps[:, 7, D:D + E], rb[:], ALU.add).then_inc(lgb, 1)
                dve.wait_ge(lgb, done(t))
                dve.tensor_reduce(lmax[:, p:p + 1], lg[:, p], AX.X, ALU.max, negate=True).then_inc(lmx, 1)

            def route_b(t, p, k):
                dve.wait_ge(lex, done(t))
                dve.reciprocal(linv[:, p:p + 1], lsum[:, p:p + 1]).then_inc(lin, 1)
                dve.wait_ge(lin, done(t))
                dve.tensor_scalar(rp[:, p], lexp[:, p], linv[:, p:p + 1], None, ALU.mult).then_inc(lpr, 1)
                dve.wait_ge(lpr, done(t))
                dve.sem_inc(passed, 1)
                dve.max(mx8[:, p], rp[:, p]).then_inc(l8, 1)
                dve.wait_ge(l8, done(t))
                dve.sem_inc(passed, 1)
                dve.max_index(ix8[:, p], mx8[:, p], rp[:, p]).then_inc(li8, 1)
                dve.tensor_reduce(wsum[:, p:p + 1], mx8[:, p, 0:K], AX.X, ALU.add).then_inc(lws, 1)
                dve.wait_ge(li8, done(t))
                dve.tensor_copy(ixf[:, p], ix8[:, p, 0:K]).then_inc(lif, 1)
                dve.wait_ge(lws, done(t))
                dve.reciprocal(winv[:, p:p + 1], wsum[:, p:p + 1]).then_inc(lwi, 1)
                dve.wait_ge(lif, done(t))
                dve.tensor_tensor(oh[:, p], iota16[:].unsqueeze(1).broadcast_to([P, K, E]),
                                  ixf[:, p].unsqueeze(2).broadcast_to([P, K, E]), ALU.is_equal).then_inc(loh, 1)
                dve.tensor_copy(exp_all[:, ds(t, 1), :].rearrange("p a r -> p (a r)"), ixf[:, p]).then_inc(lxa, 1)
                dve.wait_ge(lwi, done(t))
                dve.tensor_scalar(wts_all[:, ds(t, 1), :].rearrange("p a r -> p (a r)"), mx8[:, p, 0:K], winv[:, p:p + 1], None, ALU.mult).then_inc(lw, 1)
                dve.wait_ge(loh, done(t))
                dve.wait_ge(pos_ps, freed(t))
                dve.tensor_reduce(mk[:, p], oh[:, p].rearrange("p r e -> p e r"), AX.X, ALU.add).then_inc(lmk, 1)

            def route_c(t, p, k):
                dve.wait_ge(pos_ps, done(t))
                dve.wait_ge(lcar, freed(t) + 1)
                dve.tensor_tensor(pos[:, p], ps[:, 7, D + E:D + 2 * E], carry[:], ALU.add).then_inc(lpos, 1)
                dve.tensor_tensor(carry[:], ps[:, 7, D + 2 * E:D + 3 * E], carry[:], ALU.add).then_inc(lcar, 1)

            def route_d(t, p, k):
                dve.wait_ge(lpos, done(t))
                dve.tensor_tensor(ohp[:, p], oh[:, p], pos[:, p].unsqueeze(1).broadcast_to([P, K, E]), ALU.mult).then_inc(lohp, 1)
                dve.wait_ge(lohp, done(t))
                dve.tensor_reduce(slotf[:, p], ohp[:, p], AX.X, ALU.add).then_inc(lsl, 1)
                dve.wait_ge(lsl, done(t))
                for r in range(K):
                    if not (isinstance(t, int) and t < 2):
                        dve.wait_ge(sc_dma[p][r], 16 * k)
                dve.tensor_copy(idx[:, p], slotf[:, p]).then_inc(lidx, 1)
                dve.tensor_copy(slot_all[:, ds(t, 1), :].rearrange("p a r -> p (a r)"), slotf[:, p]).then_inc(lall, 1)

            pipeline(dve, NT, [(1, mask_mul), (6, route_c), (5, route_a), (0, cq_low), (2, cp_low), (3, o_low), (1, head_max),
                               (2, head_norm), (3, finish2), (6, route_d), (5, route_b)])

            m = [0]

            def tstep(ins):
                m[0] += 1
                ins.then_inc(tb_pool, 1)
                dve.wait_ge(tb_pool, m[0])

            NB = CAP // SLOT
            dve.wait_ge(lcar, done(NT - 1))
            tstep(dve.scalar_tensor_tensor(cnt[:], iota16[:], -float(CAP), carry[:], ALU.mult, ALU.add))
            tstep(dve.tensor_tensor(cmp8[:], cnt[:].unsqueeze(2).broadcast_to([P, E, NB]),
                                    thr[:].unsqueeze(1).broadcast_to([P, E, NB]), ALU.is_gt))
            tstep(dve.tensor_reduce(ntile[:], cmp8[:], AX.X, ALU.add))
            tstep(dve.tensor_tensor(cmpe[:], trie[:], ntile[:].unsqueeze(1).broadcast_to([P, E, E]), ALU.mult))
            tstep(dve.tensor_reduce(ends[:], cmpe[:], AX.X, ALU.add))
            tstep(dve.tensor_tensor(past[:], sid[:].unsqueeze(2).broadcast_to([1, NSTEP, E]),
                                    ends[0:1].unsqueeze(1).broadcast_to([1, NSTEP, E]), ALU.is_ge))
            tstep(dve.tensor_reduce(es[:], past[:], AX.X, ALU.add))
            tstep(dve.tensor_tensor(past2[:], past[:], ntile[0:1].unsqueeze(1).broadcast_to([1, NSTEP, E]), ALU.mult))
            tstep(dve.tensor_reduce(st[:], past2[:], AX.X, ALU.add))
            tstep(dve.tensor_scalar(live[:], es[:], float(E), None, ALU.is_lt))
            tstep(dve.tensor_tensor(row[:], sid[:], st[:], ALU.subtract))
            tstep(dve.tensor_scalar(row[:], row[:], float(SLOT), None, ALU.mult))
            tstep(dve.scalar_tensor_tensor(row[:], es[:], float(CAP), row[:], ALU.mult, ALU.add))
            tstep(dve.tensor_tensor(tabf[:, :, 0], row[:], live[:], ALU.mult))
            tstep(dve.tensor_scalar(tabf[:, :, 1], es[:], float(E - 1), None, ALU.min))
            tstep(dve.tensor_scalar(tabf[:, :, 2], tabf[:, :, 1], float(D), None, ALU.mult))
            tstep(dve.tensor_scalar(tabf[:, :, 3], tabf[:, :, 1], float(I), None, ALU.mult))
            dve.tensor_copy(tab[:], tabf[:]).then_inc(tb, 1)
            tstep(dve.tensor_tensor(first_row[:], ends[:], ntile[:], ALU.subtract))
            tstep(dve.tensor_scalar(first_row[:], first_row[:], float(SLOT), None, ALU.mult))
            tstep(dve.scalar_tensor_tensor(delta[:], iota16[:], -float(CAP), first_row[:], ALU.mult, ALU.add))
            dve.wait_ge(lall, done(NT - 1))
            tstep(dve.tensor_tensor(owner[:], iota16[:].unsqueeze(1).broadcast_to([P, NT * K, E]),
                                    exp_all[:].rearrange("p t r -> p (t r)").unsqueeze(2).broadcast_to([P, NT * K, E]), ALU.is_equal))
            tstep(dve.tensor_tensor(shift[:], owner[:], delta[:].unsqueeze(1).broadcast_to([P, NT * K, E]), ALU.mult))
            tstep(dve.tensor_reduce(moved[:], shift[:], AX.X, ALU.add))
            tstep(dve.tensor_tensor(yrow_all[:].rearrange("p t r -> p (t r)"), moved[:], slot_all[:].rearrange("p t r -> p (t r)"), ALU.add))

            def split_w1(t, p, k):
                dve.wait_ge(f_w1[p], 16 * k + 16)
                dve.wait_ge(hps, freed(t))
                dve.tensor_copy(w1_h[:, p], w1f[:, p]).then_inc(w1h, 1)
                dve.wait_ge(w1h, done(t))
                dve.tensor_tensor(w1_l[:, p], w1f[:, p], f(w1_h[:, p]), ALU.subtract).then_inc(w1l, 1)

            def w2_high(t, p, k):
                dve.wait_ge(f_w2[p], 16 * k + 16)
                dve.wait_ge(yps, freed(t))
                dve.tensor_copy(w2_h[:, p], w2f[:, p]).then_inc(w2h, 1)

            def g_low(t, p, k):
                dve.wait_ge(gth, done(t))
                dve.wait_ge(hps, freed(t))
                dve.tensor_tensor(gT_l[:, p].rearrange(flat), ps[:, p], f(gT_h[:, p].rearrange(flat)), ALU.subtract).then_inc(gtl, 1)

            def h_low(t, p, k):
                dve.wait_ge(hh, done(t))
                dve.wait_ge(yps, freed(t))
                dve.tensor_tensor(h_l[:, p], hf[:, p], f(h_h[:, p]), ALU.subtract).then_inc(hl, 1)

            def y_out(t, p, k):
                dve.wait_ge(yps, done(t))
                dve.wait_ge(f_b2[p], 16 * k + 16)
                if not (isinstance(t, int) and t < 2):
                    dve.wait_ge(st_y[p], 16 * k)
                dve.tensor_tensor(yb[:, p], ps[:, 6 + p].rearrange("p (c d) -> p c d", d=D),
                                  b2f[:, p].unsqueeze(1).broadcast_to([P, 2, D]), ALU.add).then_inc(yok, 1)

            pipeline(dve, NSTEP, [(3, y_out), (1, w2_high), (0, split_w1), (0, g_low), (1, h_low)])

            def stage_idx(t, p, k):
                if not (isinstance(t, int) and t < 2):
                    for r in range(K):
                        dve.wait_ge(g_dma[p][r], 16 * k)
                dve.tensor_copy(gidx[:, p], yrow_all[:, ds(t, 1), :].rearrange("p a r -> p (a r)")).then_inc(gix, 1)

            def combine(t, p, k):
                prev = x_all[:, ds(t, 1), :].rearrange("p a d -> p (a d)")
                for r in range(K):
                    dve.wait_ge(g_dma[p][r], 16 * k + 16)
                    if r:
                        dve.wait_ge(ac[r - 1], done(t))
                    dve.scalar_tensor_tensor(acc[:, p, r], gat[:, p, r], wts_all[:, ds(t, 1), r:r + 1].rearrange("p a r -> p (a r)"),
                                             prev, ALU.mult, ALU.add).then_inc(ac[r], 1)
                    prev = acc[:, p, r]
                if not (isinstance(t, int) and t < 2):
                    dve.wait_ge(st_o[p], 16 * k)
                norm(t, p, acc[:, p, K - 1], ot[:, p], ac[K - 1], ebns, ebna, evar, erst, eo)

            pipeline(dve, NT, [(0, stage_idx), (1, combine)])


_INS = ['x', 'ctx_1024', 'mask_BxS2_ik0', 'L0_attn_qkv_w', 'L0_attn_qkv_b', 'L0_attn_out_w', 'L0_attn_out_b',
        'L0_xattn_Wq', 'L0_xattn_Wk', 'L0_xattn_Wv', 'L0_xattn_Wo', 'L0_ffn_router_w', 'L0_ffn_router_b',
        'L0_ffn_w1', 'L0_ffn_b1', 'L0_ffn_w2', 'L0_ffn_b2']


def kernel(**inputs):
    import numpy as np
    import concourse.bacc as bacc
    from concourse.bass_utils import run_bass_kernel_spmd

    nc = bacc.Bacc("TRN2", target_bir_lowering=False, num_devices=1)
    arrays, args = {}, []
    for name in _INS:
        a = np.ascontiguousarray(inputs[name])
        arrays[f"in_{name}"] = a
        args.append(nc.dram_tensor(f"in_{name}", a.shape, mybir.dt.from_np(a.dtype), kind="ExternalInput").ap())
    args.append(nc.dram_tensor("out", (B, S, D), F32, kind="ExternalOutput").ap())
    decoder_layer(nc, *args)
    r = run_bass_kernel_spmd(nc, [arrays], core_ids=[0])
    return r.results[0]["out"]
```

```python
from contextlib import ExitStack

import concourse.bass as bass
from concourse import mybir
from concourse.alu_op_type import AluOpType as ALU

F32 = mybir.dt.float32
F32R = mybir.dt.float32r
I32 = mybir.dt.int32
U32 = mybir.dt.uint32
ACT = mybir.ActivationFunctionType
AX = mybir.AxisListType
ds = bass.ds

P = 128
B, S, D = 2, 1024, 256
KD = D // P
NT = B * S // P
TPB = S // P
HEADS, DK, SK = 16, 16, 64
HPC = P // DK
PAIRS = HEADS // 2
VW = DK + 1
LG = PAIRS * 2 * VW
E, K, I = 16, 4, 512
KI = I // P
CAP = B * S
SLOT = 256
NSTEP = (B * S * K) // SLOT + E - 1
EPS = 1e-5
NEG = -10000.0
HIDDEN = NEG * 4.0
VO_OK, SETUP_DVE = 18, 29
BIAS = 2


def done(t):
    return t + 1 + BIAS


def freed(t):
    return t + 1


def upto(t, ahead):
    return min(t + ahead, NT - 1) if isinstance(t, int) else t + ahead


def pipeline(eng, n, stages):
    depth = max(skew for skew, _ in stages)
    first = depth + depth % 2 + 2
    pairs = (n - first) // 2

    def static(t):
        for skew, fn in stages:
            if 0 <= t - skew < n:
                fn(t - skew, (t - skew) % 2, (t - skew) // 2)

    for t in range(first):
        static(t)
    if pairs > 0:
        with eng.Fori(first // 2, first // 2 + pairs) as i:
            for q in range(2):
                for skew, fn in stages:
                    par = (q - skew) % 2
                    half = (q - skew - par) // 2
                    fn(i * 2 + (q - skew), par, i + half)
    for t in range(first + 2 * max(pairs, 0), n + depth):
        static(t)


def decoder_layer(nc, x, ctx, mask, qkv_w, qkv_b, out_w, out_b, wq, wk, wv, wo,
                  router_w, router_b, w1, b1, w2, b2, out):
    xg_dram = nc.dram_tensor("expert_rows", [E * CAP, D], F32, kind="Internal").ap()
    yg_dram = nc.dram_tensor("expert_out", [NSTEP * SLOT, D], F32, kind="Internal").ap()
    x_rows = x.rearrange("b s d -> (b s) d")
    out_rows = out.rearrange("b s d -> (b s) d")
    w1_rows = w1.rearrange("e d h -> (e d) h")
    w2_rows = w2.rearrange("e h d -> (e h) d")

    with ExitStack() as stack:
        names = []

        def sem(name):
            return stack.enter_context(nc.semaphore(name))

        def count(name):
            s = sem(name)
            names.append(s)
            return s

        def sb(name, shape, dt=F32, where=stack):
            return where.enter_context(nc.sbuf_tensor(name, shape, dt))

        ps = stack.enter_context(nc.psum_tensor("ps", [P, 8, 512], F32))

        ident = sb("ident", [P, P])
        ones = sb("ones", [P, P])
        tri = sb("tri", [P, P])
        iota16i = sb("iota16i", [P, E], I32)
        iota16 = sb("iota16", [P, E])
        mhalf = sb("mhalf", [P, 1])
        carry = sb("carry", [P, E])
        x_all = sb("x_all", [P, NT, D])
        slot_all = sb("slot_all", [P, NT, K])
        exp_all = sb("exp_all", [P, NT, K])
        yrow_all = sb("yrow_all", [P, NT, K], U32)
        wts_all = sb("wts_all", [P, NT, K])
        bn = sb("bn", [P, 2, 6])
        mv = sb("mv", [P, 2, 2])
        ve = sb("ve", [P, 2])
        rstd = sb("rstd", [P, 2])
        yres = sb("yres", [P, 2, D])
        xs = sb("xs", [P, 2, D])
        tab = sb("tab", [1, NSTEP, 4], I32)
        thr_i = sb("thr_i", [P, CAP // SLOT], I32)
        thr = sb("thr", [P, CAP // SLOT])
        trie = sb("trie", [P, E, E])
        sid_i = sb("sid_i", [1, NSTEP], I32)
        sid = sb("sid", [1, NSTEP])

        early = ExitStack()

        def sbe(name, shape, dt=F32):
            return sb(name, shape, dt, early)

        a_h, a_l = sbe("a_h", [P, KD, D], F32R), sbe("a_l", [P, KD, D], F32R)
        wvo_h, wvo_l = sbe("wvo_h", [P, KD, D], F32R), sbe("wvo_l", [P, KD, D], F32R)
        zeros = sbe("zeros", [P, 1, D])
        blk = sbe("blk", [P, HPC])
        mask_i = sbe("mask_i", [P, B, SK], I32)
        keep = sbe("keep", [P, B, SK])
        hide = sbe("hide", [1, B, SK])
        hide_r = sbe("hide_r", [1, B, HPC, SK], F32R)
        one_r = sbe("one_r", [1, P], F32R)
        rb = sbe("rb", [P, E])
        rw = sbe("rw", [P, KD, E])
        bq = sbe("bq", [P, KD])
        bv = sbe("bv", [P, KD])
        bo = sbe("bo", [P, D])
        u = sbe("u", [P, KD])
        vo = sbe("vo", [P, D])
        wqT = sbe("wqT", [P, KD, D])
        woT = sbe("woT", [P, KD, D])
        kb = sbe("kb", [P, B * KD, HPC, SK])
        vb = sbe("vb", [P, B, PAIRS, 2 * VW])
        xT_h, xT_l = sbe("xT_h", [P, KD, B * S], F32R), sbe("xT_l", [P, KD, B * S], F32R)
        v_h, v_l = sbe("v_h", [P, NT, D], F32R), sbe("v_l", [P, NT, D], F32R)
        sT_h, sT_l = sbe("sT_h", [P, 2, KD, P], F32R), sbe("sT_l", [P, 2, KD, P], F32R)
        q_h, q_l = sbe("q_h", [P, 2, KD, P], F32R), sbe("q_l", [P, 2, KD, P], F32R)
        prob = sbe("prob", [P, 2, S])
        pT_h, pT_l = sbe("pT_h", [P, TPB, P], F32R), sbe("pT_l", [P, TPB, P], F32R)
        cq = sbe("cq", [P, 2, KD, P])
        cpT = sbe("cpT", [P, PAIRS, P])
        nmax = sbe("nmax", [P, 2])
        nmaxs = sbe("nmaxs", [P, 2])
        rsum = sbe("rsum", [P, 2])
        rinv = sbe("rinv", [P, 2])
        hmax = sbe("hmax", [P, 2, HEADS])
        hinv = sbe("hinv", [P, 2, HEADS])
        octx = sbe("octx", [P, 2, D])
        oT = sbe("oT", [P, KD, P])
        x2T = sbe("x2T", [P, 2, KD, P])
        lg = sbe("lg", [P, 2, E])
        lmax = sbe("lmax", [P, 2])
        lexp = sbe("lexp", [P, 2, E])
        lsum = sbe("lsum", [P, 2])
        linv = sbe("linv", [P, 2])
        rp = sbe("rp", [P, 2, E])
        mx8 = sbe("mx8", [P, 2, 8])
        ix8 = sbe("ix8", [P, 2, 8], U32)
        ixf = sbe("ixf", [P, 2, K])
        wsum = sbe("wsum", [P, 2])
        winv = sbe("winv", [P, 2])
        oh = sbe("oh", [P, 2, K, E])
        mk = sbe("mk", [P, 2, E])
        pos = sbe("pos", [P, 2, E])
        ohp = sbe("ohp", [P, 2, K, E])
        slotf = sbe("slotf", [P, 2, K])
        idx = sbe("idx", [P, 2, K], U32)
        xd = sbe("xd", [P, 2, D])

        setup = ExitStack()

        def sbs(name, shape, dt=F32):
            return sb(name, shape, dt, setup)

        n_qkv = sbs("n_qkv", [P, 3 * KD, D])
        n_out = sbs("n_out", [P, KD, D])
        n_x = sbs("n_x", [P, 4, KD, D])
        n_ctx = sbs("n_ctx", [P, D])
        aoT = sbs("aoT", [P, KD, D])
        wkT = sbs("wkT", [P, KD, D])
        wvT = sbs("wvT", [P, KD, D])
        cT = sbs("cT", [P, KD, P])
        cT2 = sbs("cT2", [P, KD, B, 2, SK])
        bvr = sbs("bvr", [P, KD, P])
        kt = sbs("kt", [P, KD, P])
        setup.close()
        x1T = sbe("x1T", [P, KD, B * S])
        early.close()

        late = ExitStack()

        def sbl(name, shape, dt=F32):
            return sb(name, shape, dt, late)

        ends = sbl("ends", [P, E])
        ntile = sbl("ntile", [P, E])
        cnt = sbl("cnt", [P, E])
        cmp8 = sbl("cmp8", [P, E, CAP // SLOT])
        cmpe = sbl("cmpe", [P, E, E])
        past = sbl("past", [1, NSTEP, E])
        past2 = sbl("past2", [1, NSTEP, E])
        es = sbl("es", [1, NSTEP])
        st = sbl("st", [1, NSTEP])
        live = sbl("live", [1, NSTEP])
        row = sbl("row", [1, NSTEP])
        delta = sbl("delta", [P, E])
        first_row = sbl("first_row", [P, E])
        owner = sbl("owner", [P, NT * K, E])
        shift = sbl("shift", [P, NT * K, E])
        moved = sbl("moved", [P, NT * K])
        tabf = sbl("tabf", [1, NSTEP, 4])
        xg = sbl("xg", [P, 2, 2, D])
        w1f = sbl("w1f", [P, 2, KD, I])
        w2f = sbl("w2f", [P, 2, KI, D])
        b1f = sbl("b1f", [P, 2, KI])
        b2f = sbl("b2f", [P, 2, D])
        w1_h, w1_l = sbl("w1_h", [P, 2, KD, I], F32R), sbl("w1_l", [P, 2, KD, I], F32R)
        w2_h, w2_l = sbl("w2_h", [P, 2, KI, D], F32R), sbl("w2_l", [P, 2, KI, D], F32R)
        gT_h, gT_l = sbl("gT_h", [P, 2, KD, SLOT], F32R), sbl("gT_l", [P, 2, KD, SLOT], F32R)
        hf = sbl("hf", [P, 2, KI, SLOT])
        h_h, h_l = sbl("h_h", [P, 2, KI, SLOT], F32R), sbl("h_l", [P, 2, KI, SLOT], F32R)
        yb = sbl("yb", [P, 2, 2, D])
        gat = sbl("gat", [P, 2, K, D])
        gidx = sbl("gidx", [P, 2, K], U32)
        acc = sbl("acc", [P, 2, K, D])
        ot = sbl("ot", [P, 2, D])
        late.close()

        ld_w = sem("ld_w"); ld_wx = sem("ld_wx"); ld_c = sem("ld_c"); ld_zero = sem("ld_zero")
        ld_x = [sem("ld_x0"), sem("ld_x1")]
        c_pool = sem("c_pool"); c_dve = sem("c_dve"); c_pe = sem("c_pe"); c_act = sem("c_act")
        passed = sem("passed")
        c_mm = sem("c_mm"); z_ok = sem("z_ok")
        xT_ps = count("xT_ps"); sTh = count("sTh"); sTl = count("sTl"); v_ps = count("v_ps")
        vh = count("vh"); vl = count("vl"); xres = count("xres"); xTh = count("xTh"); xTl = count("xTl")
        q_ps = count("q_ps"); qh = count("qh"); ql = count("ql"); s_ps = count("s_ps")
        mx = count("mx"); mxs = count("mxs"); ex = count("ex"); tp = count("tp"); pth = count("pth"); ptl = count("ptl")
        o_ps = count("o_ps"); ri = count("ri"); res = count("res"); bns = count("bns"); bna = count("bna")
        var = count("var"); rst = count("rst"); x1 = count("x1"); x1k = count("x1k")
        t1 = count("t1"); x1c = count("x1c")
        cq_ps = count("cq_ps"); cqc = count("cqc"); cs_ps = count("cs_ps"); first_ok = sem("first_ok"); causal_ok = sem("causal_ok")
        cmx = count("cmx"); csub = count("csub"); cex = count("cex"); ctp = count("ctp"); cpc = count("cpc"); co_ps = count("co_ps")
        cinv = count("cinv"); co = count("co"); cot = count("cot"); coc = count("coc")
        cy = count("cy"); cres = count("cres"); cbns = count("cbns"); cbna = count("cbna")
        cvar = count("cvar"); crst = count("crst"); x2 = count("x2")
        t2 = count("t2"); x2t = count("x2t"); lg_ps = count("lg_ps"); lgb = count("lgb"); lmx = count("lmx")
        lex = count("lex"); lin = count("lin"); lpr = count("lpr"); l8 = count("l8"); li8 = count("li8")
        lif = count("lif"); lxa = count("lxa"); loh = count("loh"); lmk = count("lmk"); lws = count("lws"); lwi = count("lwi")
        lw = count("lw"); pos_ps = count("pos_ps"); lpos = count("lpos"); lcar = count("lcar"); lohp = count("lohp"); lsl = count("lsl")
        lidx = count("lidx"); xdc = count("xdc"); lall = count("lall")
        sc_dma = [[sem(f"sc_dma{p}{r}") for r in range(K)] for p in range(2)]
        tb = sem("tb"); tb_pool = sem("tb_pool")
        f_x = [sem("f_x0"), sem("f_x1")]; f_w1 = [sem("f_w10"), sem("f_w11")]
        f_w2 = [sem("f_w20"), sem("f_w21")]; f_b1 = [sem("f_b10"), sem("f_b11")]; f_b2 = [sem("f_b20"), sem("f_b21")]
        w1h = count("w1h"); w1l = count("w1l"); w2h = count("w2h"); w2l = count("w2l")
        gt = count("gt"); gth = count("gth"); gtl = count("gtl"); hps = count("hps"); gel = count("gel")
        hh = count("hh"); hl = count("hl"); yps = count("yps"); yok = count("yok")
        st_y = [sem("st_y0"), sem("st_y1")]
        gix = count("gix")
        g_dma = [[sem(f"g_dma{p}{r}") for r in range(K)] for p in range(2)]
        ac = [count(f"ac{r}") for r in range(K)]
        ebns = count("ebns"); ebna = count("ebna"); evar = count("evar"); erst = count("erst"); eo = count("eo")
        st_o = [sem("st_o0"), sem("st_o1")]

        def mm3(pe, o, ah, al, bh, bl, first, last):
            pe.matmul(o, ah, bh, start=first, stop=False)
            pe.matmul(o, ah, bl, start=False, stop=False)
            return pe.matmul(o, al, bh, start=False, stop=last)

        f = lambda ap: ap.bitcast(F32)

        block = stack.enter_context(nc.Block())

        @block.sync
        def _(sp):
            for s in names:
                sp.sem_inc(s, BIAS)
            sp.dma_start(n_qkv[:], qkv_w.rearrange("(k p) c -> p k c", p=P)).then_inc(ld_w, 16)
            sp.dma_start(n_out[:], out_w.rearrange("(k p) c -> p k c", p=P)).then_inc(ld_w, 16)
            for n, w in enumerate((wq, wk, wv, wo)):
                sp.dma_start(n_x[:, n], w.rearrange("(k p) c -> p k c", p=P)).then_inc(ld_wx, 16)
            sp.dma_start(n_ctx[:], ctx.rearrange("b s d -> (b s) d")).then_inc(ld_wx, 16)

            def load_x(t, p, k):
                sp.wait_ge(xT_ps, freed(t))
                sp.wait_ge(xres, freed(t))
                sp.dma_start(xs[:, p], x_rows[ds(t * P, P), :]).then_inc(ld_x[p], 16)

            pipeline(sp, NT, [(0, load_x)])
            sp.wait_ge(z_ok, 1)
            with sp.Fori(0, E * CAP // (8 * P)) as i:
                sp.dma_start(xg_dram[ds(i * (8 * P), 8 * P), :].rearrange("(p c) d -> p c d", c=8),
                             zeros[:].broadcast_to([P, 8, D])).then_inc(ld_zero, 16)

            sp.wait_ge(tb, 1)
            for p in range(2):
                for r in range(K):
                    sp.wait_ge(sc_dma[p][r], 16 * (NT // 2))

            def load_step(t, p, k):
                rx = sp.value_load(tab[0:1, ds(t, 1), 0:1], min_val=0, max_val=E * CAP - SLOT)
                re = sp.value_load(tab[0:1, ds(t, 1), 1:2], min_val=0, max_val=E - 1)
                sp.wait_ge(gt, freed(t))
                sp.dma_start(xg[:, p], xg_dram[ds(rx, SLOT), :].rearrange("(c p) d -> p c d", p=P)).then_inc(f_x[p], 16)
                sp.wait_ge(w1h, freed(t))
                sp.wait_ge(w1l, freed(t))
                sp.dma_start(w1f[:, p], w1_rows[ds(re * D, D), :].rearrange("(k p) h -> p k h", p=P)).then_inc(f_w1[p], 16)
                sp.wait_ge(w2h, freed(t))
                sp.wait_ge(w2l, freed(t))
                sp.dma_start(w2f[:, p], w2_rows[ds(re * I, I), :].rearrange("(p j) d -> p j d", j=KI)).then_inc(f_w2[p], 16)
                sp.wait_ge(gel, freed(t))
                sp.sem_inc(passed, 1)
                sp.dma_start(b1f[:, p], b1[ds(re, 1), :].rearrange("o (p j) -> (o p) j", j=KI)).then_inc(f_b1[p], 16)

            def load_b2(t, p, k):
                r = sp.value_load(tab[0:1, ds(t, 1), 1:2], min_val=0, max_val=E - 1)
                sp.wait_ge(yok, freed(t))
                sp.dma_start(b2f[:, p], b2[ds(r, 1), :].broadcast_to([P, D])).then_inc(f_b2[p], 16)

            pipeline(sp, NSTEP, [(0, load_step), (2, load_b2)])

            def store_out(t, p, k):
                sp.wait_ge(eo, done(t))
                sp.dma_start(out_rows[ds(t * P, P), :], ot[:, p]).then_inc(st_o[p], 16)

            pipeline(sp, NT, [(0, store_out)])
            for p in range(2):
                sp.wait_ge(st_o[p], 16 * (NT // 2))

        @block.gpsimd
        def _(pool):
            pool.memset(ident[:], 0.0).then_inc(c_pool, 1)
            pool.memset(ones[:], 1.0).then_inc(c_pool, 1)
            pool.memset(tri[:], 1.0).then_inc(c_pool, 1)
            pool.memset(blk[:], 1.0).then_inc(c_pool, 1)
            pool.memset(mhalf[:], -0.5).then_inc(c_pool, 1)
            pool.memset(trie[:], 1.0).then_inc(c_pool, 1)
            pool.iota(iota16i[:], [[1, E]], base=0, channel_multiplier=0).then_inc(c_pool, 1)
            pool.iota(thr_i[:], [[SLOT, CAP // SLOT]], base=0, channel_multiplier=0).then_inc(c_pool, 1)
            pool.iota(sid_i[:], [[1, NSTEP]], base=0, channel_multiplier=0).then_inc(c_pool, 1)
            pool.wait_ge(c_pool, 9)
            pool.affine_select(ident[:], ident[:], [[-1, P]], ALU.not_equal, 1.0, base=0, channel_multiplier=1).then_inc(c_pool, 1)
            pool.affine_select(tri[:], tri[:], [[1, P]], ALU.is_gt, 0.0, base=0, channel_multiplier=-1).then_inc(c_pool, 1)
            pool.affine_select(blk[:], blk[:], [[-DK, HPC]], ALU.is_ge, 0.0, base=0, channel_multiplier=1).then_inc(c_pool, 1)
            pool.affine_select(trie[:], trie[:], [[1, E], [-1, E]], ALU.is_ge, 0.0, base=0, channel_multiplier=0).then_inc(c_pool, 1)
            pool.wait_ge(c_pool, 13)
            pool.affine_select(blk[:], blk[:], [[DK, HPC]], ALU.is_ge, 0.0, base=DK - 1, channel_multiplier=-1).then_inc(c_pool, 1)
            pool.tensor_copy(iota16[:], iota16i[:]).then_inc(c_pool, 1)
            pool.tensor_copy(thr[:], thr_i[:]).then_inc(c_pool, 1)
            pool.tensor_copy(sid[:], sid_i[:]).then_inc(c_pool, 1)
            pool.wait_ge(c_pool, 17)
            pool.tensor_scalar(carry[:], iota16[:], float(CAP), 0.0, ALU.mult, ALU.add).then_inc(c_pool, 1)
            pool.memset(zeros[:], 0.0).then_inc(z_ok, 1)
            def residual(t, p, k):
                if isinstance(t, int) and t == 0:
                    pool.wait_ge(c_dve, VO_OK)
                pool.wait_ge(ld_x[p], 16 * k + 16)
                pool.tensor_tensor(x_all[:, ds(t, 1), :], xs[:, ds(p, 1), :], vo[:].unsqueeze(1), ALU.add).then_inc(xres, 1)

            pipeline(pool, NT, [(0, residual)])

            def root(t, p, k):
                pool.wait_ge(var, done(t))
                pool.tensor_tensor(rstd[:, p:p + 1], ve[:, p:p + 1], mhalf[:], ALU.pow).then_inc(rst, 1)

            def keep_x1(t, p, k):
                pool.wait_ge(x1, done(t))
                pool.tensor_copy(x_all[:, ds(p * TPB + k, 1), :], xs[:, ds(p, 1), :]).then_inc(x1k, 1)

            pipeline(pool, NT, [(0, root), (0, keep_x1)])

            def causal(t, p, k):
                if isinstance(t, int) and t < B:
                    pool.wait_ge(first_ok, t + 1)
                    pool.affine_select(prob[:, p].rearrange("p (h k) -> p h k", k=SK), prob[:, p].rearrange("p (h k) -> p h k", k=SK),
                                       [[0, HEADS], [-1, SK]], ALU.is_ge, HIDDEN, base=0, channel_multiplier=1).then_inc(causal_ok, 1)

            def root2(t, p, k):
                pool.wait_ge(cvar, done(t))
                pool.tensor_tensor(rstd[:, p:p + 1], ve[:, p:p + 1], mhalf[:], ALU.pow).then_inc(crst, 1)

            def dispatch(t, p, k):
                pool.wait_ge(lidx, done(t))
                pool.wait_ge(xdc, done(t))
                pool.sem_inc(passed, 1)
                for r in range(K):
                    pool.indirect_dma_start(
                        out=xg_dram, out_offset=bass.IndirectOffsetOnAxis(ap=idx[:, p, r:r + 1], axis=0),
                        in_=xd[:, p], in_offset=None).then_inc(sc_dma[p][r], 16)

            pool.wait_ge(ld_zero, 16 * (E * CAP // (8 * P)))
            pipeline(pool, NT, [(1, causal), (3, root2), (5, dispatch)])

            def split_w2(t, p, k):
                pool.wait_ge(w2h, done(t))
                pool.wait_ge(yps, freed(t))
                pool.tensor_tensor(w2_l[:, p], w2f[:, p], f(w2_h[:, p]), ALU.subtract).then_inc(w2l, 1)

            pipeline(pool, NSTEP, [(0, split_w2)])

            for p in range(2):
                pool.wait_ge(st_y[p], 16 * ((NSTEP + 1 - p) // 2))

            def gather(t, p, k):
                pool.wait_ge(gix, done(t))
                pool.wait_ge(ac[K - 1], freed(t))
                pool.sem_inc(passed, 1)
                for r in range(K):
                    pool.indirect_dma_start(
                        out=gat[:, p, r], out_offset=None, in_=yg_dram,
                        in_offset=bass.IndirectOffsetOnAxis(ap=gidx[:, p, r:r + 1], axis=0)).then_inc(g_dma[p][r], 16)

            def root3(t, p, k):
                pool.wait_ge(evar, done(t))
                pool.tensor_tensor(rstd[:, p:p + 1], ve[:, p:p + 1], mhalf[:], ALU.pow).then_inc(erst, 1)

            pipeline(pool, NT, [(0, gather), (1, root3)])

        @block.tensor
        def _(pe):
            def turn(bank, w):
                for kc in range(KD):
                    for ko in range(KD):
                        mm = pe.transpose(ps[:, bank, kc * D + ko * P:kc * D + (ko + 1) * P],
                                          w[:, ko, kc * P:(kc + 1) * P], ident[:])
                mm.then_inc(c_pe, 1)

            pe.wait_ge(c_pool, 18)
            pe.wait_ge(ld_w, 32)
            turn(0, n_out)
            pe.wait_ge(ld_wx, 80)
            for n in range(4):
                turn(1 + n, n_x[:, n])
            for kc in range(KD):
                mm = pe.transpose(ps[:, 5, kc * P:(kc + 1) * P], n_ctx[:, kc * P:(kc + 1) * P], ident[:])
            mm.then_inc(c_pe, 1)
            for kc in range(KD):
                for ko in range(KD):
                    mm = pe.matmul(ps[:, 6, kc * D:(kc + 1) * D], n_qkv[:, ko, kc * P:(kc + 1) * P],
                                   n_qkv[:, KD + ko], start=ko == 0, stop=ko == KD - 1)
            mm.then_inc(c_mm, 1)
            pe.wait_ge(c_dve, 1)
            for kc in range(KD):
                for ko in range(KD):
                    mm = pe.matmul(ps[:, 7, kc * D:(kc + 1) * D], n_qkv[:, 2 * KD + ko, kc * P:(kc + 1) * P],
                                   aoT[:, ko], start=ko == 0, stop=ko == KD - 1)
            mm.then_inc(c_mm, 1)
            pe.wait_ge(c_dve, 8)
            pe.wait_ge(ld_c, 16 * 9)
            for ko in range(KD):
                pe.matmul(ps[:, 0, 0:D], bvr[:, ko], aoT[:, ko], start=ko == 0, stop=ko == KD - 1)
            for kc in range(KD):
                for ko in range(KD):
                    mm = pe.matmul(ps[:, 0, D + kc:D + kc + 1], n_qkv[:, KD + ko, kc * P:(kc + 1) * P],
                                   bq[:, ko:ko + 1], start=ko == 0, stop=ko == KD - 1)
            mm.then_inc(c_mm, 1)
            pe.wait_ge(c_dve, 9)
            for ko in range(KD):
                for ki in range(KD):
                    mm = pe.matmul(ps[:, 1, ko * P:(ko + 1) * P], wkT[:, ki, ko * P:(ko + 1) * P], cT[:, ki],
                                   start=ki == 0, stop=ki == KD - 1)
            mm.then_inc(c_mm, 1)
            for b in range(B):
                for ki in range(KD):
                    mm = pe.matmul(ps[:, 2, b * D:(b + 1) * D], cT2[:, ki, b].rearrange("p a k -> p (a k)"),
                                   wvT[:, ki], start=ki == 0, stop=ki == KD - 1)
            mm.then_inc(c_mm, 1)
            pe.wait_ge(c_dve, SETUP_DVE)
            pe.wait_ge(c_act, 4)

            def turn_x(t, p, k):
                pe.wait_ge(ld_x[p], 16 * k + 16)
                pe.wait_ge(sTl, freed(t))
                for kc in range(KD):
                    mm = pe.transpose(ps[:, p, kc * P:(kc + 1) * P], xs[:, p, kc * P:(kc + 1) * P], ident[:])
                mm.then_inc(xT_ps, 1)

            def values(t, p, k):
                pe.wait_ge(sTl, done(t))
                pe.wait_ge(sTh, done(t))
                pe.wait_ge(vl, freed(t))
                for kc in range(KD):
                    mm = mm3(pe, ps[:, 2 + p, 0:D], sT_h[:, p, kc], sT_l[:, p, kc], wvo_h[:, kc], wvo_l[:, kc],
                             kc == 0, kc == KD - 1)
                mm.then_inc(v_ps, 1)

            pipeline(pe, NT, [(0, turn_x), (1, values)])
            pe.wait_ge(vl, done(NT - 1))
            pe.wait_ge(vh, done(NT - 1))
            pe.wait_ge(xTl, done(NT - 1))

            def query(t, p, k):
                pe.wait_ge(ql, freed(t) + 1)
                for jc in range(KD):
                    for ic in range(KD):
                        mm = mm3(pe, ps[:, 6, jc * P:(jc + 1) * P],
                                 a_h[:, ic, jc * P:(jc + 1) * P], a_l[:, ic, jc * P:(jc + 1) * P],
                                 xT_h[:, ic, ds(p * S + k * P, P)], xT_l[:, ic, ds(p * S + k * P, P)], ic == 0, ic == KD - 1)
                mm.then_inc(q_ps, 1)

            def scores(t, p, k):
                pe.wait_ge(ql, done(t))
                pe.wait_ge(qh, done(t))
                pe.wait_ge(ex, freed(t))
                for jc in range(KD):
                    for kh in range(2):
                        mm = mm3(pe, ps[:, 2 * p + kh, :], q_h[:, p, jc], q_l[:, p, jc],
                                 xT_h[:, jc, p * S + kh * 512:p * S + (kh + 1) * 512],
                                 xT_l[:, jc, p * S + kh * 512:p * S + (kh + 1) * 512],
                                 jc == 0, jc == KD - 1)
                mm.then_inc(s_ps, 1)

            def turn_p(t, p, k):
                pe.wait_ge(ex, done(t))
                pe.wait_ge(ptl, freed(t) + 1)
                for kt in range(TPB):
                    mm = pe.transpose(ps[:, 4 + kt // 4, (kt % 4) * P:(kt % 4 + 1) * P],
                                      prob[:, p, kt * P:(kt + 1) * P], ident[:])
                mm.then_inc(tp, 1)

            def attend(t, p, k):
                pe.wait_ge(ptl, done(t))
                pe.wait_ge(pth, done(t))
                pe.wait_ge(x1c, freed(t) + 1)
                for kt in range(TPB):
                    mm = mm3(pe, ps[:, 7, 0:D], pT_h[:, kt], pT_l[:, kt], v_h[:, p * TPB + kt], v_l[:, p * TPB + kt],
                             kt == 0, kt == TPB - 1)
                mm.then_inc(o_ps, 1)

            def turn_x1(t, p, k):
                pe.wait_ge(x1, done(t))
                for kc in range(KD):
                    mm = pe.transpose(ps[:, 7, D + kc * P:D + (kc + 1) * P], xs[:, p, kc * P:(kc + 1) * P], ident[:])
                mm.then_inc(t1, 1)

            pipeline(pe, NT, [(2, turn_p), (1, scores), (3, turn_x1), (0, query), (2, attend)])
            pe.wait_ge(x1c, done(NT - 1))
            pe.wait_ge(c_dve, SETUP_DVE)

            def cquery(t, p, k):
                pe.wait_ge(cqc, freed(t) + 1)
                for oc in range(KD):
                    for ic in range(KD):
                        mm = pe.matmul(ps[:, 4, oc * P:(oc + 1) * P], wqT[:, ic, oc * P:(oc + 1) * P],
                                       x1T[:, ic, ds(p * S + k * P, P)], start=ic == 0, stop=ic == KD - 1)
                mm.then_inc(cq_ps, 1)

            def cscores(t, p, k):
                pe.wait_ge(cqc, done(t))
                pe.wait_ge(csub, freed(t) + 1)
                for hc in range(KD):
                    pe.matmul(ps[:, hc], cq[:, p, hc], kb[:, p * KD + hc].rearrange("p h k -> p (h k)"), start=True, stop=False)
                    mm = pe.matmul(ps[:, hc], one_r[:], hide_r[:, p].rearrange("p h k -> p (h k)"), start=False, stop=True)
                mm.then_inc(cs_ps, 1)

            def cturn_p(t, p, k):
                pe.wait_ge(cex, done(t))
                pe.wait_ge(cpc, freed(t) + 1)
                for g in range(PAIRS):
                    mm = pe.transpose(ps[:, 2 + g // 4, (g % 4) * P:(g % 4 + 1) * P],
                                      prob[:, p, g * P:(g + 1) * P], ident[:])
                mm.then_inc(ctp, 1)

            def cattend(t, p, k):
                pe.wait_ge(cpc, done(t))
                pe.wait_ge(co, freed(t) + 1)
                if not (isinstance(t, int) and t < 3):
                    pe.wait_ge(lgb, done(t - 3))
                for g in range(PAIRS):
                    mm = pe.matmul(ps[:, 5, g * 2 * VW:(g + 1) * 2 * VW], cpT[:, g], vb[:, p, g], start=True, stop=True)
                mm.then_inc(co_ps, 1)

            def turn_o(t, p, k):
                pe.wait_ge(co, done(t))
                pe.wait_ge(coc, freed(t) + 1)
                pe.wait_ge(x2t, freed(t))
                for kc in range(KD):
                    mm = pe.transpose(ps[:, 6, kc * P:(kc + 1) * P], octx[:, p, kc * P:(kc + 1) * P], ident[:])
                mm.then_inc(cot, 1)

            def project(t, p, k):
                pe.wait_ge(coc, done(t))
                pe.wait_ge(cres, freed(t) + 1)
                if not (isinstance(t, int) and t < 3):
                    pe.wait_ge(lcar, done(t - 3))
                for kc in range(KD):
                    mm = pe.matmul(ps[:, 7, 0:D], oT[:, kc], woT[:, kc], start=kc == 0, stop=kc == KD - 1)
                mm.then_inc(cy, 1)

            def turn_x2(t, p, k):
                pe.wait_ge(x2, done(t))
                pe.wait_ge(x2t, freed(t) + 1)
                pe.wait_ge(coc, done(upto(t, 1)))
                for kc in range(KD):
                    mm = pe.transpose(ps[:, 6, D + kc * P:D + (kc + 1) * P], xs[:, p, kc * P:(kc + 1) * P], ident[:])
                mm.then_inc(t2, 1)

            def logits(t, p, k):
                pe.wait_ge(x2t, done(t))
                pe.wait_ge(lgb, freed(t) + 1)
                pe.wait_ge(co, done(upto(t, 1)))
                for kc in range(KD):
                    mm = pe.matmul(ps[:, 5, LG:LG + E], x2T[:, p, kc], rw[:, kc], start=kc == 0, stop=kc == KD - 1)
                mm.then_inc(lg_ps, 1)

            def positions(t, p, k):
                pe.wait_ge(lmk, done(t))
                pe.wait_ge(lcar, freed(t) + 1)
                pe.wait_ge(cres, done(upto(t, 1)))
                pe.matmul(ps[:, 7, D:D + E], tri[:], mk[:, p], start=True, stop=True)
                pe.matmul(ps[:, 7, D + E:D + 2 * E], ones[:], mk[:, p], start=True, stop=True).then_inc(pos_ps, 1)

            pipeline(pe, NT, [(2, cturn_p), (3, turn_o), (1, cscores), (4, turn_x2), (5, positions), (3, project),
                              (4, logits), (2, cattend), (0, cquery)])
            pe.wait_ge(lcar, done(NT - 1))

            def turn_g(t, p, k):
                pe.wait_ge(f_x[p], 16 * k + 16)
                pe.wait_ge(gtl, freed(t))
                for c in range(2):
                    for kc in range(KD):
                        mm = pe.transpose(ps[:, p, kc * SLOT + c * P:kc * SLOT + (c + 1) * P],
                                          xg[:, p, c, kc * P:(kc + 1) * P], ident[:])
                mm.then_inc(gt, 1)

            def up(t, p, k):
                pe.wait_ge(gtl, done(t))
                pe.wait_ge(gth, done(t))
                pe.wait_ge(w1l, done(t))
                pe.wait_ge(gel, freed(t))
                for j in range(KI):
                    for kc in range(KD):
                        mm = mm3(pe, ps[:, 2 + 2 * p + j // 2, (j % 2) * SLOT:(j % 2 + 1) * SLOT],
                                 w1_h[:, p, kc, j::KI], w1_l[:, p, kc, j::KI], gT_h[:, p, kc], gT_l[:, p, kc],
                                 kc == 0, kc == KD - 1)
                mm.then_inc(hps, 1)

            def down(t, p, k):
                pe.wait_ge(hl, done(t))
                pe.wait_ge(hh, done(t))
                pe.wait_ge(w2l, done(t))
                pe.wait_ge(yok, freed(t))
                for c in range(2):
                    for j in range(KI):
                        mm = mm3(pe, ps[:, 6 + p, c * D:(c + 1) * D], h_h[:, p, j, c * P:(c + 1) * P],
                                 h_l[:, p, j, c * P:(c + 1) * P], w2_h[:, p, j], w2_l[:, p, j], j == 0, j == KI - 1)
                mm.then_inc(yps, 1)

            pipeline(pe, NSTEP, [(1, up), (0, turn_g), (2, down)])

        @block.scalar
        def _(act):
            for kc in range(KD):
                for dst, base in ((bq, 0), (bv, 2 * D)):
                    act.dma_start(dst[:, kc:kc + 1], qkv_b[base + kc * P:base + (kc + 1) * P].rearrange("(p o) -> p o", o=1)).then_inc(ld_c, 16)
            act.dma_start(bo[:], out_b.rearrange("(o d) -> o d", o=1).broadcast_to([P, D])).then_inc(ld_c, 16)
            act.dma_start(mask_i[:].rearrange("p b k -> p (b k)"),
                          mask.rearrange("b k -> (b k)").rearrange("(o n) -> o n", o=1).broadcast_to([P, B * SK])).then_inc(ld_c, 16)
            act.dma_start(rb[:], router_b.rearrange("(o e) -> o e", o=1).broadcast_to([P, E])).then_inc(ld_c, 16)
            for kc in range(KD):
                act.dma_start(rw[:, kc], router_w[kc * P:(kc + 1) * P, :]).then_inc(ld_c, 16)

            act.wait_ge(c_pe, 2)
            act.activation(wqT[:].rearrange("p k c -> p (k c)"), ps[:, 1], ACT.Copy).then_inc(c_act, 1)
            act.wait_ge(c_pe, 5)
            act.activation(woT[:].rearrange("p k c -> p (k c)"), ps[:, 4], ACT.Copy).then_inc(c_act, 1)
            act.wait_ge(c_mm, 1)
            act.activation(a_h[:].rearrange("p k c -> p (k c)"), ps[:, 6], ACT.Copy).then_inc(c_act, 1)
            act.wait_ge(c_mm, 2)
            act.activation(wvo_h[:].rearrange("p k c -> p (k c)"), ps[:, 7], ACT.Copy).then_inc(c_act, 1)

            def x_high(t, p, k):
                act.wait_ge(xT_ps, done(t))
                act.wait_ge(v_ps, freed(t))
                act.activation(sT_h[:, p].rearrange("p k c -> p (k c)"), ps[:, p, 0:D], ACT.Copy).then_inc(sTh, 1)
                act.activation(xT_h[:, :, ds(t * P, P)], ps[:, p, 0:D].rearrange("p (k c) -> p k c", c=P), ACT.Copy).then_inc(xTh, 1)

            def v_high(t, p, k):
                act.wait_ge(v_ps, done(t))
                act.activation(v_h[:, ds(t, 1), :].rearrange("p a d -> p (a d)"), ps[:, 2 + p, 0:D], ACT.Copy).then_inc(vh, 1)

            pipeline(act, NT, [(0, x_high), (1, v_high)])

            def q_high(t, p, k):
                act.wait_ge(q_ps, done(t))
                act.wait_ge(s_ps, freed(t))
                for jc in range(KD):
                    ins = act.activation(q_h[:, p, jc], ps[:, 6, jc * P:(jc + 1) * P], ACT.Identity,
                                         bias=u[:, jc:jc + 1])
                ins.then_inc(qh, 1)

            def p_high(t, p, k):
                act.wait_ge(tp, done(t))
                act.wait_ge(o_ps, freed(t) + 1)
                act.activation(pT_h[:].rearrange("p k c -> p (k c)"), ps[:, 4:6].rearrange("p b c -> p (b c)"),
                               ACT.Copy).then_inc(pth, 1)

            def exps(t, p, k):
                act.wait_ge(mxs, done(t))
                act.wait_ge(s_ps, done(t))
                act.wait_ge(tp, freed(t))
                act.wait_ge(ri, freed(t))
                act.activation(prob[:, p], ps[:, 2 * p:2 * p + 2].rearrange("p b c -> p (b c)"), ACT.Exp,
                               bias=nmaxs[:, p:p + 1], scale=1.0 / 16.0, accum_out=rsum[:, p:p + 1]).then_inc(ex, 1)

            def x1_turned(t, p, k):
                act.wait_ge(t1, done(t))
                act.activation(x1T[:, :, ds(p * S + k * P, P)], ps[:, 7, D:2 * D].rearrange("p (k c) -> p k c", c=P),
                               ACT.Copy).then_inc(x1c, 1)

            pipeline(act, NT, [(2, p_high), (3, x1_turned), (0, q_high), (1, exps)])

            def q_out(t, p, k):
                act.wait_ge(cq_ps, done(t))
                act.wait_ge(cs_ps, freed(t))
                act.activation(cq[:, p].rearrange("p k c -> p (k c)"), ps[:, 4, 0:D], ACT.Copy).then_inc(cqc, 1)

            def p_out(t, p, k):
                act.wait_ge(ctp, done(t))
                act.wait_ge(co_ps, freed(t) + 1)
                act.activation(cpT[:].rearrange("p k c -> p (k c)"), ps[:, 2:4].rearrange("p b c -> p (b c)"),
                               ACT.Copy).then_inc(cpc, 1)

            def o_out(t, p, k):
                act.wait_ge(cot, done(t))
                act.wait_ge(cy, freed(t) + 1)
                act.activation(oT[:].rearrange("p k c -> p (k c)"), ps[:, 6, 0:D], ACT.Copy).then_inc(coc, 1)

            def cexps(t, p, k):
                act.wait_ge(csub, done(t))
                act.activation(prob[:, p], prob[:, p], ACT.Exp, scale=0.25).then_inc(cex, 1)

            def x2_turned(t, p, k):
                act.wait_ge(t2, done(t))
                act.wait_ge(lg_ps, freed(t))
                act.activation(x2T[:, p].rearrange("p k c -> p (k c)"), ps[:, 6, D:2 * D], ACT.Copy).then_inc(x2t, 1)

            def keep_x2(t, p, k):
                act.wait_ge(x2, done(t))
                act.activation(x_all[:, ds(p * TPB + k, 1), :], xs[:, ds(p, 1), :], ACT.Copy)
                if not (isinstance(t, int) and t < 2):
                    for r in range(K):
                        act.wait_ge(sc_dma[p][r], 16 * k)
                act.activation(xd[:, p], xs[:, p], ACT.Copy).then_inc(xdc, 1)

            def rexps(t, p, k):
                act.wait_ge(lmx, done(t))
                act.activation(lexp[:, p], lg[:, p], ACT.Exp, bias=lmax[:, p:p + 1], accum_out=lsum[:, p:p + 1]).then_inc(lex, 1)

            pipeline(act, NT, [(3, o_out), (2, p_out), (4, x2_turned), (4, keep_x2), (0, q_out), (1, cexps), (4, rexps)])

            def g_high(t, p, k):
                act.wait_ge(gt, done(t))
                act.wait_ge(hps, freed(t))
                act.activation(gT_h[:, p].rearrange("p k c -> p (k c)"), ps[:, p], ACT.Copy).then_inc(gth, 1)

            def gelus(t, p, k):
                act.wait_ge(hps, done(t))
                act.wait_ge(f_b1[p], 16 * k + 16)
                act.wait_ge(hl, freed(t))
                act.wait_ge(hh, freed(t))
                for j in range(KI):
                    ins = act.activation(hf[:, p, j], ps[:, 2 + 2 * p + j // 2, (j % 2) * SLOT:(j % 2 + 1) * SLOT],
                                         ACT.Gelu, bias=b1f[:, p, j:j + 1])
                ins.then_inc(gel, 1)

            def h_high(t, p, k):
                act.wait_ge(gel, done(t))
                act.wait_ge(yps, freed(t))
                act.activation(h_h[:, p], hf[:, p], ACT.Copy).then_inc(hh, 1)

            def store_step(t, p, k):
                act.wait_ge(yok, done(t))
                act.dma_start(yg_dram[ds(t * SLOT, SLOT), :].rearrange("(c p) d -> p c d", p=P), yb[:, p]).then_inc(st_y[p], 16)

            pipeline(act, NSTEP, [(4, store_step), (1, gelus), (0, g_high), (1, h_high)])

        @block.vector
        def _(dve):
            n = [0]

            def step(ins):
                n[0] += 1
                ins.then_inc(c_dve, 1)

            def low(o, src, hi):
                step(dve.tensor_tensor(o, src, f(hi), ALU.subtract))

            flat = "p k c -> p (k c)"
            dve.wait_ge(c_pe, 1)
            step(dve.tensor_copy(aoT[:].rearrange(flat), ps[:, 0]))
            dve.wait_ge(c_pe, 4)
            step(dve.tensor_copy(wkT[:].rearrange(flat), ps[:, 2]))
            step(dve.tensor_copy(wvT[:].rearrange(flat), ps[:, 3]))
            dve.wait_ge(c_pe, 6)
            step(dve.tensor_copy(cT[:].rearrange(flat), ps[:, 5, 0:D]))
            for a in range(2):
                step(dve.tensor_copy(cT2[:, :, :, a], ps[:, 5, 0:D].rearrange("p (k b s) -> p k b s", b=B, s=SK)))
            dve.wait_ge(ld_c, 16 * 9)
            for kc in range(KD):
                step(dve.tensor_copy(bvr[:, kc], bv[:, kc:kc + 1].broadcast_to([P, P])))
            dve.wait_ge(c_act, 3)
            low(a_l[:].rearrange(flat), ps[:, 6], a_h[:].rearrange(flat))
            dve.wait_ge(c_act, 4)
            low(wvo_l[:].rearrange(flat), ps[:, 7], wvo_h[:].rearrange(flat))
            step(dve.tensor_scalar(keep[:], mask_i[:], 0.0, None, ALU.not_equal))
            dve.wait_ge(c_pool, 18)
            step(dve.tensor_copy(one_r[:], ones[0:1]))
            step(dve.memset(vb[:], 0.0))
            dve.wait_ge(c_dve, n[0])
            step(dve.tensor_scalar(hide[:], keep[0:1], -1.0, -HIDDEN, ALU.add, ALU.mult))
            dve.wait_ge(c_dve, n[0])
            for b in range(B):
                step(dve.tensor_copy(hide_r[:, b], hide[:, b].unsqueeze(1).broadcast_to([1, HPC, SK])))
            dve.wait_ge(c_mm, 3)
            step(dve.tensor_copy(u[:], ps[:, 0, D:D + KD]))
            step(dve.tensor_tensor(vo[:], ps[:, 0, 0:D], bo[:], ALU.add))
            assert n[0] == VO_OK, n[0]
            dve.wait_ge(c_mm, 4)
            step(dve.tensor_tensor(kt[:].rearrange("p k (b s) -> p k b s", s=SK), ps[:, 1, 0:D].rearrange("p (k b s) -> p k b s", b=B, s=SK),
                                   keep[:].unsqueeze(1).broadcast_to([P, KD, B, SK]), ALU.mult))
            dve.wait_ge(c_dve, n[0])
            for b in range(B):
                for hc in range(KD):
                    step(dve.tensor_tensor(kb[:, b * KD + hc], kt[:, hc, b * SK:(b + 1) * SK].unsqueeze(1).broadcast_to([P, HPC, SK]),
                                           blk[:].unsqueeze(2).broadcast_to([P, HPC, SK]), ALU.mult))
            dve.wait_ge(c_mm, 5)
            for b in range(B):
                for a in range(2):
                    rows = slice(a * SK, (a + 1) * SK)
                    src = ps[rows, 2, b * D:(b + 1) * D].rearrange("p (g h d) -> p g h d", h=2, d=DK)[:, :, a]
                    step(dve.tensor_copy(vb[rows, b, :, a * VW:a * VW + DK], src))
            for a in range(2):
                rows = slice(a * SK, (a + 1) * SK)
                step(dve.memset(vb[rows, :, :, a * VW + DK:(a + 1) * VW], 1.0))
            assert n[0] == SETUP_DVE, n[0]

            def x_low(t, p, k):
                dve.wait_ge(xTh, done(t))
                dve.wait_ge(v_ps, freed(t))
                dve.tensor_tensor(sT_l[:, p].rearrange(flat), ps[:, p, 0:D], f(sT_h[:, p].rearrange(flat)), ALU.subtract).then_inc(sTl, 1)
                dve.wait_ge(sTl, done(t))
                dve.tensor_copy(xT_l[:, :, ds(t * P, P)], f(sT_l[:, p])).then_inc(xTl, 1)

            def v_low(t, p, k):
                dve.wait_ge(vh, done(t))
                dve.tensor_tensor(v_l[:, ds(t, 1), :].rearrange("p a d -> p (a d)"), ps[:, 2 + p, 0:D],
                                  f(v_h[:, ds(t, 1), :].rearrange("p a d -> p (a d)")), ALU.subtract).then_inc(vl, 1)

            pipeline(dve, NT, [(0, x_low), (1, v_low)])

            def norm(t, p, src, dst, s_in, s_bn, s_ag, s_var, s_rst, s_out):
                dve.wait_ge(s_in, done(t))
                dve.bn_stats(bn[:, p], src).then_inc(s_bn, 1)
                dve.wait_ge(s_bn, done(t))
                dve.sem_inc(passed, 1)
                dve.bn_aggr(mv[:, p], bn[:, p]).then_inc(s_ag, 1)
                dve.wait_ge(s_ag, done(t))
                dve.tensor_scalar(ve[:, p:p + 1], mv[:, p, 1:2], EPS, None, ALU.add).then_inc(s_var, 1)
                dve.wait_ge(s_rst, done(t))
                dve.tensor_scalar(dst, src, mv[:, p, 0:1], rstd[:, p:p + 1], ALU.subtract, ALU.mult).then_inc(s_out, 1)

            dve.wait_ge(xres, done(NT - 1))

            def row_max(t, p, k):
                dve.wait_ge(s_ps, done(t))
                dve.wait_ge(ex, freed(t))
                dve.tensor_reduce(nmax[:, p:p + 1], ps[:, 2 * p:2 * p + 2].rearrange("p b c -> p (b c)"), AX.X, ALU.max).then_inc(mx, 1)
                dve.wait_ge(mx, done(t))
                dve.tensor_scalar(nmaxs[:, p:p + 1], nmax[:, p:p + 1], -1.0 / 16.0, None, ALU.mult).then_inc(mxs, 1)

            def q_low(t, p, k):
                dve.wait_ge(qh, done(t))
                dve.wait_ge(s_ps, freed(t))
                for jc in range(KD):
                    ins = dve.scalar_tensor_tensor(q_l[:, p, jc], ps[:, 6, jc * P:(jc + 1) * P], u[:, jc:jc + 1],
                                                   f(q_h[:, p, jc]), ALU.add, ALU.subtract)
                ins.then_inc(ql, 1)

            def p_low(t, p, k):
                dve.wait_ge(pth, done(t))
                dve.wait_ge(o_ps, freed(t) + 1)
                dve.tensor_tensor(pT_l[:].rearrange(flat), ps[:, 4:6].rearrange("p b c -> p (b c)"), f(pT_h[:].rearrange(flat)),
                                  ALU.subtract).then_inc(ptl, 1)

            def finish(t, p, k):
                dve.wait_ge(ex, done(t))
                dve.reciprocal(rinv[:, p:p + 1], rsum[:, p:p + 1]).then_inc(ri, 1)
                dve.wait_ge(ri, done(t))
                dve.wait_ge(o_ps, done(t))
                dve.scalar_tensor_tensor(yres[:, p], ps[:, 7, 0:D], rinv[:, p:p + 1],
                                         x_all[:, ds(p * TPB + k, 1), :].rearrange("p a d -> p (a d)"), ALU.mult, ALU.add).then_inc(res, 1)
                dve.wait_ge(t1, freed(t))
                dve.wait_ge(x1k, freed(t))
                norm(t, p, yres[:, p], xs[:, p], res, bns, bna, var, rst, x1)

            pipeline(dve, NT, [(3, finish), (2, p_low), (1, row_max), (0, q_low)])

            heads = "p (h k) -> p h k"

            def scored(t, p):
                if isinstance(t, int) and t < B:
                    return prob[:, p].rearrange(heads, k=SK)
                return ps[:, 0:2].rearrange("p b (h k) -> p (b h) k", k=SK)

            def head_max(t, p, k):
                dve.wait_ge(cs_ps, done(t))
                if isinstance(t, int) and t < B:
                    dve.tensor_copy(prob[:, p], ps[:, 0:2].rearrange("p b c -> p (b c)")).then_inc(first_ok, 1)
                    dve.wait_ge(causal_ok, t + 1)
                dve.tensor_reduce(hmax[:, p], scored(t, p), AX.X, ALU.max).then_inc(cmx, 1)

            def sub_max(t, p, k):
                dve.wait_ge(cmx, done(t))
                dve.wait_ge(ctp, freed(t))
                dve.tensor_tensor(prob[:, p].rearrange(heads, k=SK), scored(t, p),
                                  hmax[:, p].unsqueeze(2).broadcast_to([P, HEADS, SK]), ALU.subtract).then_inc(csub, 1)

            pv = ps[:, 5, 0:PAIRS * 2 * VW].rearrange("p (h c) -> p h c", c=VW)

            def head_inv(t, p, k):
                dve.wait_ge(co_ps, done(t))
                dve.reciprocal(hinv[:, p].unsqueeze(2), pv[:, :, DK:VW]).then_inc(cinv, 1)

            def head_norm(t, p, k):
                dve.wait_ge(cinv, done(t))
                dve.wait_ge(cot, freed(t))
                dve.tensor_tensor(octx[:, p].rearrange("p (h d) -> p h d", d=DK), pv[:, :, 0:DK],
                                  hinv[:, p].unsqueeze(2).broadcast_to([P, HEADS, DK]), ALU.mult).then_inc(co, 1)

            def residual2(t, p, k):
                dve.wait_ge(cy, done(t))
                dve.tensor_tensor(yres[:, p], ps[:, 7, 0:D],
                                  x_all[:, ds(p * TPB + k, 1), :].rearrange("p a d -> p (a d)"), ALU.add).then_inc(cres, 1)

            def stats2(t, p, k):
                dve.wait_ge(cres, done(t))
                dve.bn_stats(bn[:, p], yres[:, p]).then_inc(cbns, 1)

            def aggr2(t, p, k):
                dve.wait_ge(cbns, done(t))
                dve.sem_inc(passed, 1)
                dve.bn_aggr(mv[:, p], bn[:, p]).then_inc(cbna, 1)

            def var2(t, p, k):
                dve.wait_ge(cbna, done(t))
                dve.tensor_scalar(ve[:, p:p + 1], mv[:, p, 1:2], EPS, None, ALU.add).then_inc(cvar, 1)

            def norm2(t, p, k):
                dve.wait_ge(crst, done(t))
                dve.wait_ge(t2, freed(t))
                dve.wait_ge(xdc, freed(t))
                dve.tensor_scalar(xs[:, p], yres[:, p], mv[:, p, 0:1], rstd[:, p:p + 1], ALU.subtract, ALU.mult).then_inc(x2, 1)

            def logits_out(t, p, k):
                dve.wait_ge(lg_ps, done(t))
                dve.wait_ge(co_ps, done(upto(t, 2)))
                dve.tensor_tensor(lg[:, p], ps[:, 5, LG:LG + E], rb[:], ALU.add).then_inc(lgb, 1)

            def logits_max(t, p, k):
                dve.wait_ge(lgb, done(t))
                dve.tensor_reduce(lmax[:, p:p + 1], lg[:, p], AX.X, ALU.max, negate=True).then_inc(lmx, 1)

            def router_inv(t, p, k):
                dve.wait_ge(lex, done(t))
                dve.reciprocal(linv[:, p:p + 1], lsum[:, p:p + 1]).then_inc(lin, 1)

            def router_probs(t, p, k):
                dve.wait_ge(lin, done(t))
                dve.tensor_scalar(rp[:, p], lexp[:, p], linv[:, p:p + 1], None, ALU.mult).then_inc(lpr, 1)

            def largest(t, p, k):
                dve.wait_ge(lpr, done(t))
                dve.sem_inc(passed, 1)
                dve.max(mx8[:, p], rp[:, p]).then_inc(l8, 1)

            def chosen(t, p, k):
                dve.wait_ge(l8, done(t))
                dve.sem_inc(passed, 1)
                dve.max_index(ix8[:, p], mx8[:, p], rp[:, p]).then_inc(li8, 1)
                dve.tensor_reduce(wsum[:, p:p + 1], mx8[:, p, 0:K], AX.X, ALU.add).then_inc(lws, 1)
                dve.wait_ge(li8, done(t))
                dve.tensor_copy(ixf[:, p], ix8[:, p, 0:K]).then_inc(lif, 1)
                dve.wait_ge(lws, done(t))
                dve.reciprocal(winv[:, p:p + 1], wsum[:, p:p + 1]).then_inc(lwi, 1)
                dve.wait_ge(lif, done(t))
                dve.tensor_tensor(oh[:, p], iota16[:].unsqueeze(1).broadcast_to([P, K, E]),
                                  ixf[:, p].unsqueeze(2).broadcast_to([P, K, E]), ALU.is_equal).then_inc(loh, 1)
                dve.tensor_copy(exp_all[:, ds(p * TPB + k, 1), :].rearrange("p a r -> p (a r)"), ixf[:, p]).then_inc(lxa, 1)
                dve.wait_ge(lwi, done(t))
                dve.tensor_scalar(wts_all[:, ds(p * TPB + k, 1), :].rearrange("p a r -> p (a r)"), mx8[:, p, 0:K], winv[:, p:p + 1],
                                  None, ALU.mult).then_inc(lw, 1)
                dve.wait_ge(loh, done(t))
                dve.wait_ge(pos_ps, freed(t))
                dve.tensor_reduce(mk[:, p], oh[:, p].rearrange("p r e -> p e r"), AX.X, ALU.add).then_inc(lmk, 1)

            def rows_of(t, p, k):
                dve.wait_ge(pos_ps, done(t))
                dve.wait_ge(cy, done(upto(t, 2)))
                dve.wait_ge(lcar, freed(t) + 1)
                dve.tensor_tensor(pos[:, p], ps[:, 7, D:D + E], carry[:], ALU.add).then_inc(lpos, 1)

            def next_rows(t, p, k):
                dve.wait_ge(pos_ps, done(t))
                dve.tensor_tensor(carry[:], ps[:, 7, D + E:D + 2 * E], carry[:], ALU.add).then_inc(lcar, 1)

            def pick_rows(t, p, k):
                dve.wait_ge(lpos, done(t))
                dve.tensor_tensor(ohp[:, p], oh[:, p], pos[:, p].unsqueeze(1).broadcast_to([P, K, E]), ALU.mult).then_inc(lohp, 1)

            def slots(t, p, k):
                dve.wait_ge(lohp, done(t))
                dve.tensor_reduce(slotf[:, p], ohp[:, p], AX.X, ALU.add).then_inc(lsl, 1)

            def indices(t, p, k):
                dve.wait_ge(lsl, done(t))
                for r in range(K):
                    if not (isinstance(t, int) and t < 2):
                        dve.wait_ge(sc_dma[p][r], 16 * k)
                dve.tensor_copy(idx[:, p], slotf[:, p]).then_inc(lidx, 1)
                dve.tensor_copy(slot_all[:, ds(p * TPB + k, 1), :].rearrange("p a r -> p (a r)"), slotf[:, p]).then_inc(lall, 1)

            pipeline(dve, NT, [(1, head_max), (1, sub_max), (2, head_inv), (3, residual2), (2, head_norm), (4, logits_out),
                               (3, stats2), (4, logits_max), (5, rows_of), (3, aggr2), (5, next_rows), (3, var2), (5, pick_rows),
                               (4, router_inv), (5, slots), (4, router_probs), (3, norm2), (5, indices), (4, largest), (4, chosen)])

            m = [0]

            def tstep(ins):
                m[0] += 1
                ins.then_inc(tb_pool, 1)
                dve.wait_ge(tb_pool, m[0])

            NB = CAP // SLOT
            dve.wait_ge(lcar, done(NT - 1))
            tstep(dve.scalar_tensor_tensor(cnt[:], iota16[:], -float(CAP), carry[:], ALU.mult, ALU.add))
            tstep(dve.tensor_tensor(cmp8[:], cnt[:].unsqueeze(2).broadcast_to([P, E, NB]),
                                    thr[:].unsqueeze(1).broadcast_to([P, E, NB]), ALU.is_gt))
            tstep(dve.tensor_reduce(ntile[:], cmp8[:], AX.X, ALU.add))
            tstep(dve.tensor_tensor(cmpe[:], trie[:], ntile[:].unsqueeze(1).broadcast_to([P, E, E]), ALU.mult))
            tstep(dve.tensor_reduce(ends[:], cmpe[:], AX.X, ALU.add))
            tstep(dve.tensor_tensor(past[:], sid[:].unsqueeze(2).broadcast_to([1, NSTEP, E]),
                                    ends[0:1].unsqueeze(1).broadcast_to([1, NSTEP, E]), ALU.is_ge))
            tstep(dve.tensor_reduce(es[:], past[:], AX.X, ALU.add))
            tstep(dve.tensor_tensor(past2[:], past[:], ntile[0:1].unsqueeze(1).broadcast_to([1, NSTEP, E]), ALU.mult))
            tstep(dve.tensor_reduce(st[:], past2[:], AX.X, ALU.add))
            tstep(dve.tensor_scalar(live[:], es[:], float(E), None, ALU.is_lt))
            tstep(dve.tensor_tensor(row[:], sid[:], st[:], ALU.subtract))
            tstep(dve.tensor_scalar(row[:], row[:], float(SLOT), None, ALU.mult))
            tstep(dve.scalar_tensor_tensor(row[:], es[:], float(CAP), row[:], ALU.mult, ALU.add))
            tstep(dve.tensor_tensor(tabf[:, :, 0], row[:], live[:], ALU.mult))
            tstep(dve.tensor_scalar(tabf[:, :, 1], es[:], float(E - 1), None, ALU.min))
            tstep(dve.tensor_scalar(tabf[:, :, 2], tabf[:, :, 1], float(D), None, ALU.mult))
            tstep(dve.tensor_scalar(tabf[:, :, 3], tabf[:, :, 1], float(I), None, ALU.mult))
            dve.tensor_copy(tab[:], tabf[:]).then_inc(tb, 1)
            tstep(dve.tensor_tensor(first_row[:], ends[:], ntile[:], ALU.subtract))
            tstep(dve.tensor_scalar(first_row[:], first_row[:], float(SLOT), None, ALU.mult))
            tstep(dve.scalar_tensor_tensor(delta[:], iota16[:], -float(CAP), first_row[:], ALU.mult, ALU.add))
            dve.wait_ge(lall, done(NT - 1))
            tstep(dve.tensor_tensor(owner[:], iota16[:].unsqueeze(1).broadcast_to([P, NT * K, E]),
                                    exp_all[:].rearrange("p t r -> p (t r)").unsqueeze(2).broadcast_to([P, NT * K, E]), ALU.is_equal))
            tstep(dve.tensor_tensor(shift[:], owner[:], delta[:].unsqueeze(1).broadcast_to([P, NT * K, E]), ALU.mult))
            tstep(dve.tensor_reduce(moved[:], shift[:], AX.X, ALU.add))
            tstep(dve.tensor_tensor(yrow_all[:].rearrange("p t r -> p (t r)"), moved[:], slot_all[:].rearrange("p t r -> p (t r)"), ALU.add))

            def split_w1(t, p, k):
                dve.wait_ge(f_w1[p], 16 * k + 16)
                dve.wait_ge(hps, freed(t))
                dve.tensor_copy(w1_h[:, p], w1f[:, p]).then_inc(w1h, 1)
                dve.wait_ge(w1h, done(t))
                dve.tensor_tensor(w1_l[:, p], w1f[:, p], f(w1_h[:, p]), ALU.subtract).then_inc(w1l, 1)

            def w2_high(t, p, k):
                dve.wait_ge(f_w2[p], 16 * k + 16)
                dve.wait_ge(yps, freed(t))
                dve.tensor_copy(w2_h[:, p], w2f[:, p]).then_inc(w2h, 1)

            def g_low(t, p, k):
                dve.wait_ge(gth, done(t))
                dve.wait_ge(hps, freed(t))
                dve.tensor_tensor(gT_l[:, p].rearrange(flat), ps[:, p], f(gT_h[:, p].rearrange(flat)), ALU.subtract).then_inc(gtl, 1)

            def h_low(t, p, k):
                dve.wait_ge(hh, done(t))
                dve.wait_ge(yps, freed(t))
                dve.tensor_tensor(h_l[:, p], hf[:, p], f(h_h[:, p]), ALU.subtract).then_inc(hl, 1)

            def y_out(t, p, k):
                dve.wait_ge(yps, done(t))
                dve.wait_ge(f_b2[p], 16 * k + 16)
                if not (isinstance(t, int) and t < 2):
                    dve.wait_ge(st_y[p], 16 * k)
                dve.tensor_tensor(yb[:, p], ps[:, 6 + p].rearrange("p (c d) -> p c d", d=D),
                                  b2f[:, p].unsqueeze(1).broadcast_to([P, 2, D]), ALU.add).then_inc(yok, 1)

            pipeline(dve, NSTEP, [(3, y_out), (1, w2_high), (0, split_w1), (0, g_low), (1, h_low)])

            def stage_idx(t, p, k):
                if not (isinstance(t, int) and t < 2):
                    for r in range(K):
                        dve.wait_ge(g_dma[p][r], 16 * k)
                dve.tensor_copy(gidx[:, p], yrow_all[:, ds(t, 1), :].rearrange("p a r -> p (a r)")).then_inc(gix, 1)

            def combine(t, p, k):
                prev = x_all[:, ds(t, 1), :].rearrange("p a d -> p (a d)")
                for r in range(K):
                    dve.wait_ge(g_dma[p][r], 16 * k + 16)
                    if r:
                        dve.wait_ge(ac[r - 1], done(t))
                    dve.scalar_tensor_tensor(acc[:, p, r], gat[:, p, r], wts_all[:, ds(t, 1), r:r + 1].rearrange("p a r -> p (a r)"),
                                             prev, ALU.mult, ALU.add).then_inc(ac[r], 1)
                    prev = acc[:, p, r]
                if not (isinstance(t, int) and t < 2):
                    dve.wait_ge(st_o[p], 16 * k)
                norm(t, p, acc[:, p, K - 1], ot[:, p], ac[K - 1], ebns, ebna, evar, erst, eo)

            pipeline(dve, NT, [(0, stage_idx), (1, combine)])


_INS = ['x', 'ctx_1024', 'mask_BxS2_ik0', 'L0_attn_qkv_w', 'L0_attn_qkv_b', 'L0_attn_out_w', 'L0_attn_out_b',
        'L0_xattn_Wq', 'L0_xattn_Wk', 'L0_xattn_Wv', 'L0_xattn_Wo', 'L0_ffn_router_w', 'L0_ffn_router_b',
        'L0_ffn_w1', 'L0_ffn_b1', 'L0_ffn_w2', 'L0_ffn_b2']


def kernel(**inputs):
    import numpy as np
    import concourse.bacc as bacc
    from concourse.bass_utils import run_bass_kernel_spmd

    nc = bacc.Bacc("TRN2", target_bir_lowering=False, num_devices=1)
    arrays, args = {}, []
    for name in _INS:
        a = np.ascontiguousarray(inputs[name])
        arrays[f"in_{name}"] = a
        args.append(nc.dram_tensor(f"in_{name}", a.shape, mybir.dt.from_np(a.dtype), kind="ExternalInput").ap())
    args.append(nc.dram_tensor("out", (B, S, D), F32, kind="ExternalOutput").ap())
    decoder_layer(nc, *args)
    r = run_bass_kernel_spmd(nc, [arrays], core_ids=[0])
    return r.results[0]["out"]
```

```python
from contextlib import ExitStack

import concourse.bass as bass
from concourse import mybir
from concourse.alu_op_type import AluOpType as ALU

F32 = mybir.dt.float32
F32R = mybir.dt.float32r
I32 = mybir.dt.int32
U32 = mybir.dt.uint32
ACT = mybir.ActivationFunctionType
AX = mybir.AxisListType
ds = bass.ds

P = 128
B, S, D = 2, 1024, 256
KD = D // P
NT = B * S // P
TPB = S // P
HEADS, DK, SK = 16, 16, 64
HPC = P // DK
PAIRS = HEADS // 2
VW = DK + 1
LG = PAIRS * 2 * VW
E, K, I = 16, 4, 512
KI = I // P
CAP = B * S
SLOT = 256
RW = D + 16
TOKENS = B * S
LEAST = (TOKENS * K) // SLOT
PAIRS_LEAST = LEAST // 2
PAIRS_MOST = (LEAST + E) // 2
NSTEP = 2 * PAIRS_MOST
SUM_BANKS = 5
EPS = 1e-5
NEG = -10000.0
HIDDEN = NEG * 4.0
POOL_SETUP = 23
TABLE_STEPS = 17
KEEP_OK, VO_OK, SETUP_DVE = 2, 13, 15
RAMP = 3
BIAS = 2


def done(t):
    return t + 1 + BIAS


def freed(t):
    return t + 1


def upto(t, ahead):
    return min(t + ahead, NT - 1) if isinstance(t, int) else t + ahead


def score_bank(t, p):
    return 4 if isinstance(t, int) and t == 0 else 2 * p


def pipeline(eng, n, stages, ramp=None, ramp_steps=0):
    depth = max(skew for skew, _ in stages)
    first = depth + depth % 2 + 2
    pairs = (n - first) // 2

    def static(t):
        for skew, fn in ramp if t < ramp_steps else stages:
            if 0 <= t - skew < n:
                fn(t - skew, (t - skew) % 2, (t - skew) // 2)

    for t in range(first):
        static(t)
    if pairs > 0:
        with eng.Fori(first // 2, first // 2 + pairs) as i:
            for q in range(2):
                for skew, fn in stages:
                    par = (q - skew) % 2
                    half = (q - skew - par) // 2
                    fn(i * 2 + (q - skew), par, i + half)
    for t in range(first + 2 * max(pairs, 0), n + depth):
        static(t)


def pipeline_upto(eng, more, stages):
    depth = max(skew for skew, _ in stages)
    first = depth + depth % 2 + 2

    for t in range(first):
        for skew, fn in stages:
            if t >= skew:
                fn(t - skew, (t - skew) % 2, (t - skew) // 2)
    with eng.Fori(first // 2, PAIRS_MOST) as i:
        with eng.If(i < more + PAIRS_LEAST):
            for q in range(2):
                for skew, fn in stages:
                    par = (q - skew) % 2
                    fn(i * 2 + (q - skew), par, i + (q - skew - par) // 2)
    for q in range(depth):
        for skew, fn in stages:
            if q < skew:
                par = (q - skew) % 2
                fn(more * 2 + (2 * PAIRS_LEAST + q - skew), par, more + (PAIRS_LEAST + (q - skew - par) // 2))


def decoder_layer(nc, x, ctx, mask, qkv_w, qkv_b, out_w, out_b, wq, wk, wv, wo,
                  router_w, router_b, w1, b1, w2, b2, out):
    xg_dram = nc.dram_tensor("expert_rows", [E * CAP + SLOT, RW], F32, kind="Internal").ap()
    sum_dram = nc.dram_tensor("expert_sum", [TOKENS + SLOT, D], F32, kind="Internal").ap()
    x_rows = x.rearrange("b s d -> (b s) d")
    out_rows = out.rearrange("b s d -> (b s) d")
    w1_rows = w1.rearrange("e d h -> (e d) h")
    w2_rows = w2.rearrange("e h d -> (e h) d")

    with ExitStack() as stack:
        names = []

        def sem(name):
            return stack.enter_context(nc.semaphore(name))

        def count(name):
            s = sem(name)
            names.append(s)
            return s

        def sb(name, shape, dt=F32, where=stack):
            return where.enter_context(nc.sbuf_tensor(name, shape, dt))

        ps = stack.enter_context(nc.psum_tensor("ps", [P, 8, 512], F32))

        ident = sb("ident", [P, P])
        ones = sb("ones", [P, P])
        tri = sb("tri", [P, P])
        iota16i = sb("iota16i", [P, E], I32)
        iota16 = sb("iota16", [P, E])
        mhalf = sb("mhalf", [P, 1])
        carry = sb("carry", [P, E])
        x_all = sb("x_all", [P, NT, D])
        shares = sb("shares", [P, NT, E])
        b2s = sb("b2s", [E, D])
        bn = sb("bn", [P, 2, 6])
        mv = sb("mv", [P, 2, 2])
        ve = sb("ve", [P, 2])
        rstd = sb("rstd", [P, 2])
        yres = sb("yres", [P, 2, D])
        xs = sb("xs", [P, 2, D])
        tab = sb("tab", [2, NSTEP], I32)
        more_pairs = sb("more_pairs", [1, 1], I32)
        even_i = sb("even_i", [P, PAIRS_MOST], I32)
        even = sb("even", [P, PAIRS_MOST])
        thr_i = sb("thr_i", [P, CAP // SLOT], I32)
        thr = sb("thr", [P, CAP // SLOT])
        trie = sb("trie", [P, E, E])
        sid_i = sb("sid_i", [NSTEP, 1], I32)
        sid = sb("sid", [NSTEP, 1])

        early = ExitStack()

        def sbe(name, shape, dt=F32):
            return sb(name, shape, dt, early)

        a_h, a_l = sbe("a_h", [P, KD, D], F32R), sbe("a_l", [P, KD, D], F32R)
        wvo_h, wvo_l = sbe("wvo_h", [P, KD, D], F32R), sbe("wvo_l", [P, KD, D], F32R)
        zeros = sbe("zeros", [P, SLOT // P, RW])
        spare_i = sbe("spare_i", [P, SLOT // P], I32)
        home_i = sbe("home_i", [P, 2, K], I32)
        blk = sbe("blk", [P, HPC])
        mask_i = sbe("mask_i", [P, B, SK], I32)
        keep = sbe("keep", [P, B, SK])
        hide = sbe("hide", [1, B, SK])
        hide_r = sbe("hide_r", [1, B, HPC, SK], F32R)
        ones_r = sbe("ones_r", [P, P], F32R)
        tri_r = sbe("tri_r", [P, P], F32R)
        rb = sbe("rb", [P, E])
        rw = sbe("rw", [P, KD, E])
        bq = sbe("bq", [P, KD])
        bv = sbe("bv", [P, KD])
        bo = sbe("bo", [P, D])
        u = sbe("u", [P, KD])
        vo = sbe("vo", [P, D])
        wqT = sbe("wqT", [P, KD, D])
        woT = sbe("woT", [P, KD, D])
        x_in = sbe("x_in", [P, 2, 2, D])
        kt = sbe("kt", [P, KD, P])
        v_sb = sbe("v_sb", [P, B, D])
        kb = sbe("kb", [P, B * KD, HPC, SK])
        vb = sbe("vb", [P, B, PAIRS, 2 * VW])
        xT_h, xT_l = sbe("xT_h", [P, KD, B * S], F32R), sbe("xT_l", [P, KD, B * S], F32R)
        v_h, v_l = sbe("v_h", [P, NT, D], F32R), sbe("v_l", [P, NT, D], F32R)
        sT_h, sT_l = sbe("sT_h", [P, 2, KD, 2, P], F32R), sbe("sT_l", [P, 2, KD, 2, P], F32R)
        q_h, q_l = sbe("q_h", [P, KD, 2, P], F32R), sbe("q_l", [P, KD, 2, P], F32R)
        prob = sbe("prob", [P, 2, S])
        pT_h, pT_l = sbe("pT_h", [P, TPB, P], F32R), sbe("pT_l", [P, TPB, P], F32R)
        cq = sbe("cq", [P, 2, KD, P])
        cpT = sbe("cpT", [P, PAIRS, P])
        nmax = sbe("nmax", [P, 2])
        nmaxs = sbe("nmaxs", [P, 2])
        rsum = sbe("rsum", [P, 2])
        rinv = sbe("rinv", [P, 2])
        hmax = sbe("hmax", [P, 2, HEADS])
        hinv = sbe("hinv", [P, 2, HEADS])
        octx = sbe("octx", [P, 2, D])
        oT = sbe("oT", [P, KD, P])
        x2T = sbe("x2T", [P, 2, KD, P])
        lg = sbe("lg", [P, 2, E])
        lmax = sbe("lmax", [P, 2])
        lexp = sbe("lexp", [P, 2, E])
        lsum = sbe("lsum", [P, 2])
        linv = sbe("linv", [P, 2])
        rp = sbe("rp", [P, 2, E])
        mx8 = sbe("mx8", [P, 2, 8])
        ix8 = sbe("ix8", [P, 2, 8], U32)
        ixf = sbe("ixf", [P, 2, K])
        wsum = sbe("wsum", [P, 2])
        winv = sbe("winv", [P, 2])
        oh = sbe("oh", [P, 2, K, E])
        mk = sbe("mk", [P, 2, E], F32R)
        pos = sbe("pos", [P, 2, E])
        ohp = sbe("ohp", [P, 2, K, E])
        slotf = sbe("slotf", [P, 2, K])
        idx = sbe("idx", [P, 2, K], U32)
        xd = sbe("xd", [P, 2, K, RW])

        setup = ExitStack()

        def sbs(name, shape, dt=F32):
            return sb(name, shape, dt, setup)

        n_qkv = sbs("n_qkv", [P, 3 * KD, D])
        n_out = sbs("n_out", [P, KD, D])
        n_x = sbs("n_x", [P, 4, KD, D])
        n_ctx = sbs("n_ctx", [P, D])
        aoT = sbs("aoT", [P, KD, D])
        wkT = sbs("wkT", [P, KD, D])
        wvT = sbs("wvT", [P, KD, D])
        cT = sbs("cT", [P, KD, P])
        cT2 = sbs("cT2", [P, KD, B, 2, SK])
        bvr = sbs("bvr", [P, KD, P])
        setup.close()
        x1T = sbe("x1T", [P, KD, B * S])
        early.close()

        late = ExitStack()

        def sbl(name, shape, dt=F32):
            return sb(name, shape, dt, late)

        ends = sbl("ends", [P, E])
        ntile = sbl("ntile", [P, E])
        cnt = sbl("cnt", [P, E])
        cmp8 = sbl("cmp8", [P, E, CAP // SLOT])
        cmpe = sbl("cmpe", [P, E, E])
        past = sbl("past", [NSTEP, E])
        past2 = sbl("past2", [NSTEP, E])
        es = sbl("es", [NSTEP, 1])
        st = sbl("st", [NSTEP, 1])
        row = sbl("row", [NSTEP, 1])
        tabf = sbl("tabf", [NSTEP, 2])
        begun = sbl("begun", [P, PAIRS_MOST])
        npf = sbl("npf", [P, 1])
        xg = sbl("xg", [P, 2, 2, RW])
        home = sbl("home", [P, 2, 2, 2])
        home_on = sbl("home_on", [P, 2, 2, 2])
        home_row = sbl("home_row", [P, 2, 2], U32)
        w1f = sbl("w1f", [P, 2, KD, I])
        w2f = sbl("w2f", [P, 2, KI, D])
        b1f = sbl("b1f", [P, 2, KI])
        w1_h, w1_l = sbl("w1_h", [P, 2, KD, I], F32R), sbl("w1_l", [P, 2, KD, I], F32R)
        w2_h, w2_l = sbl("w2_h", [P, 2, KI, D], F32R), sbl("w2_l", [P, 2, KI, D], F32R)
        gT_h, gT_l = sbl("gT_h", [P, 2, KD, SLOT], F32R), sbl("gT_l", [P, 2, KD, SLOT], F32R)
        hf = sbl("hf", [P, 2, KI, SLOT])
        h_h, h_l = sbl("h_h", [P, 2, KI, SLOT], F32R), sbl("h_l", [P, 2, KI, SLOT], F32R)
        yb = sbl("yb", [P, 2, 2, D])
        total = sbl("total", [P, NT, D])
        ot = sbl("ot", [P, NT, D])
        shT = sbl("shT", [E, NT, P])
        tbn = sbl("tbn", [P, 2, 2, 6])
        tmv = sbl("tmv", [P, 2, 2, 2])
        tve = sbl("tve", [P, 2, 2])
        trstd = sbl("trstd", [P, 2, 2])
        shift = sbl("shift", [P, 2, 2])
        late.close()

        ld_out = sem("ld_out"); ld_qkv = sem("ld_qkv"); ld_wx = sem("ld_wx"); ld_c = sem("ld_c"); ld_zero = sem("ld_zero"); ld_b2 = sem("ld_b2")
        ld_x = [sem("ld_x0"), sem("ld_x1")]
        c_pool = sem("c_pool"); c_dve = sem("c_dve"); c_pe = sem("c_pe"); c_act = sem("c_act")
        passed = sem("passed")
        c_mm = sem("c_mm"); ident_0 = sem("ident_0"); ident_ok = sem("ident_ok"); mask_ok = sem("mask_ok"); kv_ok = sem("kv_ok"); z_ok = sem("z_ok")
        xT_ps = count("xT_ps"); sTh = count("sTh"); sTl = count("sTl"); v_ps = count("v_ps")
        vh = count("vh"); vl = count("vl"); xres = count("xres"); xTh = count("xTh"); xTl = count("xTl")
        q_ps = count("q_ps"); qh = count("qh"); ql = count("ql"); s_ps = count("s_ps")
        mx = count("mx"); mxs = count("mxs"); ex = count("ex"); tp = count("tp"); pth = count("pth"); ptl = count("ptl")
        o_ps = count("o_ps"); ri = count("ri"); res = count("res"); bns = count("bns"); bna = count("bna")
        var = count("var"); rst = count("rst"); x1 = count("x1"); x1k = count("x1k")
        t1 = count("t1"); x1c = count("x1c")
        cq_ps = count("cq_ps"); cqc = count("cqc"); cs_ps = count("cs_ps"); first_ok = sem("first_ok"); causal_ok = sem("causal_ok")
        cmx = count("cmx"); csub = count("csub"); cex = count("cex"); ctp = count("ctp"); cpc = count("cpc"); co_ps = count("co_ps")
        cinv = count("cinv"); co = count("co"); cot = count("cot"); coc = count("coc")
        cy = count("cy"); cres = count("cres"); cbns = count("cbns"); cbna = count("cbna")
        cvar = count("cvar"); crst = count("crst"); x2 = count("x2")
        t2 = count("t2"); x2t = count("x2t"); lg_ps = count("lg_ps"); lgb = count("lgb"); lmx = count("lmx")
        lex = count("lex"); lin = count("lin"); lpr = count("lpr"); l8 = count("l8"); li8 = count("li8")
        lif = count("lif"); loh = count("loh"); lmk = count("lmk"); lws = count("lws"); lwi = count("lwi")
        lw = count("lw"); pos_ps = count("pos_ps"); lpos = count("lpos"); lcar = count("lcar"); lohp = count("lohp"); lsl = count("lsl")
        lidx = count("lidx"); xdc = count("xdc"); x2k = count("x2k"); dest = count("dest")
        sc_dma = [[sem(f"sc_dma{p}{r}") for r in range(K)] for p in range(2)]
        tb = sem("tb"); tb_ps = sem("tb_ps"); tb_dve = sem("tb_dve")
        f_x = [sem("f_x0"), sem("f_x1")]; f_w1 = [sem("f_w10"), sem("f_w11")]
        f_w2 = [sem("f_w20"), sem("f_w21")]; f_b1 = [sem("f_b10"), sem("f_b11")]; lsh = count("lsh")
        w1h = count("w1h"); w1l = count("w1l"); w2h = count("w2h"); w2l = count("w2l")
        gt = count("gt"); gth = count("gth"); gtl = count("gtl"); hps = count("hps"); gel = count("gel")
        hh = count("hh"); hl = count("hl"); yps = count("yps"); yok = count("yok")
        st_y = [[sem(f"st_y{p}{c}") for c in range(2)] for p in range(2)]
        hm = count("hm"); hmon = count("hmon"); hmrow = count("hmrow")
        sh_pe = sem("sh_pe"); sh_act = sem("sh_act"); eb = sem("eb"); xb = sem("xb"); ld_sum = sem("ld_sum")
        g_dma = [sem(f"g_dma{m}") for m in range(NT // 2)]
        ebns = sem("ebns"); ebna = sem("ebna"); evar = sem("evar"); erst = sem("erst"); shift_ok = sem("shift_ok"); eo = sem("eo")
        st_o = sem("st_o")

        def mm3(pe, o, ah, al, bh, bl, first, last):
            pe.matmul(o, ah, bh, start=first, stop=False)
            pe.matmul(o, ah, bl, start=False, stop=False)
            return pe.matmul(o, al, bh, start=False, stop=last)

        f = lambda ap: ap.bitcast(F32)

        block = stack.enter_context(nc.Block())

        @block.sync
        def _(sp):
            sp.dma_start(n_out[:], out_w.rearrange("(k p) c -> p k c", p=P)).then_inc(ld_out, 16)
            sp.dma_start(n_qkv[:], qkv_w.rearrange("(k p) c -> p k c", p=P)).then_inc(ld_qkv, 16)
            for n, w in enumerate((wq, wk, wv, wo)):
                sp.dma_start(n_x[:, n], w.rearrange("(k p) c -> p k c", p=P)).then_inc(ld_wx, 16)
            sp.dma_start(n_ctx[:], ctx.rearrange("b s d -> (b s) d")).then_inc(ld_wx, 16)
            for s in names:
                sp.sem_inc(s, BIAS)

            def load_x(t, p, k):
                sp.wait_ge(xT_ps, freed(t))
                sp.wait_ge(xres, freed(t))
                sp.dma_start(x_in[:, p], x_rows[ds(t * 2 * P, 2 * P), :].rearrange("(a p) d -> p a d", p=P)).then_inc(ld_x[p], 16)

            pipeline(sp, NT // 2, [(0, load_x)])
            sp.wait_ge(z_ok, 1)
            with sp.Fori(0, E * CAP // (4 * SLOT)) as i:
                sp.dma_start(xg_dram[ds(i * (4 * SLOT), 4 * SLOT), :].rearrange("(g p c) d -> p g c d", g=4, p=P),
                             zeros[:].unsqueeze(1).broadcast_to([P, 4, SLOT // P, RW])).then_inc(ld_zero, 16)
            sp.dma_start(xg_dram[E * CAP:E * CAP + SLOT, :].rearrange("(p c) d -> p c d", p=P),
                         zeros[:]).then_inc(ld_zero, 16)
            sp.dma_start(sum_dram[TOKENS:TOKENS + SLOT, :].rearrange("(p c) d -> p c d", p=P), zeros[:, :, 0:D]).then_inc(ld_zero, 16)

            sp.wait_ge(tb, 1)
            def step_place(t):
                rx = sp.value_load(tab[0:1, ds(t, 1)], min_val=0, max_val=E * CAP)
                re = sp.value_load(tab[1:2, ds(t, 1)], min_val=0, max_val=E - 1)
                return rx, re

            def load_rows(t, p, rx):
                sp.wait_ge(gt, freed(t))
                sp.wait_ge(hm, freed(t))
                sp.dma_start(xg[:, p], xg_dram[ds(rx, SLOT), :].rearrange("(c p) d -> p c d", p=P)).then_inc(f_x[p], 16)

            def load_weights(t, p, re):
                sp.wait_ge(w1h, freed(t))
                sp.wait_ge(w1l, freed(t))
                sp.dma_start(w1f[:, p], w1_rows[ds(re * D, D), :].rearrange("(k p) h -> p k h", p=P)).then_inc(f_w1[p], 16)
                sp.wait_ge(w2h, freed(t))
                sp.wait_ge(w2l, freed(t))
                sp.dma_start(w2f[:, p], w2_rows[ds(re * I, I), :].rearrange("(p j) d -> p j d", j=KI)).then_inc(f_w2[p], 16)
                sp.wait_ge(gel, freed(t))
                sp.sem_inc(passed, 1)
                sp.dma_start(b1f[:, p], b1[ds(re, 1), :].rearrange("o (p j) -> (o p) j", j=KI)).then_inc(f_b1[p], 16)

            places = [step_place(t) for t in range(2)]
            load_weights(0, 0, places[0][1])
            for p in range(2):
                for r in range(K):
                    sp.wait_ge(sc_dma[p][r], 16 * (NT // 2))
            for t in range(2):
                load_rows(t, t, places[t][0])

            def load_step(t, p, k):
                if isinstance(t, int) and t < 2:
                    if t == 1:
                        load_weights(t, p, places[t][1])
                    return
                rx, re = step_place(t)
                load_rows(t, p, rx)
                load_weights(t, p, re)

            more = sp.value_load(more_pairs[0:1, 0:1], min_val=0, max_val=PAIRS_MOST - PAIRS_LEAST)
            pipeline_upto(sp, more, [(0, load_step)])

            for p in range(2):
                for c in range(2):
                    sp.wait_ge(st_y[p][c], more * 16 + 16 * PAIRS_LEAST)
            for m in range(NT // 2):
                sp.dma_start(total[:, 2 * m:2 * m + 2], sum_dram[m * 2 * P:(m + 1) * 2 * P, :].rearrange("(a p) d -> p a d", p=P)).then_inc(g_dma[m], 16)
            for m in range(NT // 2):
                sp.wait_ge(eo, 2 * m + 2)
                sp.dma_start(out_rows[m * 2 * P:(m + 1) * 2 * P, :].rearrange("(a p) d -> p a d", p=P), ot[:, 2 * m:2 * m + 2]).then_inc(st_o, 16)
            sp.wait_ge(st_o, 16 * (NT // 2))

        @block.gpsimd
        def _(pool):
            pool.memset(ident[:], 0.0).then_inc(ident_0, 1)
            pool.wait_ge(ident_0, 1)
            pool.affine_select(ident[:], ident[:], [[-1, P]], ALU.not_equal, 1.0, base=0, channel_multiplier=1).then_inc(ident_ok, 1)
            pool.memset(ones[:], 1.0).then_inc(c_pool, 1)
            pool.memset(tri[:], 1.0).then_inc(c_pool, 1)
            pool.memset(blk[:], 1.0).then_inc(c_pool, 1)
            pool.memset(mhalf[:], -0.5).then_inc(c_pool, 1)
            pool.memset(trie[:], 1.0).then_inc(c_pool, 1)
            pool.iota(iota16i[:], [[1, E]], base=0, channel_multiplier=0).then_inc(c_pool, 1)
            pool.iota(thr_i[:], [[SLOT, CAP // SLOT]], base=0, channel_multiplier=0).then_inc(c_pool, 1)
            pool.iota(even_i[:], [[2, PAIRS_MOST]], base=0, channel_multiplier=0).then_inc(c_pool, 1)
            pool.iota(sid_i[:], [[1, 1]], base=0, channel_multiplier=1).then_inc(c_pool, 1)
            pool.memset(xd[:], 0.0).then_inc(c_pool, 1)
            pool.iota(home_i[:], [[S, 2], [0, K]], base=-P, channel_multiplier=1).then_inc(c_pool, 1)
            pool.wait_ge(c_pool, 11)
            pool.affine_select(tri[:], tri[:], [[1, P]], ALU.is_gt, 0.0, base=0, channel_multiplier=-1).then_inc(c_pool, 1)
            pool.affine_select(blk[:], blk[:], [[-DK, HPC]], ALU.is_ge, 0.0, base=0, channel_multiplier=1).then_inc(c_pool, 1)
            pool.affine_select(trie[:], trie[:], [[1, E], [-1, E]], ALU.is_ge, 0.0, base=0, channel_multiplier=0).then_inc(c_pool, 1)
            pool.wait_ge(c_pool, 14)
            pool.affine_select(blk[:], blk[:], [[DK, HPC]], ALU.is_ge, 0.0, base=DK - 1, channel_multiplier=-1).then_inc(c_pool, 1)
            pool.tensor_copy(iota16[:], iota16i[:]).then_inc(c_pool, 1)
            pool.tensor_copy(thr[:], thr_i[:]).then_inc(c_pool, 1)
            pool.tensor_copy(even[:], even_i[:]).then_inc(c_pool, 1)
            pool.tensor_copy(sid[:], sid_i[:]).then_inc(c_pool, 1)
            pool.tensor_copy(xd[:, :, :, D], home_i[:]).then_inc(c_pool, 1)
            pool.wait_ge(c_pool, 20)
            pool.tensor_scalar(carry[:], iota16[:], float(CAP), 0.0, ALU.mult, ALU.add).then_inc(c_pool, 1)
            pool.memset(zeros[:], 0.0).then_inc(c_pool, 1)
            pool.iota(spare_i[:], [[1, SLOT // P]], base=TOKENS, channel_multiplier=SLOT // P).then_inc(c_pool, 1)
            pool.wait_ge(c_pool, 23)
            pool.tensor_copy(zeros[:, :, D], spare_i[:]).then_inc(z_ok, 1)
            pool.memset(vb[:], 0.0).then_inc(mask_ok, 1)
            pool.wait_ge(c_dve, KEEP_OK)
            pool.tensor_scalar(hide[:], keep[0:1], -1.0, -HIDDEN, ALU.add, ALU.mult).then_inc(mask_ok, 1)
            pool.tensor_copy(ones_r[:], ones[:]).then_inc(mask_ok, 1)
            pool.tensor_copy(tri_r[:], tri[:]).then_inc(mask_ok, 1)
            pool.wait_ge(mask_ok, 4)
            for b in range(B):
                pool.tensor_copy(hide_r[:, b], hide[:, b].unsqueeze(1).broadcast_to([1, HPC, SK])).then_inc(mask_ok, 1)
            def residual(t, p, k):
                if isinstance(t, int) and t == 0:
                    pool.wait_ge(c_dve, VO_OK)
                pool.wait_ge(ld_x[p], 16 * k + 16)
                pool.tensor_tensor(x_all[:, ds(t * 2, 2), :], x_in[:, p], vo[:].unsqueeze(1).broadcast_to([P, 2, D]), ALU.add).then_inc(xres, 1)

            pipeline(pool, NT // 2, [(0, residual)])

            pool.wait_ge(c_dve, SETUP_DVE)
            kv = 0

            def kv_step(ins, kv):
                ins.then_inc(kv_ok, 1)
                pool.wait_ge(kv_ok, kv + 1)
                return kv + 1

            for b in range(B):
                for hc in range(KD):
                    kv = kv_step(pool.tensor_tensor(kb[:, b * KD + hc], kt[:, hc, b * SK:(b + 1) * SK].unsqueeze(1).broadcast_to([P, HPC, SK]),
                                                    blk[:].unsqueeze(2).broadcast_to([P, HPC, SK]), ALU.mult), kv)
                for a in range(2):
                    rows = slice(a * SK, (a + 1) * SK)
                    kv = kv_step(pool.tensor_copy(vb[rows, b, :, a * VW:a * VW + DK],
                                                  v_sb[rows, b].rearrange("p (g h d) -> p g h d", h=2, d=DK)[:, :, a]), kv)
                    kv = kv_step(pool.memset(vb[rows, b, :, a * VW + DK:(a + 1) * VW], 1.0), kv)

            def root(t, p, k):
                pool.wait_ge(var, done(t))
                pool.tensor_tensor(rstd[:, p:p + 1], ve[:, p:p + 1], mhalf[:], ALU.pow).then_inc(rst, 1)

            def keep_x1(t, p, k):
                pool.wait_ge(x1, done(t))
                pool.tensor_copy(x_all[:, ds(t, 1), :], xs[:, ds(p, 1), :]).then_inc(x1k, 1)

            pipeline(pool, NT, [(0, root), (0, keep_x1)])

            def causal(t, p, k):
                if isinstance(t, int) and t < B:
                    pool.wait_ge(first_ok, t + 1)
                    pool.affine_select(prob[:, p].rearrange("p (h k) -> p h k", k=SK), prob[:, p].rearrange("p (h k) -> p h k", k=SK),
                                       [[0, HEADS], [-1, SK]], ALU.is_ge, HIDDEN, base=0, channel_multiplier=1).then_inc(causal_ok, 1)

            def root2(t, p, k):
                pool.wait_ge(cvar, done(t))
                pool.tensor_tensor(rstd[:, p:p + 1], ve[:, p:p + 1], mhalf[:], ALU.pow).then_inc(crst, 1)

            def dispatch(t, p, k):
                pool.wait_ge(lidx, done(t))
                pool.wait_ge(dest, done(t))
                pool.wait_ge(lw, done(t))
                pool.wait_ge(xdc, done(t))
                pool.sem_inc(passed, 1)
                for r in range(K):
                    pool.indirect_dma_start(
                        out=xg_dram, out_offset=bass.IndirectOffsetOnAxis(ap=idx[:, p, r:r + 1], axis=0),
                        in_=xd[:, p, r], in_offset=None).then_inc(sc_dma[p][r], 16)

            pool.wait_ge(ld_zero, 16 * (E * CAP // (4 * SLOT) + 2))
            pipeline(pool, NT, [(1, causal), (3, root2), (6, dispatch)])

            def split_w2(t, p, k):
                pool.wait_ge(w2h, done(t))
                pool.wait_ge(yps, freed(t))
                pool.tensor_tensor(w2_l[:, p], w2f[:, p], f(w2_h[:, p]), ALU.subtract).then_inc(w2l, 1)

            def results(t, p, k):
                pool.wait_ge(yok, done(t))
                pool.wait_ge(hmrow, done(t))
                if isinstance(t, int) and t == 0:
                    pool.wait_ge(ld_sum, 16 * (NT // 2))
                else:
                    for c in range(2):
                        pool.wait_ge(st_y[1 - p][c], 16 * k + 16 * p)
                pool.sem_inc(passed, 1)
                for c in range(2):
                    pool.indirect_dma_start(
                        out=sum_dram, out_offset=bass.IndirectOffsetOnAxis(ap=home_row[:, p, c:c + 1], axis=0),
                        in_=yb[:, p, c], in_offset=None, compute_op=ALU.add).then_inc(st_y[p][c], 16)

            pool.wait_ge(tb, 1)
            more = pool.value_load(more_pairs[0:1, 0:1], min_val=0, max_val=PAIRS_MOST - PAIRS_LEAST)
            pipeline_upto(pool, more, [(3, results), (0, split_w2)])

            for m in range(NT // 2):
                pool.wait_ge(evar, m + 1)
                if m >= 2:
                    pool.wait_ge(eo, 2 * m - 2)
                pool.tensor_tensor(trstd[:, m % 2], tve[:, m % 2], mhalf[:].broadcast_to([P, 2]), ALU.pow).then_inc(erst, 1)

        @block.tensor
        def _(pe):
            def turn(bank, w):
                for kc in range(KD):
                    for ko in range(KD):
                        mm = pe.transpose(ps[:, bank, kc * D + ko * P:kc * D + (ko + 1) * P],
                                          w[:, ko, kc * P:(kc + 1) * P], ident[:])
                mm.then_inc(c_pe, 1)

            pe.wait_ge(ident_ok, 1)
            pe.wait_ge(ld_out, 16)
            turn(0, n_out)
            pe.wait_ge(ld_qkv, 16)
            for kc in range(KD):
                for ko in range(KD):
                    mm = pe.matmul(ps[:, 6, kc * D:(kc + 1) * D], n_qkv[:, ko, kc * P:(kc + 1) * P],
                                   n_qkv[:, KD + ko], start=ko == 0, stop=ko == KD - 1)
            mm.then_inc(c_mm, 1)
            pe.wait_ge(c_dve, 1)
            for kc in range(KD):
                for ko in range(KD):
                    mm = pe.matmul(ps[:, 7, kc * D:(kc + 1) * D], n_qkv[:, 2 * KD + ko, kc * P:(kc + 1) * P],
                                   aoT[:, ko], start=ko == 0, stop=ko == KD - 1)
            mm.then_inc(c_mm, 1)
            pe.wait_ge(ld_wx, 80)
            for n in range(4):
                turn(1 + n, n_x[:, n])
            for kc in range(KD):
                mm = pe.transpose(ps[:, 5, kc * P:(kc + 1) * P], n_ctx[:, kc * P:(kc + 1) * P], ident[:])
            mm.then_inc(c_pe, 1)
            pe.wait_ge(c_dve, 11)
            pe.wait_ge(ld_c, 16 * 9)
            for ko in range(KD):
                pe.matmul(ps[:, 0, 0:D], bvr[:, ko], aoT[:, ko], start=ko == 0, stop=ko == KD - 1)
            for kc in range(KD):
                for ko in range(KD):
                    mm = pe.matmul(ps[:, 0, D + kc:D + kc + 1], n_qkv[:, KD + ko, kc * P:(kc + 1) * P],
                                   bq[:, ko:ko + 1], start=ko == 0, stop=ko == KD - 1)
            mm.then_inc(c_mm, 1)
            pe.wait_ge(c_act, 3)
            for ko in range(KD):
                for ki in range(KD):
                    mm = pe.matmul(ps[:, 1, ko * P:(ko + 1) * P], wkT[:, ki, ko * P:(ko + 1) * P], cT[:, ki],
                                   start=ki == 0, stop=ki == KD - 1)
            mm.then_inc(c_mm, 1)
            for b in range(B):
                for ki in range(KD):
                    mm = pe.matmul(ps[:, 2, b * D:(b + 1) * D], cT2[:, ki, b].rearrange("p a k -> p (a k)"),
                                   wvT[:, ki], start=ki == 0, stop=ki == KD - 1)
            mm.then_inc(c_mm, 1)
            pe.wait_ge(c_dve, SETUP_DVE)
            pe.wait_ge(c_act, 4)
            pe.wait_ge(c_pool, POOL_SETUP)

            def turn_x(t, p, k):
                pe.wait_ge(ld_x[p], 16 * k + 16)
                pe.wait_ge(sTl, freed(t))
                for kc in range(KD):
                    for a in range(2):
                        mm = pe.transpose(ps[:, p, (kc * 2 + a) * P:(kc * 2 + a + 1) * P], x_in[:, p, a, kc * P:(kc + 1) * P], ident[:])
                mm.then_inc(xT_ps, 1)

            def values(t, p, k):
                pe.wait_ge(sTl, done(t))
                pe.wait_ge(sTh, done(t))
                pe.wait_ge(vl, freed(t))
                for a in range(2):
                    for kc in range(KD):
                        mm = mm3(pe, ps[:, 2 + p, a * D:(a + 1) * D], sT_h[:, p, kc, a], sT_l[:, p, kc, a],
                                 wvo_h[:, kc], wvo_l[:, kc], kc == 0, kc == KD - 1)
                mm.then_inc(v_ps, 1)

            def query(t, p, k):
                if not p and not (isinstance(t, int) and t == 0):
                    query_of(t, p, k)

            def query_of(t, p, k):
                pe.wait_ge(ql, freed(k) + 1)
                for jc in range(KD):
                    for ic in range(KD):
                        mm = mm3(pe, ps[:, 6, jc * 2 * P:(jc + 1) * 2 * P],
                                 a_h[:, ic, jc * P:(jc + 1) * P], a_l[:, ic, jc * P:(jc + 1) * P],
                                 xT_h[:, ic, ds(t * P, 2 * P)], xT_l[:, ic, ds(t * P, 2 * P)], ic == 0, ic == KD - 1)
                mm.then_inc(q_ps, 1)

            def scores(t, p, k):
                if not (isinstance(t, int) and t == 0):
                    scores_of(t, p, k)

            def scores_of(t, p, k):
                pe.wait_ge(ql, done(k))
                pe.wait_ge(qh, done(k))
                pe.wait_ge(ex, freed(t))
                b = t // TPB
                for jc in range(KD):
                    for kh in range(2):
                        mm = mm3(pe, ps[:, score_bank(t, p) + kh, :], q_h[:, jc, p], q_l[:, jc, p],
                                 xT_h[:, jc, ds(b * S + kh * 512, 512)], xT_l[:, jc, ds(b * S + kh * 512, 512)],
                                 jc == 0, jc == KD - 1)
                mm.then_inc(s_ps, 1)

            def values_and_first(t, p, k):
                last = isinstance(t, int) and t == NT // 2 - 1
                if last:
                    pe.wait_ge(xTh, done(TPB // 2 - 1))
                    pe.wait_ge(xTl, done(TPB // 2 - 1))
                    query_of(0, 0, 0)
                values(t, p, k)
                if last:
                    scores_of(0, 0, 0)

            pipeline(pe, NT // 2, [(0, turn_x), (1, values_and_first)])
            pe.wait_ge(vl, done(NT // 2 - 1))
            pe.wait_ge(vh, done(NT // 2 - 1))
            pe.wait_ge(xTl, done(NT // 2 - 1))

            def turn_p(t, p, k):
                pe.wait_ge(ex, done(t))
                pe.wait_ge(ptl, freed(t) + 1)
                for kt in range(TPB):
                    mm = pe.transpose(ps[:, 4 + kt // 4, (kt % 4) * P:(kt % 4 + 1) * P],
                                      prob[:, p, kt * P:(kt + 1) * P], ident[:])
                mm.then_inc(tp, 1)

            def attend(t, p, k):
                pe.wait_ge(ptl, done(t))
                pe.wait_ge(pth, done(t))
                pe.wait_ge(x1c, freed(t) + 1)
                b = t // TPB
                for kt in range(TPB):
                    mm = mm3(pe, ps[:, 7, 0:D], pT_h[:, kt], pT_l[:, kt],
                             v_h[:, ds(b * TPB + kt, 1), :].rearrange("p a d -> p (a d)"),
                             v_l[:, ds(b * TPB + kt, 1), :].rearrange("p a d -> p (a d)"), kt == 0, kt == TPB - 1)
                mm.then_inc(o_ps, 1)

            def turn_x1(t, p, k):
                pe.wait_ge(x1, done(t))
                for kc in range(KD):
                    mm = pe.transpose(ps[:, 7, D + kc * P:D + (kc + 1) * P], xs[:, p, kc * P:(kc + 1) * P], ident[:])
                mm.then_inc(t1, 1)


            def cquery(t, p, k):
                if not (isinstance(t, int) and t == 0):
                    cquery_of(t, p, k)

            def cquery_of(t, p, k):
                pe.wait_ge(cqc, freed(t) + 1)
                if not (isinstance(t, int) and t < 4):
                    pe.wait_ge(x2t, done(t - 4))
                for oc in range(KD):
                    for ic in range(KD):
                        mm = pe.matmul(ps[:, 4, oc * P:(oc + 1) * P], wqT[:, ic, oc * P:(oc + 1) * P],
                                       x1T[:, ic, ds(p * S + k * P, P)], start=ic == 0, stop=ic == KD - 1)
                mm.then_inc(cq_ps, 1)

            def cscores(t, p, k):
                if not (isinstance(t, int) and t == 0):
                    cscores_of(t, p, k)

            def cscores_of(t, p, k):
                pe.wait_ge(cqc, done(t))
                if isinstance(t, int) and 0 < t <= B:
                    pe.wait_ge(first_ok, t)
                else:
                    pe.wait_ge(csub, freed(t) + 1)
                for hc in range(KD):
                    pe.matmul(ps[:, hc], cq[:, p, hc], kb[:, p * KD + hc].rearrange("p h k -> p (h k)"), start=True, stop=False)
                    mm = pe.matmul(ps[:, hc], ones_r[0:1], hide_r[:, p].rearrange("p h k -> p (h k)"), start=False, stop=True)
                mm.then_inc(cs_ps, 1)

            def cturn_p(t, p, k):
                pe.wait_ge(cex, done(t))
                pe.wait_ge(cpc, freed(t) + 1)
                for g in range(PAIRS):
                    mm = pe.transpose(ps[:, 2 + g // 4, (g % 4) * P:(g % 4 + 1) * P],
                                      prob[:, p, g * P:(g + 1) * P], ident[:])
                mm.then_inc(ctp, 1)

            def cattend(t, p, k):
                pe.wait_ge(cpc, done(t))
                pe.wait_ge(co, freed(t) + 1)
                if not (isinstance(t, int) and t < 3):
                    pe.wait_ge(lgb, done(t - 3))
                for g in range(PAIRS):
                    mm = pe.matmul(ps[:, 5, g * 2 * VW:(g + 1) * 2 * VW], cpT[:, g], vb[:, p, g], start=True, stop=True)
                mm.then_inc(co_ps, 1)

            def turn_o(t, p, k):
                pe.wait_ge(co, done(t))
                pe.wait_ge(coc, freed(t) + 1)
                for kc in range(KD):
                    mm = pe.transpose(ps[:, 6, kc * P:(kc + 1) * P], octx[:, p, kc * P:(kc + 1) * P], ident[:])
                mm.then_inc(cot, 1)

            def project(t, p, k):
                pe.wait_ge(coc, done(t))
                pe.wait_ge(cres, freed(t) + 1)
                if not (isinstance(t, int) and t < 4):
                    pe.wait_ge(lcar, done(t - 4))
                for kc in range(KD):
                    mm = pe.matmul(ps[:, 7, 0:D], oT[:, kc], woT[:, kc], start=kc == 0, stop=kc == KD - 1)
                mm.then_inc(cy, 1)

            def turn_x2(t, p, k):
                pe.wait_ge(x2, done(t))
                pe.wait_ge(x2t, freed(t) + 1)
                pe.wait_ge(cqc, done(upto(t, 3)))
                for kc in range(KD):
                    mm = pe.transpose(ps[:, 4, D + kc * P:D + (kc + 1) * P], xs[:, p, kc * P:(kc + 1) * P], ident[:])
                mm.then_inc(t2, 1)

            def logits(t, p, k):
                pe.wait_ge(x2t, done(t))
                pe.wait_ge(lgb, freed(t) + 1)
                pe.wait_ge(co, done(upto(t, 1)))
                for kc in range(KD):
                    mm = pe.matmul(ps[:, 5, LG:LG + E], x2T[:, p, kc], rw[:, kc], start=kc == 0, stop=kc == KD - 1)
                mm.then_inc(lg_ps, 1)

            def positions(t, p, k):
                pe.wait_ge(lmk, done(t))
                pe.wait_ge(lcar, freed(t) + 1)
                pe.wait_ge(cres, done(upto(t, 2)))
                pe.matmul(ps[:, 7, D:D + E], tri_r[:], mk[:, p], start=True, stop=True)
                pe.matmul(ps[:, 7, D + E:D + 2 * E], ones_r[:], mk[:, p], start=True, stop=True).then_inc(pos_ps, 1)

            def last_turn_x1(t, p, k):
                if isinstance(t, int) and t == NT - 1:
                    pe.wait_ge(kv_ok, B * (KD + 4))
                    pe.wait_ge(mask_ok, 4 + B)
                    cquery_of(0, 0, 0)
                    cscores_of(0, 0, 0)
                turn_x1(t, p, k)

            pipeline(pe, NT, [(2, turn_p), (1, scores), (3, last_turn_x1), (0, query), (2, attend)],
                     ramp=[(1, scores), (2, turn_p), (3, last_turn_x1), (0, query), (2, attend)], ramp_steps=3)
            pe.wait_ge(x1c, done(NT - 1))
            pipeline(pe, NT, [(1, cscores), (3, turn_o), (4, turn_x2), (2, cturn_p), (6, positions), (3, project),
                              (0, cquery), (4, logits), (2, cattend)])
            pe.wait_ge(lcar, done(NT - 1))
            pe.wait_ge(csub, done(NT - 1))
            pe.wait_ge(cpc, done(NT - 1))
            pe.wait_ge(cqc, done(NT - 1))
            pe.wait_ge(lgb, done(NT - 1))
            pe.wait_ge(x2t, done(NT - 1))
            pe.wait_ge(ld_b2, 16)
            pe.wait_ge(lsh, done(NT - 1))
            for g in range(NT // 4):
                if g >= 2:
                    pe.wait_ge(sh_act, g - 1)
                for t in range(4 * g, 4 * g + 4):
                    mm = pe.transpose(ps[0:E, g % 2, (t % 4) * P:(t % 4 + 1) * P], shares[:, t], ident[:])
                mm.then_inc(sh_pe, 1)
            for m in range(NT // 2):
                pe.wait_ge(sh_act, m // 2 + 1)
                if m == 2:
                    pe.wait_ge(tb_dve, TABLE_STEPS)
                    pe.transpose(ps[0:2, 7, 0:NSTEP], tabf[:], ident[0:NSTEP, 0:NSTEP]).then_inc(tb_ps, 1)
                if m >= SUM_BANKS:
                    pe.wait_ge(xb, m - SUM_BANKS + 1)
                for t in range(2 * m, 2 * m + 2):
                    mm = pe.matmul(ps[:, 2 + m % SUM_BANKS, (t % 2) * D:(t % 2 + 1) * D], shT[:, t], b2s[:], start=True, stop=True)
                mm.then_inc(eb, 1)
            pe.wait_ge(xb, NT // 2)
            pe.wait_ge(tb, 1)

            def turn_g(t, p, k):
                pe.wait_ge(f_x[p], 16 * k + 16)
                pe.wait_ge(gtl, freed(t))
                for c in range(2):
                    for kc in range(KD):
                        mm = pe.transpose(ps[:, p, kc * SLOT + c * P:kc * SLOT + (c + 1) * P],
                                          xg[:, p, c, kc * P:(kc + 1) * P], ident[:])
                mm.then_inc(gt, 1)

            def up(t, p, k):
                pe.wait_ge(gtl, done(t))
                pe.wait_ge(gth, done(t))
                pe.wait_ge(w1l, done(t))
                pe.wait_ge(gel, freed(t))
                for j in range(KI):
                    for kc in range(KD):
                        mm = mm3(pe, ps[:, 2 + 2 * p + j // 2, (j % 2) * SLOT:(j % 2 + 1) * SLOT],
                                 w1_h[:, p, kc, j::KI], w1_l[:, p, kc, j::KI], gT_h[:, p, kc], gT_l[:, p, kc],
                                 kc == 0, kc == KD - 1)
                mm.then_inc(hps, 1)

            def down(t, p, k):
                pe.wait_ge(hl, done(t))
                pe.wait_ge(hh, done(t))
                pe.wait_ge(w2l, done(t))
                pe.wait_ge(yok, freed(t))
                for c in range(2):
                    for j in range(KI):
                        mm = mm3(pe, ps[:, 6 + p, c * D:(c + 1) * D], h_h[:, p, j, c * P:(c + 1) * P],
                                 h_l[:, p, j, c * P:(c + 1) * P], w2_h[:, p, j], w2_l[:, p, j], j == 0, j == KI - 1)
                mm.then_inc(yps, 1)

            more = pe.value_load(more_pairs[0:1, 0:1], min_val=0, max_val=PAIRS_MOST - PAIRS_LEAST)
            pipeline_upto(pe, more, [(0, turn_g), (1, up), (2, down)])

        @block.scalar
        def _(act):
            for kc in range(KD):
                for dst, base in ((bq, 0), (bv, 2 * D)):
                    act.dma_start(dst[:, kc:kc + 1], qkv_b[base + kc * P:base + (kc + 1) * P].rearrange("(p o) -> p o", o=1)).then_inc(ld_c, 16)
            act.dma_start(bo[:], out_b.rearrange("(o d) -> o d", o=1).broadcast_to([P, D])).then_inc(ld_c, 16)
            act.dma_start(mask_i[:].rearrange("p b k -> p (b k)"),
                          mask.rearrange("b k -> (b k)").rearrange("(o n) -> o n", o=1).broadcast_to([P, B * SK])).then_inc(ld_c, 16)
            act.dma_start(rb[:], router_b.rearrange("(o e) -> o e", o=1).broadcast_to([P, E])).then_inc(ld_c, 16)
            for kc in range(KD):
                act.dma_start(rw[:, kc], router_w[kc * P:(kc + 1) * P, :]).then_inc(ld_c, 16)

            act.dma_start(b2s[:], b2).then_inc(ld_b2, 16)

            act.wait_ge(c_mm, 1)
            act.activation(a_h[:].rearrange("p k c -> p (k c)"), ps[:, 6], ACT.Copy).then_inc(c_act, 1)
            act.wait_ge(c_mm, 2)
            act.activation(wvo_h[:].rearrange("p k c -> p (k c)"), ps[:, 7], ACT.Copy).then_inc(c_act, 1)
            act.wait_ge(c_pe, 2)
            act.activation(wqT[:].rearrange("p k c -> p (k c)"), ps[:, 1], ACT.Copy).then_inc(c_act, 1)
            act.wait_ge(c_pe, 5)
            act.activation(woT[:].rearrange("p k c -> p (k c)"), ps[:, 4], ACT.Copy).then_inc(c_act, 1)

            def x_high(t, p, k):
                act.wait_ge(xT_ps, done(t))
                act.wait_ge(v_ps, freed(t))
                act.activation(sT_h[:, p].rearrange("p k a c -> p (k a c)"), ps[:, p], ACT.Copy).then_inc(sTh, 1)
                act.activation(xT_h[:, :, ds(t * 2 * P, 2 * P)], ps[:, p].rearrange("p (k c) -> p k c", k=KD), ACT.Copy).then_inc(xTh, 1)

            def v_high(t, p, k):
                act.wait_ge(v_ps, done(t))
                act.activation(v_h[:, ds(t * 2, 2), :].rearrange("p a d -> p (a d)"), ps[:, 2 + p], ACT.Copy).then_inc(vh, 1)

            def q_high(t, p, k):
                if not p and not (isinstance(t, int) and t == 0):
                    q_high_of(t, p, k)

            def q_high_of(t, p, k):
                act.wait_ge(q_ps, done(k))
                act.wait_ge(s_ps, freed(t) + 1)
                for jc in range(KD):
                    ins = act.activation(q_h[:, jc].rearrange("p a c -> p (a c)"), ps[:, 6, jc * 2 * P:(jc + 1) * 2 * P], ACT.Identity,
                                         bias=u[:, jc:jc + 1])
                ins.then_inc(qh, 1)

            def v_high_and_first(t, p, k):
                if isinstance(t, int) and t == NT // 2 - 1:
                    q_high_of(0, 0, 0)
                v_high(t, p, k)

            pipeline(act, NT // 2, [(0, x_high), (1, v_high_and_first)])

            def p_high(t, p, k):
                act.wait_ge(tp, done(t))
                act.wait_ge(o_ps, freed(t) + 1)
                act.activation(pT_h[:].rearrange("p k c -> p (k c)"), ps[:, 4:6].rearrange("p b c -> p (b c)"),
                               ACT.Copy).then_inc(pth, 1)

            def exps(t, p, k):
                act.wait_ge(mxs, done(t))
                act.wait_ge(s_ps, done(t))
                act.wait_ge(tp, freed(t))
                act.wait_ge(ri, freed(t))
                act.activation(prob[:, p], ps[:, score_bank(t, p):score_bank(t, p) + 2].rearrange("p b c -> p (b c)"), ACT.Exp,
                               bias=nmaxs[:, p:p + 1], scale=1.0 / 16.0, accum_out=rsum[:, p:p + 1]).then_inc(ex, 1)

            def x1_turned(t, p, k):
                act.wait_ge(t1, done(t))
                act.activation(x1T[:, :, ds(t * P, P)], ps[:, 7, D:2 * D].rearrange("p (k c) -> p k c", c=P),
                               ACT.Copy).then_inc(x1c, 1)

            def q_out(t, p, k):
                if not (isinstance(t, int) and t == 0):
                    q_copy(t, p, k)

            def q_copy(t, p, k):
                act.wait_ge(cq_ps, done(t))
                act.wait_ge(cs_ps, freed(t))
                act.activation(cq[:, p].rearrange("p k c -> p (k c)"), ps[:, 4, 0:D], ACT.Copy).then_inc(cqc, 1)

            def last_x1_turned(t, p, k):
                if isinstance(t, int) and t == NT - 1:
                    q_copy(0, 0, 0)
                x1_turned(t, p, k)

            pipeline(act, NT, [(2, p_high), (3, last_x1_turned), (0, q_high), (1, exps)])

            def p_out(t, p, k):
                act.wait_ge(ctp, done(t))
                act.wait_ge(co_ps, freed(t) + 1)
                act.activation(cpT[:].rearrange("p k c -> p (k c)"), ps[:, 2:4].rearrange("p b c -> p (b c)"),
                               ACT.Copy).then_inc(cpc, 1)

            def o_out(t, p, k):
                act.wait_ge(cot, done(t))
                act.wait_ge(cy, freed(t) + 1)
                act.activation(oT[:].rearrange("p k c -> p (k c)"), ps[:, 6, 0:D], ACT.Copy).then_inc(coc, 1)

            def cexps(t, p, k):
                act.wait_ge(csub, done(t))
                act.activation(prob[:, p], prob[:, p], ACT.Exp, scale=0.25).then_inc(cex, 1)

            def x2_turned(t, p, k):
                act.wait_ge(t2, done(t))
                act.wait_ge(lg_ps, freed(t))
                act.activation(x2T[:, p].rearrange("p k c -> p (k c)"), ps[:, 4, D:2 * D], ACT.Copy).then_inc(x2t, 1)

            def keep_x2(t, p, k):
                act.wait_ge(x2, done(t))
                act.activation(x_all[:, ds(p * TPB + k, 1), :], xs[:, ds(p, 1), :], ACT.Copy).then_inc(x2k, 1)

            def pack(t, p, k):
                act.wait_ge(x2k, done(t))
                if not (isinstance(t, int) and t < 2):
                    for r in range(K):
                        act.wait_ge(sc_dma[p][r], 16 * k)
                act.sem_inc(passed, 1)
                act.activation(xd[:, p, :, 0:D], x_all[:, ds(p * TPB + k, 1), :].broadcast_to([P, K, D]), ACT.Copy).then_inc(xdc, 1)

            def rexps(t, p, k):
                act.wait_ge(lmx, done(t))
                act.activation(lexp[:, p], lg[:, p], ACT.Exp, bias=lmax[:, p:p + 1], accum_out=lsum[:, p:p + 1]).then_inc(lex, 1)

            pipeline(act, NT, [(3, o_out), (4, x2_turned), (2, p_out), (1, cexps), (0, q_out), (5, pack), (4, keep_x2), (4, rexps)],
                     ramp=[(3, o_out), (4, x2_turned), (2, p_out), (0, q_out), (1, cexps), (5, pack), (4, keep_x2), (4, rexps)], ramp_steps=RAMP)

            for g in range(NT // 4):
                act.wait_ge(sh_pe, g + 1)
                act.activation(shT[:, 4 * g:4 * g + 4].rearrange("e t c -> e (t c)"), ps[0:E, g % 2], ACT.Copy).then_inc(sh_act, 1)

            for m in range(NT // 2):
                act.wait_ge(xb, m + 1)
                act.dma_start(sum_dram[m * 2 * P:(m + 1) * 2 * P, :].rearrange("(a p) d -> p a d", p=P), x_all[:, 2 * m:2 * m + 2]).then_inc(ld_sum, 16)

            def y_out(t, p, k):
                act.wait_ge(yps, done(t))
                act.wait_ge(hmon, done(t))
                if not (isinstance(t, int) and t < 2):
                    for c in range(2):
                        act.wait_ge(st_y[p][c], 16 * k)
                act.sem_inc(passed, 1)
                for c in range(2):
                    ins = act.activation(yb[:, p, c], ps[:, 6 + p, c * D:(c + 1) * D], ACT.Copy, scale=home_on[:, p, c, 1:2])
                ins.then_inc(yok, 1)

            def g_high(t, p, k):
                act.wait_ge(gt, done(t))
                act.wait_ge(hps, freed(t))
                act.activation(gT_h[:, p].rearrange("p k c -> p (k c)"), ps[:, p], ACT.Copy).then_inc(gth, 1)

            def gelus(t, p, k):
                act.wait_ge(hps, done(t))
                act.wait_ge(f_b1[p], 16 * k + 16)
                act.wait_ge(hl, freed(t))
                act.wait_ge(hh, freed(t))
                for j in range(KI):
                    ins = act.activation(hf[:, p, j], ps[:, 2 + 2 * p + j // 2, (j % 2) * SLOT:(j % 2 + 1) * SLOT],
                                         ACT.Gelu, bias=b1f[:, p, j:j + 1])
                ins.then_inc(gel, 1)

            def h_high(t, p, k):
                act.wait_ge(gel, done(t))
                act.wait_ge(yps, freed(t))
                act.activation(h_h[:, p], hf[:, p], ACT.Copy).then_inc(hh, 1)

            act.wait_ge(tb, 1)
            more = act.value_load(more_pairs[0:1, 0:1], min_val=0, max_val=PAIRS_MOST - PAIRS_LEAST)
            pipeline_upto(act, more, [(3, y_out), (0, g_high), (1, gelus), (1, h_high)])

            for m in range(NT // 2):
                act.wait_ge(shift_ok, m + 1)
                for a in range(2):
                    act.activation(ot[:, 2 * m + a], total[:, 2 * m + a], ACT.Identity,
                                   bias=shift[:, m % 2, a:a + 1], scale=trstd[:, m % 2, a:a + 1]).then_inc(eo, 1)

        @block.vector
        def _(dve):
            n = [0]

            def step(ins):
                n[0] += 1
                ins.then_inc(c_dve, 1)

            def low(o, src, hi):
                step(dve.tensor_tensor(o, src, f(hi), ALU.subtract))

            flat = "p k c -> p (k c)"
            dve.wait_ge(c_pe, 1)
            step(dve.tensor_copy(aoT[:].rearrange(flat), ps[:, 0]))
            dve.wait_ge(ld_c, 16 * 9)
            step(dve.tensor_scalar(keep[:], mask_i[:], 0.0, None, ALU.not_equal))
            assert n[0] == KEEP_OK, n[0]
            dve.wait_ge(c_act, 1)
            low(a_l[:].rearrange(flat), ps[:, 6], a_h[:].rearrange(flat))
            dve.wait_ge(c_act, 2)
            low(wvo_l[:].rearrange(flat), ps[:, 7], wvo_h[:].rearrange(flat))
            dve.wait_ge(c_pe, 4)
            step(dve.tensor_copy(wkT[:].rearrange(flat), ps[:, 2]))
            step(dve.tensor_copy(wvT[:].rearrange(flat), ps[:, 3]))
            dve.wait_ge(c_pe, 6)
            step(dve.tensor_copy(cT[:].rearrange(flat), ps[:, 5, 0:D]))
            for a in range(2):
                step(dve.tensor_copy(cT2[:, :, :, a], ps[:, 5, 0:D].rearrange("p (k b s) -> p k b s", b=B, s=SK)))
            for kc in range(KD):
                step(dve.tensor_copy(bvr[:, kc], bv[:, kc:kc + 1].broadcast_to([P, P])))
            dve.wait_ge(c_mm, 3)
            step(dve.tensor_copy(u[:], ps[:, 0, D:D + KD]))
            step(dve.tensor_tensor(vo[:], ps[:, 0, 0:D], bo[:], ALU.add))
            assert n[0] == VO_OK, n[0]
            dve.wait_ge(c_mm, 4)
            step(dve.tensor_tensor(kt[:].rearrange("p k (b s) -> p k b s", s=SK), ps[:, 1, 0:D].rearrange("p (k b s) -> p k b s", b=B, s=SK),
                                   keep[:].unsqueeze(1).broadcast_to([P, KD, B, SK]), ALU.mult))
            dve.wait_ge(c_mm, 5)
            step(dve.tensor_copy(v_sb[:].rearrange("p b d -> p (b d)"), ps[:, 2]))
            assert n[0] == SETUP_DVE, n[0]
            dve.wait_ge(c_pool, POOL_SETUP)

            def x_low(t, p, k):
                dve.wait_ge(xTh, done(t))
                dve.wait_ge(v_ps, freed(t))
                dve.tensor_tensor(sT_l[:, p].rearrange("p k a c -> p (k a c)"), ps[:, p], f(sT_h[:, p].rearrange("p k a c -> p (k a c)")),
                                  ALU.subtract).then_inc(sTl, 1)
                dve.wait_ge(sTl, done(t))
                dve.tensor_copy(xT_l[:, :, ds(t * 2 * P, 2 * P)], f(sT_l[:, p].rearrange("p k a c -> p k (a c)"))).then_inc(xTl, 1)

            def v_low(t, p, k):
                dve.wait_ge(vh, done(t))
                dve.tensor_tensor(v_l[:, ds(t * 2, 2), :].rearrange("p a d -> p (a d)"), ps[:, 2 + p],
                                  f(v_h[:, ds(t * 2, 2), :].rearrange("p a d -> p (a d)")), ALU.subtract).then_inc(vl, 1)

            def norm(t, p, src, dst, s_in, s_bn, s_ag, s_var, s_rst, s_out):
                dve.wait_ge(s_in, done(t))
                dve.bn_stats(bn[:, p], src).then_inc(s_bn, 1)
                dve.wait_ge(s_bn, done(t))
                dve.sem_inc(passed, 1)
                dve.bn_aggr(mv[:, p], bn[:, p]).then_inc(s_ag, 1)
                dve.wait_ge(s_ag, done(t))
                dve.tensor_scalar(ve[:, p:p + 1], mv[:, p, 1:2], EPS, None, ALU.add).then_inc(s_var, 1)
                dve.wait_ge(s_rst, done(t))
                dve.tensor_scalar(dst, src, mv[:, p, 0:1], rstd[:, p:p + 1], ALU.subtract, ALU.mult).then_inc(s_out, 1)

            def row_max(t, p, k):
                if not (isinstance(t, int) and t == 0):
                    row_max_of(t, p, k)

            def row_max_of(t, p, k):
                dve.wait_ge(s_ps, done(t))
                dve.wait_ge(ex, freed(t))
                dve.tensor_reduce(nmax[:, p:p + 1], ps[:, score_bank(t, p):score_bank(t, p) + 2].rearrange("p b c -> p (b c)"), AX.X, ALU.max).then_inc(mx, 1)
                dve.wait_ge(mx, done(t))
                dve.tensor_scalar(nmaxs[:, p:p + 1], nmax[:, p:p + 1], -1.0 / 16.0, None, ALU.mult).then_inc(mxs, 1)

            def q_low(t, p, k):
                if not p and not (isinstance(t, int) and t == 0):
                    q_low_of(t, p, k)

            def q_low_of(t, p, k):
                dve.wait_ge(qh, done(k))
                dve.wait_ge(s_ps, freed(t) + 1)
                for jc in range(KD):
                    ins = dve.scalar_tensor_tensor(q_l[:, jc].rearrange("p a c -> p (a c)"), ps[:, 6, jc * 2 * P:(jc + 1) * 2 * P], u[:, jc:jc + 1],
                                                   f(q_h[:, jc].rearrange("p a c -> p (a c)")), ALU.add, ALU.subtract)
                ins.then_inc(ql, 1)

            def v_low_and_first(t, p, k):
                last = isinstance(t, int) and t == NT // 2 - 1
                if last:
                    q_low_of(0, 0, 0)
                v_low(t, p, k)
                if last:
                    row_max_of(0, 0, 0)

            pipeline(dve, NT // 2, [(0, x_low), (1, v_low_and_first)])
            dve.wait_ge(xres, done(NT // 2 - 1))

            def p_low(t, p, k):
                dve.wait_ge(pth, done(t))
                dve.wait_ge(o_ps, freed(t) + 1)
                dve.tensor_tensor(pT_l[:].rearrange(flat), ps[:, 4:6].rearrange("p b c -> p (b c)"), f(pT_h[:].rearrange(flat)),
                                  ALU.subtract).then_inc(ptl, 1)

            def finish(t, p, k):
                dve.wait_ge(ex, done(t))
                dve.reciprocal(rinv[:, p:p + 1], rsum[:, p:p + 1]).then_inc(ri, 1)
                dve.wait_ge(ri, done(t))
                dve.wait_ge(o_ps, done(t))
                dve.scalar_tensor_tensor(yres[:, p], ps[:, 7, 0:D], rinv[:, p:p + 1],
                                         x_all[:, ds(t, 1), :].rearrange("p a d -> p (a d)"), ALU.mult, ALU.add).then_inc(res, 1)
                dve.wait_ge(t1, freed(t))
                dve.wait_ge(x1k, freed(t))
                norm(t, p, yres[:, p], xs[:, p], res, bns, bna, var, rst, x1)

            pipeline(dve, NT, [(3, finish), (2, p_low), (1, row_max), (0, q_low)])

            heads = "p (h k) -> p h k"

            def scored(t, p):
                if isinstance(t, int) and t < B:
                    return prob[:, p].rearrange(heads, k=SK)
                return ps[:, 0:2].rearrange("p b (h k) -> p (b h) k", k=SK)

            def head_max(t, p, k):
                dve.wait_ge(cs_ps, done(t))
                if isinstance(t, int) and t < B:
                    dve.tensor_copy(prob[:, p], ps[:, 0:2].rearrange("p b c -> p (b c)")).then_inc(first_ok, 1)
                    dve.wait_ge(causal_ok, t + 1)
                dve.tensor_reduce(hmax[:, p], scored(t, p), AX.X, ALU.max).then_inc(cmx, 1)

            def sub_max(t, p, k):
                dve.wait_ge(cmx, done(t))
                dve.wait_ge(ctp, freed(t))
                dve.tensor_tensor(prob[:, p].rearrange(heads, k=SK), scored(t, p),
                                  hmax[:, p].unsqueeze(2).broadcast_to([P, HEADS, SK]), ALU.subtract).then_inc(csub, 1)

            pv = ps[:, 5, 0:PAIRS * 2 * VW].rearrange("p (h c) -> p h c", c=VW)

            def head_inv(t, p, k):
                dve.wait_ge(co_ps, done(t))
                dve.reciprocal(hinv[:, p].unsqueeze(2), pv[:, :, DK:VW]).then_inc(cinv, 1)

            def head_norm(t, p, k):
                dve.wait_ge(cinv, done(t))
                dve.wait_ge(cot, freed(t))
                dve.tensor_tensor(octx[:, p].rearrange("p (h d) -> p h d", d=DK), pv[:, :, 0:DK],
                                  hinv[:, p].unsqueeze(2).broadcast_to([P, HEADS, DK]), ALU.mult).then_inc(co, 1)

            def residual2(t, p, k):
                dve.wait_ge(cy, done(t))
                dve.tensor_tensor(yres[:, p], ps[:, 7, 0:D],
                                  x_all[:, ds(p * TPB + k, 1), :].rearrange("p a d -> p (a d)"), ALU.add).then_inc(cres, 1)

            def stats2(t, p, k):
                dve.wait_ge(cres, done(t))
                dve.bn_stats(bn[:, p], yres[:, p]).then_inc(cbns, 1)

            def aggr2(t, p, k):
                dve.wait_ge(cbns, done(t))
                dve.sem_inc(passed, 1)
                dve.bn_aggr(mv[:, p], bn[:, p]).then_inc(cbna, 1)

            def var2(t, p, k):
                dve.wait_ge(cbna, done(t))
                dve.tensor_scalar(ve[:, p:p + 1], mv[:, p, 1:2], EPS, None, ALU.add).then_inc(cvar, 1)

            def norm2(t, p, k):
                dve.wait_ge(crst, done(t))
                dve.wait_ge(t2, freed(t))
                dve.wait_ge(x2k, freed(t))
                dve.tensor_scalar(xs[:, p], yres[:, p], mv[:, p, 0:1], rstd[:, p:p + 1], ALU.subtract, ALU.mult).then_inc(x2, 1)

            def logits_out(t, p, k):
                dve.wait_ge(lg_ps, done(t))
                dve.wait_ge(co_ps, done(upto(t, 2)))
                dve.tensor_tensor(lg[:, p], ps[:, 5, LG:LG + E], rb[:], ALU.add).then_inc(lgb, 1)

            def logits_max(t, p, k):
                dve.wait_ge(lgb, done(t))
                dve.tensor_reduce(lmax[:, p:p + 1], lg[:, p], AX.X, ALU.max, negate=True).then_inc(lmx, 1)

            def router_inv(t, p, k):
                dve.wait_ge(lex, done(t))
                dve.reciprocal(linv[:, p:p + 1], lsum[:, p:p + 1]).then_inc(lin, 1)

            def router_probs(t, p, k):
                dve.wait_ge(lin, done(t))
                dve.tensor_scalar(rp[:, p], lexp[:, p], linv[:, p:p + 1], None, ALU.mult).then_inc(lpr, 1)

            def largest(t, p, k):
                dve.wait_ge(lpr, done(t))
                dve.sem_inc(passed, 1)
                dve.max(mx8[:, p], rp[:, p]).then_inc(l8, 1)

            def chosen(t, p, k):
                dve.wait_ge(l8, done(t))
                dve.sem_inc(passed, 1)
                dve.max_index(ix8[:, p], mx8[:, p], rp[:, p]).then_inc(li8, 1)
                dve.tensor_reduce(wsum[:, p:p + 1], mx8[:, p, 0:K], AX.X, ALU.add).then_inc(lws, 1)

            def chosen_float(t, p, k):
                dve.wait_ge(li8, done(t))
                dve.tensor_copy(ixf[:, p], ix8[:, p, 0:K]).then_inc(lif, 1)
                dve.wait_ge(lws, done(t))
                dve.reciprocal(winv[:, p:p + 1], wsum[:, p:p + 1]).then_inc(lwi, 1)

            def one_hot(t, p, k):
                dve.wait_ge(lif, done(t))
                dve.tensor_tensor(oh[:, p], iota16[:].unsqueeze(1).broadcast_to([P, K, E]),
                                  ixf[:, p].unsqueeze(2).broadcast_to([P, K, E]), ALU.is_equal).then_inc(loh, 1)

            def chosen_mask(t, p, k):
                dve.wait_ge(loh, done(t))
                dve.wait_ge(pos_ps, freed(t))
                with nc.allow_low_precision(reason="a sum of zeros and at most a one is exact"):
                    dve.tensor_reduce(mk[:, p], oh[:, p].rearrange("p r e -> p e r"), AX.X, ALU.add).then_inc(lmk, 1)

            def all_shares(t, p, k):
                dve.wait_ge(lmk, done(t))
                dve.scalar_tensor_tensor(shares[:, ds(p * TPB + k, 1), :].rearrange("p a e -> p (a e)"), rp[:, p], winv[:, p:p + 1],
                                         f(mk[:, p]), ALU.mult, ALU.mult).then_inc(lsh, 1)

            def rows_of(t, p, k):
                dve.wait_ge(pos_ps, done(t))
                dve.wait_ge(cy, done(upto(t, 3)))
                dve.wait_ge(lcar, freed(t) + 1)
                dve.tensor_tensor(pos[:, p], ps[:, 7, D:D + E], carry[:], ALU.add).then_inc(lpos, 1)

            def next_rows(t, p, k):
                dve.wait_ge(pos_ps, done(t))
                dve.tensor_tensor(carry[:], ps[:, 7, D + E:D + 2 * E], carry[:], ALU.add).then_inc(lcar, 1)

            def pick_rows(t, p, k):
                dve.wait_ge(lpos, done(t))
                dve.tensor_tensor(ohp[:, p], oh[:, p], pos[:, p].unsqueeze(1).broadcast_to([P, K, E]), ALU.mult).then_inc(lohp, 1)

            def slots(t, p, k):
                dve.wait_ge(lohp, done(t))
                dve.tensor_reduce(slotf[:, p], ohp[:, p], AX.X, ALU.add).then_inc(lsl, 1)

            def indices(t, p, k):
                dve.wait_ge(lsl, done(t))
                for r in range(K):
                    if not (isinstance(t, int) and t < 2):
                        dve.wait_ge(sc_dma[p][r], 16 * k)
                dve.tensor_copy(idx[:, p], slotf[:, p]).then_inc(lidx, 1)
                dve.tensor_scalar(xd[:, p, :, D], xd[:, p, :, D], float(P), None, ALU.add).then_inc(dest, 1)
                dve.wait_ge(lwi, done(t))
                dve.tensor_scalar(xd[:, p, :, D + 1], mx8[:, p, 0:K], winv[:, p:p + 1], None, ALU.mult).then_inc(lw, 1)

            pipeline(dve, NT, [(5, router_inv), (1, head_max), (5, router_probs), (1, sub_max), (5, largest), (3, residual2),
                               (5, chosen), (3, stats2), (5, chosen_float), (6, rows_of), (3, aggr2), (6, next_rows), (5, one_hot),
                               (3, var2), (6, pick_rows), (5, chosen_mask), (6, slots), (5, all_shares), (6, indices),
                               (3, norm2), (2, head_inv), (2, head_norm), (4, logits_out), (4, logits_max)])

            m = [0]

            def tstep(ins):
                m[0] += 1
                ins.then_inc(tb_dve, 1)
                dve.wait_ge(tb_dve, m[0])

            NB = CAP // SLOT
            dve.wait_ge(lcar, done(NT - 1))
            tstep(dve.scalar_tensor_tensor(cnt[:], iota16[:], -float(CAP), carry[:], ALU.mult, ALU.add))
            tstep(dve.tensor_tensor(cmp8[:], cnt[:].unsqueeze(2).broadcast_to([P, E, NB]),
                                    thr[:].unsqueeze(1).broadcast_to([P, E, NB]), ALU.is_gt))
            tstep(dve.tensor_reduce(ntile[:], cmp8[:], AX.X, ALU.add))
            tstep(dve.tensor_tensor(cmpe[:], trie[:], ntile[:].unsqueeze(1).broadcast_to([P, E, E]), ALU.mult))
            tstep(dve.tensor_reduce(ends[:], cmpe[:], AX.X, ALU.add))
            tstep(dve.tensor_scalar(past[:], ends[0:NSTEP], sid[:], None, ALU.is_le))
            tstep(dve.tensor_reduce(es[:], past[:], AX.X, ALU.add))
            tstep(dve.tensor_tensor(past2[:], past[:], ntile[0:NSTEP], ALU.mult))
            tstep(dve.tensor_reduce(st[:], past2[:], AX.X, ALU.add))
            tstep(dve.tensor_tensor(row[:], sid[:], st[:], ALU.subtract))
            tstep(dve.tensor_scalar(row[:], row[:], float(SLOT), None, ALU.mult))
            tstep(dve.scalar_tensor_tensor(row[:], es[:], float(CAP), row[:], ALU.mult, ALU.add))
            tstep(dve.tensor_scalar(tabf[:, 0:1], row[:], float(E * CAP), None, ALU.min))
            tstep(dve.tensor_scalar(tabf[:, 1:2], es[:], float(E - 1), None, ALU.min))
            tstep(dve.tensor_scalar(begun[:], even[:], ends[:, E - 1:E], None, ALU.is_lt))
            tstep(dve.tensor_reduce(npf[:], begun[:], AX.X, ALU.add))
            tstep(dve.tensor_scalar(more_pairs[:], npf[0:1], -float(PAIRS_LEAST), None, ALU.add))
            assert m[0] == TABLE_STEPS, m[0]
            dve.wait_ge(tb_ps, 1)
            dve.tensor_copy(tab[:], ps[0:2, 7, 0:NSTEP]).then_inc(tb, 1)

            dve.wait_ge(x2k, done(NT - 1))
            dve.wait_ge(xdc, done(NT - 1))
            for m in range(NT // 2):
                dve.wait_ge(eb, m + 1)
                pair = x_all[:, 2 * m:2 * m + 2].rearrange("p a d -> p (a d)")
                dve.tensor_tensor(pair, ps[:, 2 + m % SUM_BANKS], pair, ALU.add).then_inc(xb, 1)

            def split_w1(t, p, k):
                if not (isinstance(t, int) and t == 0):
                    split_up(t, p, k)

            def split_up(t, p, k):
                dve.wait_ge(f_w1[p], 16 * k + 16)
                dve.wait_ge(hps, freed(t))
                dve.tensor_copy(w1_h[:, p], w1f[:, p]).then_inc(w1h, 1)
                dve.wait_ge(w1h, done(t))
                dve.tensor_tensor(w1_l[:, p], w1f[:, p], f(w1_h[:, p]), ALU.subtract).then_inc(w1l, 1)

            def w2_high(t, p, k):
                dve.wait_ge(f_w2[p], 16 * k + 16)
                dve.wait_ge(yps, freed(t))
                dve.tensor_copy(w2_h[:, p], w2f[:, p]).then_inc(w2h, 1)

            def home_in(t, p, k):
                dve.wait_ge(f_x[p], 16 * k + 16)
                dve.wait_ge(hmon, freed(t))
                dve.tensor_copy(home[:, p], xg[:, p, :, D:D + 2]).then_inc(hm, 1)

            def home_further(t, p, k):
                dve.wait_ge(hm, done(t))
                dve.wait_ge(hmrow, freed(t))
                dve.wait_ge(yok, freed(t))
                dve.tensor_copy(home_on[:, p], home[:, p]).then_inc(hmon, 1)

            def g_low(t, p, k):
                dve.wait_ge(gth, done(t))
                dve.wait_ge(hps, freed(t))
                dve.tensor_tensor(gT_l[:, p].rearrange(flat), ps[:, p], f(gT_h[:, p].rearrange(flat)), ALU.subtract).then_inc(gtl, 1)

            def h_low(t, p, k):
                dve.wait_ge(hh, done(t))
                dve.wait_ge(yps, freed(t))
                dve.tensor_tensor(h_l[:, p], hf[:, p], f(h_h[:, p]), ALU.subtract).then_inc(hl, 1)

            def home_rows(t, p, k):
                dve.wait_ge(hmon, done(t))
                if not (isinstance(t, int) and t < 2):
                    for c in range(2):
                        dve.wait_ge(st_y[p][c], 16 * k)
                dve.tensor_copy(home_row[:, p], home_on[:, p, :, 0]).then_inc(hmrow, 1)

            dve.wait_ge(tb, 1)
            split_up(0, 0, 0)
            more = dve.value_load(more_pairs[0:1, 0:1], min_val=0, max_val=PAIRS_MOST - PAIRS_LEAST)
            pipeline_upto(dve, more, [(1, w2_high), (3, home_rows), (2, home_further), (0, home_in), (0, g_low), (0, split_w1), (1, h_low)])

            def shifts(m):
                dve.wait_ge(erst, m + 1)
                if m >= 2:
                    dve.wait_ge(eo, 2 * m - 2)
                dve.scalar_tensor_tensor(shift[:, m % 2], tmv[:, m % 2, :, 0], -1.0, trstd[:, m % 2], ALU.mult, ALU.mult).then_inc(shift_ok, 1)

            for m in range(NT // 2):
                dve.wait_ge(g_dma[m], 16)
                for a in range(2):
                    dve.bn_stats(tbn[:, m % 2, a], total[:, 2 * m + a]).then_inc(ebns, 1)
                dve.wait_ge(ebns, 2 * m + 2)
                if m >= 2:
                    dve.wait_ge(shift_ok, m - 1)
                for a in range(2):
                    dve.bn_aggr(tmv[:, m % 2, a], tbn[:, m % 2, a]).then_inc(ebna, 1)
                if m >= 1:
                    shifts(m - 1)
                dve.wait_ge(ebna, 2 * m + 2)
                if m >= 2:
                    dve.wait_ge(erst, m - 1)
                dve.tensor_scalar(tve[:, m % 2], tmv[:, m % 2, :, 1], EPS, None, ALU.add).then_inc(evar, 1)
            shifts(NT // 2 - 1)


_INS = ['x', 'ctx_1024', 'mask_BxS2_ik0', 'L0_attn_qkv_w', 'L0_attn_qkv_b', 'L0_attn_out_w', 'L0_attn_out_b',
        'L0_xattn_Wq', 'L0_xattn_Wk', 'L0_xattn_Wv', 'L0_xattn_Wo', 'L0_ffn_router_w', 'L0_ffn_router_b',
        'L0_ffn_w1', 'L0_ffn_b1', 'L0_ffn_w2', 'L0_ffn_b2']


def kernel(**inputs):
    import numpy as np
    import concourse.bacc as bacc
    from concourse.bass_utils import run_bass_kernel_spmd

    nc = bacc.Bacc("TRN2", target_bir_lowering=False, num_devices=1)
    arrays, args = {}, []
    for name in _INS:
        a = np.ascontiguousarray(inputs[name])
        arrays[f"in_{name}"] = a
        args.append(nc.dram_tensor(f"in_{name}", a.shape, mybir.dt.from_np(a.dtype), kind="ExternalInput").ap())
    args.append(nc.dram_tensor("out", (B, S, D), F32, kind="ExternalOutput").ap())
    decoder_layer(nc, *args)
    r = run_bass_kernel_spmd(nc, [arrays], core_ids=[0])
    return r.results[0]["out"]
```
